# Optimizing a Trainium2 kernel written in Bass

```python
import numpy as np
import jax
import jax.numpy as jnp

def _softmax(x, axis=-1):
    return jax.nn.softmax(x, axis=axis)

def _gelu(x):
    return jax.nn.gelu(x, approximate=True)

def _silu(x):
    return jax.nn.silu(x)

def _sigmoid(x):
    return jax.nn.sigmoid(x)

def _layernorm(x, axis=-1, eps=1e-05):
    m = jnp.mean(x, axis=axis, keepdims=True)
    v = jnp.var(x, axis=axis, keepdims=True)
    return (x - m) / jnp.sqrt(v + eps)

def _scatter_add(tgt, idx, src, axis=0):
    return tgt.at[idx].add(src)

def _segment_sum(src, seg, n):
    return jax.ops.segment_sum(src, seg, n)
kernel_name = 'mk_gnn_ffn_d1_gnn_r8_443c77'

def setup_inputs(seed: int=0):
    np.random.seed(seed)
    _w = jnp.asarray

    def _rec_inputs():
        import jax
        import jax.numpy as jnp
        _gk = jax.random.key(seed)
        x = -0.0003713 + 1 * jax.random.normal(jax.random.fold_in(_gk, 1), (6250, 256), jnp.float32)
        src = jax.random.randint(jax.random.fold_in(_gk, 2), (100000,), 0, 6250, jnp.int32)
        dst = jax.random.randint(jax.random.fold_in(_gk, 3), (100000,), 0, 6250, jnp.int32)
        _o = jnp.argsort(dst, stable=True)
        src = src[_o]
        dst = dst[_o]
        return (x, src, dst)
    x, src, dst = _rec_inputs()

    def _L0_gnn_setup():
        import jax, jax.numpy as jnp
        import numpy as np
        N = 6250
        E = 100000
        F_IN = 256
        H = 8
        C = 32
        NEG_SLOPE = 0.2
        key = jax.random.key(seed)
        k1, k2, k3, k4, k5, k6, k7 = jax.random.split(key, 7)
        x = jax.random.normal(k1, (N, F_IN), jnp.float32)
        src = jax.random.randint(k2, (E,), 0, N, jnp.int32)
        dst = jax.random.randint(k3, (E,), 0, N, jnp.int32)
        edge_index = jnp.stack([src, dst], axis=0)
        W = jax.random.normal(k4, (H * C, F_IN), jnp.float32) / np.sqrt(F_IN)
        a_src = jax.random.normal(k5, (H, C), jnp.float32) / np.sqrt(C)
        a_dst = jax.random.normal(k6, (H, C), jnp.float32) / np.sqrt(C)
        bias = jnp.zeros((H * C,), jnp.float32)
        return {'x': x, 'edge_index': edge_index, 'W': W, 'a_src': a_src, 'a_dst': a_dst, 'bias': bias}
    _L0_gnn_all = _L0_gnn_setup()
    _L0_gnn_in = {k: v for k, v in _L0_gnn_all.items() if k in ('W', 'a_src', 'a_dst', 'bias')}
    del _L0_gnn_all

    def _L0_ffn_setup():
        import jax, jax.numpy as jnp
        import numpy as np
        C = 256
        HID = 1024
        E = 8
        TEMP = 1.0
        key = jax.random.key(seed)
        ks = jax.random.split(key, 7)
        x = jax.random.normal(ks[0], (8, 2048, C), dtype=jnp.float32)
        W1 = jax.random.normal(ks[1], (C, HID), dtype=jnp.float32) * 0.02
        b1 = jnp.zeros((HID,), dtype=jnp.float32)
        Wg = jax.random.normal(ks[2], (HID, E), dtype=jnp.float32) * 0.02
        bg = jnp.zeros((E,), dtype=jnp.float32)
        Wd = jax.random.normal(ks[3], (E, HID, C), dtype=jnp.float32) * 0.02
        bd = jnp.zeros((E, C), dtype=jnp.float32)
        return {'x': x, 'W1': W1, 'b1': b1, 'Wg': Wg, 'bg': bg, 'Wd': Wd, 'bd': bd}
    _L0_ffn_all = _L0_ffn_setup()
    _L0_ffn_in = {k: v for k, v in _L0_ffn_all.items() if k in ('W1', 'b1', 'Wg', 'bg', 'Wd', 'bd')}
    del _L0_ffn_all
    return {'x': x, 'src': src, 'dst': dst, 'L0_gnn_W': _L0_gnn_in['W'], 'L0_gnn_a_src': _L0_gnn_in['a_src'], 'L0_gnn_a_dst': _L0_gnn_in['a_dst'], 'L0_gnn_bias': _L0_gnn_in['bias'], 'L0_ffn_W1': _L0_ffn_in['W1'], 'L0_ffn_b1': _L0_ffn_in['b1'], 'L0_ffn_Wg': _L0_ffn_in['Wg'], 'L0_ffn_bg': _L0_ffn_in['bg'], 'L0_ffn_Wd': _L0_ffn_in['Wd'], 'L0_ffn_bd': _L0_ffn_in['bd']}

def reference(x, src, dst, L0_gnn_W, L0_gnn_a_src, L0_gnn_a_dst, L0_gnn_bias, L0_ffn_W1, L0_ffn_b1, L0_ffn_Wg, L0_ffn_bg, L0_ffn_Wd, L0_ffn_bd):
    import jax
    import jax.numpy as jnp

    def _L0_gnn_ref(x, edge_index, W, a_src, a_dst, bias):
        import jax, jax.numpy as jnp
        import numpy as np
        N = 6250
        E = 100000
        F_IN = 256
        H = 8
        C = 32
        NEG_SLOPE = 0.2
        h = (x @ W.T).reshape(N, H, C)
        loop = jnp.arange(N, dtype=edge_index.dtype)
        src = jnp.concatenate([edge_index[0], loop])
        dst = jnp.concatenate([edge_index[1], loop])
        alpha_src = jnp.sum(h * a_src, axis=-1)
        alpha_dst = jnp.sum(h * a_dst, axis=-1)
        e = jax.nn.leaky_relu(alpha_src[src] + alpha_dst[dst], NEG_SLOPE)
        m = jax.ops.segment_max(e, dst, num_segments=N)
        e = jnp.exp(e - m[dst])
        denom = jax.ops.segment_sum(e, dst, num_segments=N)
        alpha = e / (denom[dst] + 1e-16)
        msg = h[src] * alpha[:, :, None]
        out = jax.ops.segment_sum(msg, dst, num_segments=N)
        return out.reshape(N, H * C) + bias

    def _L0_ffn_ref(x, W1, b1, Wg, bg, Wd, bd):
        import jax, jax.numpy as jnp
        import numpy as np
        C = 256
        HID = 1024
        E = 8
        TEMP = 1.0
        orig_shape = x.shape
        xf = x.reshape(-1, orig_shape[-1])
        H = jax.nn.gelu(xf @ W1 + b1, approximate=False)
        probs = jax.nn.softmax((H @ Wg + bg) / TEMP, axis=-1)
        assign = jnp.argmax(probs, axis=-1)
        out = jnp.zeros_like(xf)
        for e in range(Wd.shape[0]):
            y = H @ Wd[e] + bd[e]
            sel = (assign == e)[:, None]
            out = out + jnp.where(sel, probs[:, e:e + 1] * y, 0.0)
        return out.reshape(orig_shape)
    edge_index = jnp.stack([src, dst])
    x = x + _L0_gnn_ref(_layernorm(x, axis=-1), edge_index, L0_gnn_W, L0_gnn_a_src, L0_gnn_a_dst, L0_gnn_bias)
    x = x + _L0_ffn_ref(_layernorm(x, axis=-1)[None], L0_ffn_W1, L0_ffn_b1, L0_ffn_Wg, L0_ffn_bg, L0_ffn_Wd, L0_ffn_bd)[0]
    return x

_drawn_inputs = setup_inputs


def setup_inputs(seed=0):
    import zlib

    import numpy as np

    out = dict(_drawn_inputs(seed))
    spreads = {'L0_gnn_bias': (0.0, 0.1),
     'L0_ffn_b1': (0.0, 0.602),
     'L0_ffn_bg': (0.0, 0.406),
     'L0_ffn_bd': (0.0, 0.599)}
    factors = {'L0_ffn_W1': 2.813, 'L0_ffn_Wg': 2.995, 'L0_ffn_Wd': 3.47}
    for name, (base, spread) in spreads.items():
        noise = np.random.default_rng([zlib.crc32(name.encode()), seed]).standard_normal(out[name].shape)
        drawn = base * np.exp(spread * noise) if base else spread * noise
        out[name] = jnp.asarray(drawn.astype(out[name].dtype))
    for name, factor in factors.items():
        out[name] = (out[name] * factor).astype(out[name].dtype)
    return out
```

```python
from contextlib import ExitStack

import numpy as np

import concourse.bass as bass
from concourse import mybir

F32 = mybir.dt.float32
I32 = mybir.dt.int32
ALU = mybir.AluOpType
ACT = mybir.ActivationFunctionType
AX = mybir.AxisListType

P = 128
NODES, EDGES, F = 6250, 100000, 256
HEADS, CH = 8, 32
HID, EXPERTS = 1024, 8
SLOPE, EPS = 0.2, 1e-5
NODE_TILES = -(-NODES // P)
GROUP = 4
GROUPS = -(-NODE_TILES // GROUP)
TILES = GROUPS * GROUP
LAST = NODES - (NODE_TILES - 1) * P
EDGE_TILES = -(-EDGES // P)
PAIRS = EDGE_TILES + NODE_TILES - 1
BATCH = 8
BATCHES = 104
ROUNDS = BATCHES // 2
PAIR_COLS = -(-(BATCHES + 1) * BATCH // P)
PAIR_PAD = PAIR_COLS * P
ROW = F + HEADS
PAD_DST = 16384
KF, KH = F // P, HID // P
SORTED_TILES = (NODES + EXPERTS * (P - 1)) // P
SORTED = SORTED_TILES * P
SPREAD = 40.0
GUARD = 1e-16 * float(np.exp(-SPREAD))


class Steps:

    def __init__(self, eng, sem):
        self.eng, self.sem, self.n = eng, sem, 0

    def then(self, ins):
        self.n += 1
        ins.then_inc(self.sem, 1)
        self.eng.wait_ge(self.sem, self.n)


def build(nc, x, src, dst, W, a_src, a_dst, bias, W1, b1, Wg, bg, Wd, bd, out):
    ctx = ExitStack()
    with ctx:
        def dram(name, shape, dt=F32):
            return nc.dram_tensor(name, shape, dt, kind="Internal").ap()

        def sb(name, shape, dt=F32):
            return ctx.enter_context(nc.sbuf_tensor(name, shape, dt))

        m = Shared()
        m.rows_d = dram("rows_d", (TILES * P, ROW))
        m.src_d = dram("src_d", (PAIR_PAD * P,), I32)
        m.dst_d = dram("dst_d", (PAIR_PAD * P,), I32)
        m.sorted_d = dram("sorted_d", (SORTED, F))
        m.y_d = dram("y_d", (SORTED, F))
        m.xres = sb("xres", [P, TILES, F])
        m.acc = sb("acc", [P, TILES, ROW])
        m.ident = sb("ident", [P, P])
        m.ones = sb("ones", [P, P])
        m.iota = sb("iota", [P, PAIR_PAD])
        m.iota_p = sb("iota_p", [P, 1])
        m.stats = sb("stats", [P, TILES, 6])
        m.mean = sb("mean", [P, TILES])
        m.rstd = sb("rstd", [P, TILES])
        m.tmp = sb("tmp", [P, TILES])
        with ExitStack() as edge:
            def esb(name, shape, dt=F32):
                return edge.enter_context(nc.sbuf_tensor(name, shape, dt))
            m.idx_t = esb("idx_t", [P, PAIR_PAD], I32)
            m.rel_t = esb("rel_t", [P, PAIR_PAD])
            m.node_t = esb("node_t", [1, PAIR_PAD], I32)
            m.score_t = esb("score_t", [P, TILES, 2 * HEADS])
            pair_tables(nc, m, src, dst)
            project(nc, m, x, W, a_src, a_dst)
            gather_edges(nc, m)
        finish_attention(nc, m, bias)
        m.w1 = sb("w1", [P, KF, HID])
        m.b1c = sb("b1c", [P, KH])
        m.prob = sb("prob", [P, TILES])
        m.pos = sb("pos", [P, TILES], I32)
        m.eid = sb("eid", [1, SORTED_TILES], I32)
        if DEBUG:
            dump(nc, m, out)
            return
        route(nc, m, W1, b1, Wg, bg)
        experts(nc, m, Wd, bd, out)


class Shared:
    pass


def scope(nc):
    ctx = ExitStack()
    sem = lambda name: ctx.enter_context(nc.semaphore(name))
    sb = lambda name, shape, dt=F32: ctx.enter_context(nc.sbuf_tensor(name, shape, dt))
    ps = lambda name, shape=(P, 512): ctx.enter_context(nc.psum_tensor(name, list(shape), F32))
    return ctx, sem, sb, ps


def layer_stats(v, m, chain):
    with v.Fori(0, GROUPS) as g:
        for k in range(GROUP):
            t = g * GROUP + k
            last = v.bn_stats(m.stats[:, bass.ds(t, 1), :].squeeze(1), m.xres[:, bass.ds(t, 1), :].squeeze(1))
        last.then_inc(chain.sem, 1)
    chain.n += GROUPS
    v.wait_ge(chain.sem, chain.n)
    st = m.stats
    chain.then(v.tensor_tensor(m.mean[:, :], st[:, :, 1], st[:, :, 4], ALU.add))
    chain.then(v.tensor_tensor(m.tmp[:, :], st[:, :, 1], st[:, :, 4], ALU.subtract))
    chain.then(v.tensor_tensor(m.tmp[:, :], m.tmp[:, :], m.tmp[:, :], ALU.mult))
    chain.then(v.tensor_tensor(m.rstd[:, :], st[:, :, 2], st[:, :, 5], ALU.add))
    chain.then(v.tensor_scalar(m.tmp[:, :], m.tmp[:, :], 0.25, EPS, ALU.mult, ALU.add))
    chain.then(v.tensor_scalar(m.mean[:, :], m.mean[:, :], 0.5, None, ALU.mult))
    chain.then(v.scalar_tensor_tensor(m.rstd[:, :], m.rstd[:, :], 1.0 / F, m.tmp[:, :], ALU.mult, ALU.add))


def pair_tables(nc, m, src, dst):
    ctx, sem, sb, ps = scope(nc)
    with ctx:
        PADN = PAIR_PAD * P - EDGES
        PADC = 153
        pad_src = sb("pad_src", [PADN // PADC, PADC], I32)
        pad_dst = sb("pad_dst", [PADN // PADC, PADC], I32)
        last_i = sb("last_i", [1, EDGE_TILES - 1], I32)
        last_f = sb("last_f", [1, EDGE_TILES - 1])
        iota_i = sb("iota_i", [P, PAIR_PAD], I32)
        iop_i = sb("iop_i", [P, 1], I32)
        bound = sb("bound", [P, 1])
        below = sb("below", [P, EDGE_TILES - 1])
        cnt = sb("cnt", [P, 1])
        turn = sb("turn", [P, 1])
        passed = sb("passed", [P, PAIR_PAD])
        inner = sb("inner", [P, 1])
        pair_i = sb("pair_i", [P, PAIR_COLS], I32)
        pair_f = sb("pair_f", [P, PAIR_COLS])
        tile_i = sb("tile_i", [P, PAIR_COLS], I32)
        first = sb("first", [P, PAIR_COLS])
        src_p = sb("src_p", [P, PAIR_COLS, P], I32)
        dst_p = sb("dst_p", [P, PAIR_COLS, P], I32)
        src_f = sb("src_f", [P, PAIR_COLS, P])
        rel_f = sb("rel_f", [P, PAIR_COLS, P])
        bank = [ps(f"tab{k}") for k in range(8)]
        s_fill, s_pad, s_edges, s_last = sem("fill"), sem("pads_stored"), sem("edges_stored"), sem("lasts_loaded")
        s_iota, s_ident, s_chain = sem("iota_made"), sem("ident_made"), sem("dve_step")
        s_lastf, s_bcast, s_passed, s_nodes = sem("lasts_ready"), sem("lasts_everywhere"), sem("passed_ready"), sem("nodes_ready")
        s_tile, s_rows, s_rel, s_tr = sem("tiles_ready"), sem("pair_rows_loaded"), sem("rel_ready"), sem("transposed")
        s_const = sem("constants_made")
        block = ctx.enter_context(nc.Block())

        @block.sync
        def _(sp):
            sp.dma_start(m.src_d[0:EDGES].rearrange("(a b) -> a b", a=16), src.rearrange("(a b) -> a b", a=16)).then_inc(s_edges, 16)
            sp.dma_start(m.dst_d[0:EDGES].rearrange("(a b) -> a b", a=16), dst.rearrange("(a b) -> a b", a=16)).then_inc(s_edges, 16)
            n = (EDGE_TILES - 1) * P
            with nc.allow_non_contiguous_dma(reason="the last destination of every full edge tile"):
                sp.dma_start(last_i[0:1, :], dst[0:n].rearrange("(t e) -> t e", e=P)[:, P - 1:P].rearrange("t a -> a t")).then_inc(s_last, 16)
            sp.wait_ge(s_fill, 2)
            sp.dma_start(m.src_d[EDGES:].rearrange("(a b) -> a b", b=PADC), pad_src[:, :]).then_inc(s_pad, 16)
            sp.dma_start(m.dst_d[EDGES:].rearrange("(a b) -> a b", b=PADC), pad_dst[:, :]).then_inc(s_pad, 16)

        @block.gpsimd
        def _(g):
            g.memset(pad_src[:, :], 0).then_inc(s_fill, 1)
            g.memset(pad_dst[:, :], PAD_DST).then_inc(s_fill, 1)
            g.iota(iota_i[:, :], [[1, PAIR_PAD]], base=0, channel_multiplier=0).then_inc(s_iota, 1)
            g.iota(iop_i[:, :], [[0, 1]], base=0, channel_multiplier=1).then_inc(s_iota, 1)
            g.iota(pair_i[:, :], [[P, PAIR_COLS]], base=0, channel_multiplier=1).then_inc(s_iota, 1)
            g.wait_ge(s_edges, 32)
            g.wait_ge(s_pad, 32)
            g.wait_ge(s_tile, 1)
            for j in range(PAIR_COLS):
                for table, rows in ((m.src_d, src_p), (m.dst_d, dst_p)):
                    g.indirect_dma_start(out=rows[:, j, :], out_offset=None, in_=table.rearrange("(t e) -> t e", e=P),
                                         in_offset=bass.IndirectOffsetOnAxis(ap=tile_i[:, j:j + 1], axis=0)).then_inc(s_rows, 16)

        @block.vector
        def _(v):
            chain = Steps(v, s_chain)
            v.memset(m.ones[:, :], 1.0).then_inc(s_const, 1)
            chain.then(v.memset(inner[:, :], 0.0))
            chain.then(v.memset(inner[0:NODE_TILES - 1, :], 1.0))
            v.wait_ge(s_last, 16)
            v.tensor_copy(last_f[:, :], last_i[:, :]).then_inc(s_lastf, 1)
            v.wait_ge(s_iota, 3)
            v.tensor_copy(m.iota[:, :], iota_i[:, :])
            v.tensor_copy(pair_f[:, :], pair_i[:, :])
            chain.then(v.tensor_copy(m.iota_p[:, :], iop_i[:, :]))
            v.tensor_scalar(m.ident[:, :], m.iota[:, 0:P], m.iota_p[:, 0:1], None, ALU.is_equal).then_inc(s_ident, 1)
            chain.then(v.tensor_scalar(bound[:, :], m.iota_p[:, :], float(P), float(P), ALU.mult, ALU.add))
            v.wait_ge(s_bcast, 1)
            v.tensor_scalar(below[:, 0:512], bank[0][:, :], bound[:, 0:1], None, ALU.is_lt)
            chain.then(v.tensor_scalar(below[:, 512:], bank[1][:, 0:EDGE_TILES - 1 - 512], bound[:, 0:1], None, ALU.is_lt))
            chain.then(v.tensor_reduce(cnt[:, :], below[:, :], axis=AX.X, op=ALU.add))
            chain.then(v.scalar_tensor_tensor(turn[:, :], cnt[:, :], 1.0, m.iota_p[:, :], ALU.add, ALU.add))
            v.tensor_scalar(passed[:, :], m.iota[:, :], turn[:, 0:1], None, ALU.is_ge).then_inc(s_passed, 1)
            v.wait_ge(s_nodes, 1)
            v.tensor_copy(m.node_t[:, 0:512], bank[2][0:1, :])
            v.tensor_copy(m.node_t[:, 512:], bank[3][0:1, 0:PAIR_PAD - 512])
            chain.then(v.tensor_copy(first[:, :], bank[4][:, 0:PAIR_COLS]))
            v.tensor_tensor(tile_i[:, :], pair_f[:, :], first[:, :], ALU.subtract).then_inc(s_tile, 1)
            chain.then(v.tensor_scalar(first[:, :], first[:, :], float(P), None, ALU.mult))
            v.wait_ge(s_rows, 32 * PAIR_COLS)
            v.tensor_copy(src_f[:, :, :], src_p[:, :, :])
            for j in range(PAIR_COLS):
                last = v.tensor_scalar(rel_f[:, j, :], dst_p[:, j, :], first[:, j:j + 1], None, ALU.subtract)
            last.then_inc(s_rel, 1)
            v.wait_ge(s_tr, 1)
            for table, b in ((m.idx_t, 4), (m.rel_t, 6)):
                v.tensor_copy(table[:, 0:512], bank[b][:, :])
                v.tensor_copy(table[:, 512:], bank[b + 1][:, 0:PAIR_PAD - 512])

        @block.tensor
        def _(pe):
            pe.wait_ge(s_const, 1)
            pe.wait_ge(s_lastf, 1)
            pe.matmul(bank[0][:, :], m.ones[0:1, :], last_f[0:1, 0:512], start=True, stop=True)
            pe.matmul(bank[1][:, 0:EDGE_TILES - 1 - 512], m.ones[0:1, :], last_f[0:1, 512:], start=True, stop=True).then_inc(s_bcast, 1)
            pe.wait_ge(s_passed, 1)
            pe.matmul(bank[2][0:1, :], inner[:, :], passed[:, 0:512], start=True, stop=True)
            pe.matmul(bank[3][0:1, 0:PAIR_PAD - 512], inner[:, :], passed[:, 512:], start=True, stop=True)
            for j in range(PAIR_COLS):
                last = pe.matmul(bank[4][:, j:j + 1], passed[:, j * P:(j + 1) * P], inner[:, :], start=True, stop=True)
            last.then_inc(s_nodes, 1)
            pe.wait_ge(s_ident, 1)
            pe.wait_ge(s_rel, 1)
            for rows, b in ((src_f, 4), (rel_f, 6)):
                for j in range(PAIR_COLS):
                    last = pe.transpose(bank[b + j // 4][:, (j % 4) * P:(j % 4 + 1) * P], rows[:, j, :], m.ident[:, :])
            last.then_inc(s_tr, 1)


def project(nc, m, x, W, a_src, a_dst):
    ctx, sem, sb, ps = scope(nc)
    with ctx:
        w = sb("w", [P, KF, F])
        a_col = sb("a_col", [P, KF, 2])
        a_blk = sb("a_blk", [P, KF, 2 * HEADS])
        head4 = sb("head4", [P, P // CH])
        wt = sb("wt", [P, KF, F + 2 * HEADS])
        xn = sb("xn", [P, GROUP, F])
        xt = sb("xt", [P, GROUP, F])
        ext = sb("ext", [P, 2 * HEADS])
        ext_c = sb("ext_c", [2 * HEADS, 1])
        ext_d = sb("ext_d", [2 * HEADS, 2 * HEADS])
        ext_b = sb("ext_b", [P, 2 * HEADS])
        own = sb("own", [P, TILES, HEADS])
        low = [ps(f"pt{k}") for k in range(4)]
        high = [ps(f"pm{k}") for k in range(4)]
        s_xz, s_x, s_w, s_a = sem("x_zeroed"), sem("x_loaded"), sem("w_loaded"), sem("a_loaded")
        s_chain, s_blk, s_wt, s_wa, s_wtc = sem("dve_step"), sem("a_ready"), sem("w_transposed"), sem("wa_done"), sem("wt_ready")
        s_var, s_sd = sem("variance_ready"), sem("deviation_ready")
        s_xn, s_xfree, s_t, s_xt, s_mm, s_h = sem("xn_ready"), sem("xn_free"), sem("xn_transposed"), sem("xt_ready"), sem("h_done"), sem("h_kept")
        s_rows, s_ext, s_extT, s_extd, s_extb, s_own, s_ownx, s_p = (sem("rows_stored"), sem("extremes_ready"), sem("extremes_turned"),
            sem("extremes_diagonal"), sem("extremes_everywhere"), sem("own_ready"), sem("own_exp"), sem("step_p"))
        block = ctx.enter_context(nc.Block())

        @block.sync
        def _(sp):
            sp.wait_ge(s_xz, 1)
            full = (NODE_TILES - 1)
            for t0 in range(0, full, 12):
                sp.dma_start(m.xres[:, t0:t0 + 12, :], x[t0 * P:(t0 + 12) * P, :].rearrange("(t p) c -> p t c", p=P)).then_inc(s_x, 16)
            sp.dma_start(m.xres[0:LAST, full, :], x[full * P:, :]).then_inc(s_x, 16)
            with sp.Fori(0, GROUPS) as g:
                sp.wait_ge(s_h, (g + 1) * GROUP)
                sp.dma_start(m.rows_d[bass.ds(g * GROUP * P, GROUP * P), :].rearrange("(t p) c -> p t c", p=P),
                             m.acc[:, bass.ds(g * GROUP, GROUP), :]).then_inc(s_rows, 16)

        @block.gpsimd
        def _(g):
            g.memset(m.xres[:, NODE_TILES - 1:, :], 0.0).then_inc(s_xz, 1)

        @block.scalar
        def _(a):
            a.dma_start(w[:, :, :], W.rearrange("(k p) c -> p k c", p=P)).then_inc(s_w, 16)
            for n, vec in enumerate((a_src, a_dst)):
                with nc.allow_non_contiguous_dma(reason="a vector over the partitions"):
                    a.dma_start(a_col[:, :, n:n + 1], vec.rearrange("h c -> (h c)").rearrange("(k p a) -> p k a", p=P, a=1)).then_inc(s_a, 16)
            a.wait_ge(s_var, 1)
            a.activation(m.rstd[:, :], m.rstd[:, :], ACT.Sqrt).then_inc(s_sd, 1)
            with a.Fori(0, GROUPS) as g:
                for k in range(GROUP):
                    a.wait_ge(s_t, g * GROUP + k + 1)
                    a.activation(xt[:, k, :], low[k][:, 0:F], ACT.Copy).then_inc(s_xt, 1)
            a.wait_ge(s_own, 1)
            a.activation(m.acc[:, :, F:ROW], own[:, :, :], ACT.Exp).then_inc(s_ownx, 1)

        @block.vector
        def _(v):
            chain = Steps(v, s_chain)
            for j in range(P // CH):
                chain.then(v.memset(head4[:, j:j + 1], 0.0))
                chain.then(v.memset(head4[j * CH:(j + 1) * CH, j:j + 1], 1.0))
            chain.then(v.memset(a_blk[:, :, :], 0.0))
            v.wait_ge(s_a, 32)
            for k in range(KF):
                for n in range(2):
                    h0 = n * HEADS + k * (P // CH)
                    last = v.tensor_scalar(a_blk[:, k, h0:h0 + P // CH], head4[:, :], a_col[:, k, n:n + 1], None, ALU.mult)
            last.then_inc(s_blk, 1)
            v.wait_ge(s_wa, 1)
            for k in range(KF):
                v.tensor_copy(wt[:, k, 0:F], low[k][:, 0:F])
                last = v.tensor_copy(wt[:, k, F:], low[2 + k][:, 0:2 * HEADS])
            last.then_inc(s_wtc, 1)
            v.wait_ge(s_x, 80)
            layer_stats(v, m, chain)
            v.sem_inc(s_var, 1)
            v.wait_ge(s_sd, 1)
            chain.then(v.reciprocal(m.rstd[:, :], m.rstd[:, :]))

            with v.Fori(0, GROUPS) as g:
                for k in range(GROUP):
                    t = g * GROUP + k
                    v.tensor_scalar(xn[:, k, :], m.xres[:, bass.ds(t, 1), :].squeeze(1), m.mean[:, bass.ds(t, 1)],
                                    m.rstd[:, bass.ds(t, 1)], ALU.subtract, ALU.mult).then_inc(s_xn, 1)
                for k in range(GROUP):
                    t = g * GROUP + k
                    v.wait_ge(s_mm, t + 1)
                    v.tensor_copy(m.acc[:, bass.ds(t, 1), :].squeeze(1), high[k][:, 0:ROW])
                    v.tensor_copy(m.score_t[:, bass.ds(t, 1), 0:HEADS].squeeze(1), high[k][:, ROW:ROW + HEADS]).then_inc(s_h, 1)
            v.wait_ge(s_h, TILES)
            as_h = m.acc[:, :, F:ROW].rearrange("p t h -> p h t")
            v.tensor_reduce(ext[:, 0:HEADS], as_h, axis=AX.X, op=ALU.max)
            chain.then(v.tensor_reduce(ext[:, HEADS:], as_h, axis=AX.X, op=ALU.min))
            v.tensor_scalar(ext[:, HEADS:], ext[:, HEADS:], -1.0, None, ALU.mult).then_inc(s_ext, 1)
            v.wait_ge(s_extT, 1)
            chain.then(v.tensor_reduce(ext_c[:, :], low[0][0:2 * HEADS, 0:P], axis=AX.X, op=ALU.max))
            v.tensor_scalar(ext_d[:, :], m.ident[0:2 * HEADS, 0:2 * HEADS], ext_c[:, 0:1], None, ALU.mult).then_inc(s_extd, 1)
            v.wait_ge(s_extb, 1)
            chain.then(v.tensor_copy(ext_b[:, :], low[1][:, 0:2 * HEADS]))
            dst_s, shift = m.score_t[:, :, 0:HEADS], m.score_t[:, :, HEADS:]
            chain.then(v.tensor_tensor(shift, dst_s, ext_b[:, 0:HEADS].unsqueeze(1).broadcast_to([P, TILES, HEADS]), ALU.add))
            chain.then(v.scalar_tensor_tensor(shift, shift, SLOPE, shift, ALU.mult, ALU.max))
            chain.then(v.tensor_tensor(own[:, :, :], dst_s, m.acc[:, :, F:ROW], ALU.add))
            chain.then(v.scalar_tensor_tensor(own[:, :, :], own[:, :, :], SLOPE, own[:, :, :], ALU.mult, ALU.max))
            v.wait_ge(s_rows, 16 * GROUPS)
            v.tensor_tensor(own[:, :, :], own[:, :, :], shift, ALU.subtract).then_inc(s_own, 1)
            v.wait_ge(s_ownx, 1)
            hh = m.acc[:, :, 0:F].rearrange("p t (h c) -> p t h c", h=HEADS)
            chain.then(v.tensor_tensor(hh, hh, m.acc[:, :, F:ROW].unsqueeze(3).broadcast_to([P, TILES, HEADS, CH]), ALU.mult))

        @block.tensor
        def _(pe):
            pe.wait_ge(s_w, 16)
            for ki in range(KF):
                for kc in range(KF):
                    pe.transpose(low[ki][:, kc * P:(kc + 1) * P], w[:, kc, ki * P:(ki + 1) * P], m.ident[:, :])
            pe.wait_ge(s_blk, 1)
            for ki in range(KF):
                for kc in range(KF):
                    last = pe.matmul(low[2 + ki][:, 0:2 * HEADS], w[:, kc, ki * P:(ki + 1) * P], a_blk[:, kc, :], start=(kc == 0), stop=(kc == KF - 1))
            last.then_inc(s_wa, 1)
            pe.wait_ge(s_wtc, 1)
            with pe.Fori(0, GROUPS) as g:
                for k in range(GROUP):
                    pe.wait_ge(s_xn, g * GROUP + k + 1)
                    for f in range(KF):
                        last = pe.transpose(low[k][:, f * P:(f + 1) * P], xn[:, k, f * P:(f + 1) * P], m.ident[:, :])
                    last.then_inc(s_t, 1)
                for k in range(GROUP):
                    pe.wait_ge(s_xt, g * GROUP + k + 1)
                    for f in range(KF):
                        last = pe.matmul(high[k][:, 0:F + 2 * HEADS], xt[:, k, f * P:(f + 1) * P], wt[:, f, :], start=(f == 0), stop=(f == KF - 1))
                    last.then_inc(s_mm, 1)
            pe.wait_ge(s_ext, 1)
            pe.transpose(low[0][0:2 * HEADS, 0:P], ext[:, :], m.ident[:, :]).then_inc(s_extT, 1)
            pe.wait_ge(s_extd, 1)
            pe.matmul(low[1][:, 0:2 * HEADS], m.ones[0:2 * HEADS, :], ext_d[:, :], start=True, stop=True).then_inc(s_extb, 1)


def gather_edges(nc, m):
    ctx, sem, sb, ps = scope(nc)
    with ctx:
        idx = sb("idx", [P, 2, BATCH], I32)
        rows = sb("rows", [P, 2, BATCH, ROW])
        msg = sb("msg", [P, 2, BATCH, ROW])
        hot = sb("hot", [P, 2, BATCH, P])
        hot_t = sb("hot_t", [P, 2, BATCH, P])
        z = sb("z", [P, 2, BATCH, HEADS])
        turn = [ps(f"turn{k}") for k in range(2)]
        dsts = ps("dsts")
        sums = [ps(f"sums{k}") for k in range(4)]
        s_idx, s_rows = sem("idx_ready"), [sem(f"rows_gathered{k}") for k in range(2)]
        s_free, s_hot, s_turn, s_hott = sem("rows_free"), sem("hot_ready"), sem("hot_turned"), sem("hot_t_ready")
        s_dst, s_dfree, s_z, s_e, s_msg = sem("dst_scores_ready"), sem("dst_bank_free"), sem("z_ready"), sem("exp_ready"), sem("msg_ready")
        s_sum, s_acc, s_step = sem("sums_ready"), sem("sums_added"), sem("dve_step")
        block = ctx.enter_context(nc.Block())

        @block.sync
        def _(sp):
            pass

        @block.gpsimd
        def _(g):
            with g.Fori(0, ROUNDS) as i:
                for h in range(2):
                    g.wait_ge(s_idx, 2 * i + h + 1)
                    g.nop(nofuse=True)
                    for k in range(BATCH):
                        g.indirect_dma_start(out=rows[:, h, k, :], out_offset=None, in_=m.rows_d,
                                             in_offset=bass.IndirectOffsetOnAxis(ap=idx[:, h, k:k + 1], axis=0)).then_inc(s_rows[h], 16)

        @block.scalar
        def _(a):
            def give_idx(b, h):
                a.wait_ge(s_free, b + 1)
                a.activation(idx[:, h, :], m.idx_t[:, bass.ds(b * BATCH, BATCH)], ACT.Copy).then_inc(s_idx, 1)

            def keep_turned(b, h):
                a.wait_ge(s_turn, b + 1)
                for k in range(2):
                    last = a.activation(hot_t[:, h, 4 * k:4 * k + 4, :], turn[k][:, :].rearrange("p (k e) -> p k e", e=P), ACT.Copy)
                last.then_inc(s_hott, 1)

            a.sem_inc(s_free, 2)
            give_idx(0, 0)
            keep_turned(0, 0)
            with a.Fori(0, ROUNDS) as i:
                for h in range(2):
                    b = 2 * i + h
                    give_idx(b + 1, 1 - h)
                    keep_turned(b + 1, 1 - h)
                    a.wait_ge(s_z, b + 1)
                    a.activation(msg[:, h, :, F:ROW], z[:, h, :, :], ACT.Exp).then_inc(s_e, 1)

        @block.vector
        def _(v):
            def make_hot(b, h):
                col = m.rel_t[:, bass.ds(b * BATCH, BATCH)]
                v.tensor_tensor(hot[:, h, :, :], m.iota[:, 0:P].unsqueeze(1).broadcast_to([P, BATCH, P]),
                                col.unsqueeze(2).broadcast_to([P, BATCH, P]), ALU.is_equal).then_inc(s_hot, 1)

            def step(n, ins):
                ins.then_inc(s_step, 1)
                v.wait_ge(s_step, n)

            v.sem_inc(s_acc, 4)
            make_hot(0, 0)
            with v.Fori(0, ROUNDS) as i:
                for h in range(2):
                    b = 2 * i + h
                    _, node = nc.values_load_multi_w_load_instructions(
                        m.node_t[0:1, bass.ds(b * BATCH, BATCH)], engines=(mybir.EngineType.DVE,), min_val=0, max_val=NODE_TILES - 1,
                        skip_runtime_bounds_check_because="counts at most 48 turns")
                    v.wait_ge(s_rows[h], 16 * BATCH * (i + 1))
                    v.wait_ge(s_dst, b + 1)
                    d = dsts[:, 0:BATCH * 2 * HEADS].rearrange("p (k c) -> p k c", k=BATCH)
                    zz = z[:, h, :, :]
                    step(2 * b + 1, v.tensor_tensor(zz, rows[:, h, :, F:ROW], d[:, :, 0:HEADS], ALU.add))
                    step(2 * b + 2, v.scalar_tensor_tensor(zz, zz, SLOPE, zz, ALU.mult, ALU.max))
                    v.tensor_tensor(zz, zz, d[:, :, HEADS:], ALU.subtract).then_inc(s_z, 1)
                    make_hot(b + 1, 1 - h)
                    v.wait_ge(s_e, b + 1)
                    for q in range(0, BATCH, 4):
                        last = v.tensor_tensor(msg[:, h, q:q + 4, 0:F].rearrange("p k (h c) -> p k h c", h=HEADS),
                                               rows[:, h, q:q + 4, 0:F].rearrange("p k (h c) -> p k h c", h=HEADS),
                                               msg[:, h, q:q + 4, F:ROW].unsqueeze(3).broadcast_to([P, 4, HEADS, CH]), ALU.mult)
                        last.then_inc(s_msg, 1)
                    v.wait_ge(s_msg, 2 * b + 2)
                    v.sem_inc(s_free, 1)
                    for k in range(BATCH):
                        p = b * BATCH + k
                        v.wait_ge(s_sum, p + 1)
                        v.wait_ge(s_acc, p + 4)
                        a = m.acc[:, bass.ds(node[k], 1), :].squeeze(1)
                        v.tensor_tensor(a, a, sums[k % 4][:, 0:ROW], ALU.add).then_inc(s_acc, 1)

        @block.tensor
        def _(pe):
            def turn_hot(b, h):
                pe.wait_ge(s_hot, b + 1)
                for k in range(BATCH):
                    last = pe.transpose(turn[k // 4][:, (k % 4) * P:(k % 4 + 1) * P], hot[:, h, k, :], m.ident[:, :])
                last.then_inc(s_turn, 1)

            def dst_scores(b, h):
                _, node = nc.values_load_multi_w_load_instructions(
                    m.node_t[0:1, bass.ds(b * BATCH, BATCH)], engines=(mybir.EngineType.PE,), min_val=0, max_val=NODE_TILES - 1,
                    skip_runtime_bounds_check_because="counts at most 48 turns")
                pe.wait_ge(s_hott, b + 1)
                for k in range(BATCH):
                    last = pe.matmul(dsts[:, k * 2 * HEADS:(k + 1) * 2 * HEADS], hot_t[:, h, k, :],
                                     m.score_t[:, bass.ds(node[k], 1), :].squeeze(1), start=True, stop=True)
                last.then_inc(s_dst, 1)

            turn_hot(0, 0)
            dst_scores(0, 0)
            with pe.Fori(0, ROUNDS) as i:
                for h in range(2):
                    b = 2 * i + h
                    turn_hot(b + 1, 1 - h)
                    for k in range(BATCH):
                        if k % 4 == 0:
                            pe.wait_ge(s_msg, 2 * b + k // 4 + 1)
                        pe.wait_ge(s_acc, b * BATCH + k + 1)
                        pe.matmul(sums[k % 4][:, 0:ROW], hot[:, h, k, :], msg[:, h, k, :], start=True, stop=True).then_inc(s_sum, 1)
                    pe.wait_ge(s_z, b + 1)
                    dst_scores(b + 1, 1 - h)


def finish_attention(nc, m, bias):
    ctx, sem, sb, ps = scope(nc)
    with ctx:
        den = sb("den", [P, TILES, HEADS])
        bias_b = sb("bias_b", [P, F])
        s_bias, s_chain, s_var, s_sd = sem("bias_loaded"), sem("dve_step"), sem("variance_ready"), sem("deviation_ready")
        block = ctx.enter_context(nc.Block())

        @block.sync
        def _(sp):
            sp.dma_start(bias_b[:, :], bias.partition_broadcast(P)).then_inc(s_bias, 16)

        @block.scalar
        def _(a):
            a.wait_ge(s_var, 1)
            a.activation(m.rstd[:, :], m.rstd[:, :], ACT.Sqrt).then_inc(s_sd, 1)

        @block.vector
        def _(v):
            chain = Steps(v, s_chain)
            a = m.acc[:, :, 0:F]
            chain.then(v.tensor_scalar(den[:, :, :], m.acc[:, :, F:ROW], GUARD, None, ALU.add))
            chain.then(v.reciprocal(den[:, :, :], den[:, :, :]))
            ah = a.rearrange("p t (h c) -> p t h c", h=HEADS)
            chain.then(v.tensor_tensor(ah, ah, den[:, :, :].unsqueeze(3).broadcast_to([P, TILES, HEADS, CH]), ALU.mult))
            chain.then(v.tensor_tensor(m.xres[:, :, :], m.xres[:, :, :], a, ALU.add))
            v.wait_ge(s_bias, 16)
            chain.then(v.tensor_tensor(m.xres[:, :, :], m.xres[:, :, :], bias_b[:, :].unsqueeze(1).broadcast_to([P, TILES, F]), ALU.add))
            layer_stats(v, m, chain)
            v.sem_inc(s_var, 1)
            v.wait_ge(s_sd, 1)
            chain.then(v.reciprocal(m.rstd[:, :], m.rstd[:, :]))

        @block.gpsimd
        def _(g):
            pass

        @block.tensor
        def _(pe):
            pass



def route(nc, m, W1, b1, Wg, bg):
    ctx, sem, sb, ps = scope(nc)
    with ctx:
        wg = sb("wg", [P, KH, EXPERTS])
        bg_b = sb("bg_b", [P, EXPERTS])
        xn = sb("xn2", [P, GROUP, F])
        xt = sb("xt2", [P, KF, GROUP * P])
        ht = sb("ht", [P, KH, GROUP * P])
        logit = sb("logit", [P, TILES, EXPERTS])
        onehot = sb("onehot", [P, TILES, EXPERTS])
        before = sb("before", [P, TILES, EXPERTS])
        tot = sb("tot", [P, TILES, EXPERTS])
        run = [sb(f"run{k}", [P, TILES, EXPERTS]) for k in range(2)]
        seen = sb("seen", [P, TILES])
        valid = sb("valid", [P, TILES])
        tok_i = sb("tok_i", [P, TILES], I32)
        upper = sb("upper", [P, P])
        thr = sb("thr", [P, NODE_TILES])
        need = sb("need", [P, EXPERTS, NODE_TILES])
        ntile = sb("ntile", [P, EXPERTS])
        cum = [sb(f"cum{k}", [P, EXPERTS]) for k in range(2)]
        base = sb("base", [P, EXPERTS])
        ends = sb("ends", [1, SORTED_TILES, EXPERTS])
        eid_f = sb("eid_f", [1, SORTED_TILES])
        pos_f = sb("pos_f", [P, TILES])
        zeros = sb("zeros", [P, F])
        turned = [ps(f"turned{k}") for k in range(KF)]
        hid = [ps(f"hid{k}") for k in range(4)]
        gate = ps("gate")
        totals = ps("totals")
        s_w1, s_wg, s_zero, s_zeroed, s_tok = sem("w1_loaded"), sem("wg_loaded"), sem("zeros_made"), sem("sorted_zeroed"), sem("token_ids")
        s_xn, s_t, s_xt, s_hid, s_ht, s_gate, s_kept = (sem("xn_ready"), sem("xn_turned"), sem("xt_ready"), sem("hidden_done"),
            sem("gelu_done"), sem("gates_done"), sem("gates_kept"))
        s_chain, s_max, s_exp, s_oh, s_cnt, s_pos, s_scat = (sem("dve_step"), sem("max_taken"), sem("exp_done"), sem("onehot_ready"),
            sem("counted"), sem("places_ready"), sem("tokens_sorted"))
        block = ctx.enter_context(nc.Block())

        @block.sync
        def _(sp):
            sp.dma_start(m.w1[:, :, :], W1.rearrange("(k p) c -> p k c", p=P)).then_inc(s_w1, 16)
            with nc.allow_non_contiguous_dma(reason="a bias over the partitions"):
                sp.dma_start(m.b1c[:, :], b1.rearrange("(k p) -> p k", p=P)).then_inc(s_w1, 16)
            sp.dma_start(wg[:, :, :], Wg.rearrange("(k p) c -> p k c", p=P)).then_inc(s_wg, 16)
            sp.dma_start(bg_b[:, :], bg.partition_broadcast(P)).then_inc(s_wg, 16)
            sp.wait_ge(s_zero, 1)
            sp.dma_start(m.sorted_d.rearrange("(t p) c -> p t c", p=P),
                         zeros[:, :].unsqueeze(1).broadcast_to([P, SORTED_TILES, F])).then_inc(s_zeroed, 16)

        @block.gpsimd
        def _(g):
            g.memset(zeros[:, :], 0.0).then_inc(s_zero, 1)
            g.iota(tok_i[:, :], [[P, TILES]], base=0, channel_multiplier=1).then_inc(s_tok, 1)
            g.wait_ge(s_zeroed, 16)
            g.wait_ge(s_pos, 1)
            for t in range(NODE_TILES):
                n = P if t < NODE_TILES - 1 else LAST
                g.indirect_dma_start(out=m.sorted_d, out_offset=bass.IndirectOffsetOnAxis(ap=m.pos[0:n, t:t + 1], axis=0),
                                     in_=m.acc[0:n, t, 0:F], in_offset=None).then_inc(s_scat, 16)
            g.wait_ge(s_scat, 16 * NODE_TILES)
            g.nop(nofuse=True)

        @block.scalar
        def _(a):
            a.wait_ge(s_w1, 32)
            with a.Fori(0, GROUPS) as g:
                for k in range(KH):
                    a.wait_ge(s_hid, g * KH + k + 1)
                    a.activation(ht[:, k, :], hid[k % 4][:, :], ACT.Gelu, bias=m.b1c[:, k:k + 1]).then_inc(s_ht, 1)
            a.wait_ge(s_max, 1)
            a.activation(logit[:, :, :], logit[:, :, :], ACT.Exp).then_inc(s_exp, 1)

        @block.vector
        def _(v):
            chain = Steps(v, s_chain)

            def normal(to, t):
                return v.tensor_scalar(to, m.xres[:, bass.ds(t, 1), :].squeeze(1),
                                       m.mean[:, bass.ds(t, 1)], m.rstd[:, bass.ds(t, 1)], ALU.subtract, ALU.mult)

            with v.Fori(0, GROUPS) as g:
                for k in range(GROUP):
                    t = g * GROUP + k
                    last = normal(xn[:, k, :], t)
                last.then_inc(s_xn, 1)
                for k in range(GROUP):
                    normal(m.acc[:, bass.ds(g * GROUP + k, 1), 0:F].squeeze(1), g * GROUP + k)
                v.wait_ge(s_t, g + 1)
                for f in range(KF):
                    last = v.tensor_copy(xt[:, f, :], turned[f][:, :])
                last.then_inc(s_xt, 1)
                v.wait_ge(s_gate, g + 1)
                v.tensor_copy(logit[:, bass.ds(g * GROUP, GROUP), :], gate[:, 0:GROUP * EXPERTS].rearrange("p (t e) -> p t e", e=EXPERTS)).then_inc(s_kept, 1)
            v.wait_ge(s_kept, GROUPS)
            v.wait_ge(s_wg, 32)
            chain.then(v.tensor_tensor(logit[:, :, :], logit[:, :, :], bg_b[:, :].unsqueeze(1).broadcast_to([P, TILES, EXPERTS]), ALU.add))
            chain.then(v.tensor_reduce(seen[:, :], logit[:, :, :], axis=AX.X, op=ALU.max))
            wide = seen[:, :].unsqueeze(2).broadcast_to([P, TILES, EXPERTS])
            v.tensor_tensor(logit[:, :, :], logit[:, :, :], wide, ALU.subtract).then_inc(s_max, 1)
            v.wait_ge(s_exp, 1)
            chain.then(v.tensor_reduce(seen[:, :], logit[:, :, :], axis=AX.X, op=ALU.add))
            chain.then(v.reciprocal(seen[:, :], seen[:, :]))
            chain.then(v.tensor_tensor(logit[:, :, :], logit[:, :, :], wide, ALU.mult))
            chain.then(v.tensor_reduce(m.prob[:, :], logit[:, :, :], axis=AX.X, op=ALU.max))
            chain.then(v.tensor_tensor(logit[:, :, :], logit[:, :, :], m.prob[:, :].unsqueeze(2).broadcast_to([P, TILES, EXPERTS]), ALU.is_ge))
            v.wait_ge(s_tok, 1)
            chain.then(v.tensor_copy(valid[:, :], tok_i[:, :]))
            chain.then(v.tensor_scalar(valid[:, :], valid[:, :], float(NODES), None, ALU.is_lt))
            chain.then(v.memset(seen[:, :], 0.0))
            for e in range(EXPERTS):
                chain.then(v.tensor_tensor(onehot[:, :, e], logit[:, :, e], seen[:, :], ALU.is_gt))
                chain.then(v.tensor_tensor(seen[:, :], seen[:, :], logit[:, :, e], ALU.max))
            chain.then(v.tensor_scalar(upper[:, :], m.iota[:, 0:P], m.iota_p[:, 0:1], None, ALU.is_gt))
            v.tensor_tensor(onehot[:, :, :], onehot[:, :, :], valid[:, :].unsqueeze(2).broadcast_to([P, TILES, EXPERTS]), ALU.mult).then_inc(s_oh, 1)
            v.wait_ge(s_cnt, 1)
            flat = lambda b: b[:, :, :].rearrange("p t e -> p (t e)")
            v.tensor_copy(flat(before), turned[0][:, 0:TILES * EXPERTS])
            chain.then(v.tensor_copy(flat(tot), totals[:, 0:TILES * EXPERTS]))
            chain.then(v.tensor_copy(flat(run[0]), flat(tot)))
            n, s = 0, 1
            while s < TILES:
                v.tensor_copy(run[1 - n][:, 0:s, :], run[n][:, 0:s, :])
                chain.then(v.tensor_tensor(run[1 - n][:, s:, :], run[n][:, s:, :], run[n][:, 0:TILES - s, :], ALU.add))
                n, s = 1 - n, 2 * s
            count = run[n][:, TILES - 1, :]
            chain.then(v.tensor_scalar(thr[:, :], m.iota[:, 0:NODE_TILES], float(P), None, ALU.mult))
            chain.then(v.tensor_tensor(need[:, :, :], count.unsqueeze(2).broadcast_to([P, EXPERTS, NODE_TILES]),
                                       thr[:, :].unsqueeze(1).broadcast_to([P, EXPERTS, NODE_TILES]), ALU.is_gt))
            chain.then(v.tensor_reduce(ntile[:, :], need[:, :, :], axis=AX.X, op=ALU.add))
            chain.then(v.tensor_copy(cum[0][:, :], ntile[:, :]))
            c, s = 0, 1
            while s < EXPERTS:
                v.tensor_copy(cum[1 - c][:, 0:s], cum[c][:, 0:s])
                chain.then(v.tensor_tensor(cum[1 - c][:, s:], cum[c][:, s:], cum[c][:, 0:EXPERTS - s], ALU.add))
                c, s = 1 - c, 2 * s
            chain.then(v.tensor_tensor(base[:, :], cum[c][:, :], ntile[:, :], ALU.subtract))
            chain.then(v.tensor_scalar(base[:, :], base[:, :], float(P), None, ALU.mult))
            chain.then(v.tensor_tensor(before[:, :, :], before[:, :, :], run[n][:, :, :], ALU.add))
            chain.then(v.tensor_tensor(before[:, :, :], before[:, :, :], tot[:, :, :], ALU.subtract))
            chain.then(v.tensor_tensor(before[:, :, :], before[:, :, :], base[:, :].unsqueeze(1).broadcast_to([P, TILES, EXPERTS]), ALU.add))
            chain.then(v.tensor_tensor(before[:, :, :], before[:, :, :], onehot[:, :, :], ALU.mult))
            chain.then(v.tensor_reduce(pos_f[:, :], before[:, :, :], axis=AX.X, op=ALU.add))
            v.tensor_copy(m.pos[:, :], pos_f[:, :]).then_inc(s_pos, 1)
            chain.then(v.tensor_tensor(ends[:, :, :], m.iota[0:1, 0:SORTED_TILES].unsqueeze(2).broadcast_to([1, SORTED_TILES, EXPERTS]),
                                       cum[c][0:1, :].unsqueeze(1).broadcast_to([1, SORTED_TILES, EXPERTS]), ALU.is_ge))
            chain.then(v.tensor_reduce(eid_f[:, :], ends[:, :, :], axis=AX.X, op=ALU.add))
            chain.then(v.tensor_scalar(m.eid[:, :], eid_f[:, :], float(EXPERTS - 1), None, ALU.min))

        @block.tensor
        def _(pe):
            pe.wait_ge(s_w1, 32)
            pe.wait_ge(s_wg, 32)
            pe.sem_inc(s_ht, 4)
            with pe.Fori(0, GROUPS) as g:
                pe.wait_ge(s_xn, g + 1)
                for k in range(GROUP):
                    for f in range(KF):
                        last = pe.transpose(turned[f][:, k * P:(k + 1) * P], xn[:, k, f * P:(f + 1) * P], m.ident[:, :])
                last.then_inc(s_t, 1)
                pe.wait_ge(s_xt, g + 1)
                for k in range(KH):
                    pe.wait_ge(s_ht, g * KH + k + 1)
                    for f in range(KF):
                        last = pe.matmul(hid[k % 4][:, :], m.w1[:, f, k * P:(k + 1) * P], xt[:, f, :], start=(f == 0), stop=(f == KF - 1))
                    last.then_inc(s_hid, 1)
                pe.wait_ge(s_ht, (g + 1) * KH + 4)
                for k in range(GROUP):
                    for f in range(KH):
                        last = pe.matmul(gate[:, k * EXPERTS:(k + 1) * EXPERTS], ht[:, f, k * P:(k + 1) * P], wg[:, f, :], start=(f == 0), stop=(f == KH - 1))
                last.then_inc(s_gate, 1)
            pe.wait_ge(s_oh, 1)
            oh = onehot[:, :, :].rearrange("p t e -> p (t e)")
            pe.matmul(turned[0][:, 0:TILES * EXPERTS], upper[:, :], oh, start=True, stop=True)
            pe.matmul(totals[:, 0:TILES * EXPERTS], m.ones[:, :], oh, start=True, stop=True).then_inc(s_cnt, 1)


def experts(nc, m, Wd, bd, out):
    ctx, sem, sb, ps = scope(nc)
    with ctx:
        wd = sb("wd", [P, EXPERTS, KH, F])
        bd_r = sb("bd_r", [1, EXPERTS, F])
        flat, at = m.acc[:, :, :].rearrange("p t c -> p (t c)"), 0
        views = []
        for a, b, c in ((2, GROUP, F), (2, GROUP, F), (1, KF, GROUP * P), (1, KH, GROUP * P)):
            views.append(flat[:, at:at + a * b * c].rearrange("p (a b c) -> p a b c", a=a, b=b))
            at += a * b * c
        xs, yb, xt, ht = views[0], views[1], views[2].squeeze(1), views[3].squeeze(1)
        turned = [ps(f"xturned{k}") for k in range(KF)]
        hid = [ps(f"xhid{k}") for k in range(4)]
        ybank = [ps(f"ybank{k}") for k in range(2)]
        s_wd, s_bd, s_xs, s_t, s_xt = sem("wd_loaded"), sem("bd_loaded"), [sem(f"tokens_loaded{k}") for k in range(2)], sem("tokens_turned"), sem("xt_ready")
        s_hid, s_ht, s_y, s_yk, s_ys = sem("hidden_done"), sem("gelu_done"), sem("y_done"), sem("y_kept"), [sem(f"y_stored{k}") for k in range(2)]
        s_back, s_out, s_fin = sem("y_back"), sem("out_ready"), sem("out_stored")
        block = ctx.enter_context(nc.Block())
        SG = SORTED_TILES // GROUP // 2

        def rows(table, g):
            return table[bass.ds(g * GROUP * P, GROUP * P), :].rearrange("(t p) c -> p t c", p=P)

        @block.sync
        def _(sp):
            sp.dma_start(bd_r[:, :, :], bd.unsqueeze(0)).then_inc(s_bd, 16)
            sp.sem_inc(s_t, 2)
            for h in range(2):
                sp.dma_start(xs[:, h, :, :], m.sorted_d[h * GROUP * P:(h + 1) * GROUP * P, :].rearrange("(t p) c -> p t c", p=P)).then_inc(s_xs[h], 16)
            for e in range(EXPERTS):
                sp.dma_start(wd[:, e, :, :], Wd[e].rearrange("(k p) c -> p k c", p=P)).then_inc(s_wd, 16)
            with sp.Fori(1, SG) as i:
                for h in range(2):
                    sp.wait_ge(s_t, 2 * i + h + 1)
                    sp.dma_start(xs[:, h, :, :], rows(m.sorted_d, 2 * i + h)).then_inc(s_xs[h], 16)
            for g in range(GROUPS - 1):
                sp.wait_ge(s_out, (g + 1) * GROUP)
                sp.dma_start(out[g * GROUP * P:(g + 1) * GROUP * P, :].rearrange("(t p) c -> p t c", p=P),
                             m.xres[:, g * GROUP:(g + 1) * GROUP, :]).then_inc(s_fin, 16)
            sp.wait_ge(s_out, NODE_TILES)
            sp.dma_start(out[(NODE_TILES - 1) * P:, :], m.xres[0:LAST, NODE_TILES - 1, :]).then_inc(s_fin, 16)
            sp.wait_ge(s_fin, 16 * GROUPS)

        @block.gpsimd
        def _(g):
            for h in range(2):
                g.wait_ge(s_ys[h], 16 * (SG + 1))
            for t in range(NODE_TILES):
                n = P if t < NODE_TILES - 1 else LAST
                g.indirect_dma_start(out=m.acc[0:n, t, 0:F], out_offset=None, in_=m.y_d,
                                     in_offset=bass.IndirectOffsetOnAxis(ap=m.pos[0:n, t:t + 1], axis=0)).then_inc(s_back, 16)

        @block.scalar
        def _(a):
            with a.Fori(0, SG) as i:
                for h in range(2):
                    g = 2 * i + h
                    for k in range(KH):
                        a.wait_ge(s_hid, g * KH + k + 1)
                        a.activation(ht[:, k, :], hid[k % 4][:, :], ACT.Gelu, bias=m.b1c[:, k:k + 1]).then_inc(s_ht, 1)
                    a.wait_ge(s_yk, (g + 1) * GROUP + 2)
                    a.dma_start(rows(m.y_d, g), yb[:, h, :, :]).then_inc(s_ys[h], 16)

        @block.vector
        def _(v):
            for h in range(2):
                v.sem_inc(s_ys[h], 16)
            with v.Fori(0, SG) as i:
                for h in range(2):
                    g = 2 * i + h
                    v.wait_ge(s_t, g + 3)
                    for f in range(KF):
                        last = v.tensor_copy(xt[:, f, :], turned[f][:, :])
                    last.then_inc(s_xt, 1)
                    v.wait_ge(s_ys[h], 16 * (i + 1))
                    for k in range(GROUP):
                        v.wait_ge(s_y, g * GROUP + k + 1)
                        v.tensor_copy(yb[:, h, k, :], ybank[k % 2][:, 0:F]).then_inc(s_yk, 1)
            v.wait_ge(s_back, 16 * NODE_TILES)
            for t in range(NODE_TILES):
                n = P if t < NODE_TILES - 1 else LAST
                v.scalar_tensor_tensor(m.xres[0:n, t, :], m.acc[0:n, t, 0:F], m.prob[0:n, t:t + 1], m.xres[0:n, t, :], ALU.mult, ALU.add).then_inc(s_out, 1)

        @block.tensor
        def _(pe):
            pe.sem_inc(s_ht, 4)
            pe.sem_inc(s_yk, 2)
            pe.wait_ge(s_bd, 16)
            pe.wait_ge(s_wd, 16 * EXPERTS)
            with pe.Fori(0, SG) as i:
                for h in range(2):
                    g = 2 * i + h
                    pe.wait_ge(s_xs[h], 16 * (i + 1))
                    for k in range(GROUP):
                        for f in range(KF):
                            last = pe.transpose(turned[f][:, k * P:(k + 1) * P], xs[:, h, k, f * P:(f + 1) * P], m.ident[:, :])
                    last.then_inc(s_t, 1)
                    pe.wait_ge(s_xt, g + 1)
                    for k in range(KH):
                        pe.wait_ge(s_ht, g * KH + k + 1)
                        for f in range(KF):
                            last = pe.matmul(hid[k % 4][:, :], m.w1[:, f, k * P:(k + 1) * P], xt[:, f, :], start=(f == 0), stop=(f == KF - 1))
                        last.then_inc(s_hid, 1)
                    _, expert = nc.values_load_multi_w_load_instructions(
                        m.eid[0:1, bass.ds(g * GROUP, GROUP)], engines=(mybir.EngineType.PE,), min_val=0, max_val=EXPERTS - 1,
                        skip_runtime_bounds_check_because="the smaller of a count and 7")
                    pe.wait_ge(s_ht, (g + 1) * KH + 4)
                    for k in range(GROUP):
                        pe.wait_ge(s_yk, g * GROUP + k + 1)
                        for f in range(KH):
                            pe.matmul(ybank[k % 2][:, 0:F], ht[:, f, k * P:(k + 1) * P], wd[:, bass.ds(expert[k], 1), f, :].squeeze(1), start=(f == 0), stop=False)
                        pe.matmul(ybank[k % 2][:, 0:F], m.ones[0:1, :], bd_r[0:1, bass.ds(expert[k], 1), :].squeeze(1), start=False, stop=True).then_inc(s_y, 1)


DEBUG = False


def dump(nc, m, out):
    ctx, sem, sb, ps = scope(nc)
    with ctx:
        s = sem("out_stored")
        block = ctx.enter_context(nc.Block())

        @block.sync
        def _(sp):
            full = NODE_TILES - 1
            sp.dma_start(out[0:full * P, :].rearrange("(t p) c -> p t c", p=P), m.xres[:, 0:full, :]).then_inc(s, 16)
            sp.dma_start(out[full * P:, :], m.xres[0:LAST, full, :]).then_inc(s, 16)
            sp.wait_ge(s, 32)


_INS = ['x', 'src', 'dst', 'L0_gnn_W', 'L0_gnn_a_src', 'L0_gnn_a_dst', 'L0_gnn_bias', 'L0_ffn_W1', 'L0_ffn_b1', 'L0_ffn_Wg',
        'L0_ffn_bg', 'L0_ffn_Wd', 'L0_ffn_bd']


def kernel(**inputs):
    import numpy as _np
    import concourse.bacc as _bacc
    from concourse import mybir as _mybir
    from concourse.bass_utils import run_bass_kernel_spmd as _run

    nc = _bacc.Bacc("TRN2", target_bir_lowering=False, num_devices=1)
    arrays, args = {}, []
    for name in _INS:
        a = _np.ascontiguousarray(inputs[name])
        arrays[f"in_{name}_dram"] = a
        args.append(nc.dram_tensor(f"in_{name}_dram", a.shape, _mybir.dt.from_np(a.dtype), kind="ExternalInput").ap())
    args.append(nc.dram_tensor("out_dram", (NODES, F), F32, kind="ExternalOutput").ap())
    build(nc, *args)
    r = _run(nc, [arrays], core_ids=[0])
    return r.results[0]["out_dram"]
```

```python
from contextlib import ExitStack

import numpy as np

import concourse.bass as bass
from concourse import mybir

F32 = mybir.dt.float32
BF16 = mybir.dt.bfloat16
I32 = mybir.dt.int32
ALU = mybir.AluOpType
ACT = mybir.ActivationFunctionType
AX = mybir.AxisListType

P = 128
NODES, EDGES, F = 6250, 100000, 256
HEADS, CH = 8, 32
HID, EXPERTS = 1024, 8
SLOPE, EPS = 0.2, 1e-5
NODE_TILES = -(-NODES // P)
GROUP = 4
GROUPS = -(-NODE_TILES // GROUP)
TILES = GROUPS * GROUP
LAST = NODES - (NODE_TILES - 1) * P
EDGE_TILES = -(-EDGES // P)
PAIRS = EDGE_TILES + NODE_TILES - 1
BATCH = 8
BATCHES = 105
UNROLL = 4
ROUNDS = BATCHES // UNROLL
RING = 4
BANKS = 4
PARTS = 3
PAIR_COLS = -(-(BATCHES + 3) * BATCH // P)
PAIR_PAD = PAIR_COLS * P
ROW = F + HEADS
PAD_DST = 16384
KF, KH = F // P, HID // P
SORTED_TILES = (NODES + EXPERTS * (P - 1)) // P
SORTED = SORTED_TILES * P
SPREAD = 40.0
HUGE = 3e38
GUARD = 1e-16 * float(np.exp(-SPREAD))


class Steps:

    def __init__(self, eng, sem):
        self.eng, self.sem, self.n = eng, sem, 0

    def then(self, ins):
        self.n += 1
        ins.then_inc(self.sem, 1)
        self.eng.wait_ge(self.sem, self.n)


def build(nc, x, src, dst, W, a_src, a_dst, bias, W1, b1, Wg, bg, Wd, bd, out):
    ctx = ExitStack()
    with ctx:
        def dram(name, shape, dt=F32):
            return nc.dram_tensor(name, shape, dt, kind="Internal").ap()

        def sb(name, shape, dt=F32):
            return ctx.enter_context(nc.sbuf_tensor(name, shape, dt))

        m = Shared()
        m.rows_d = dram("rows_d", (TILES * P, ROW))
        m.src_d = dram("src_d", (PAIR_PAD * P,), I32)
        m.dst_d = dram("dst_d", (PAIR_PAD * P,), I32)
        m.sorted_d = dram("sorted_d", (SORTED, F))
        m.y_d = dram("y_d", (SORTED, F))
        m.xres = sb("xres", [P, TILES, F])
        m.acc = sb("acc", [P, TILES, ROW])
        m.ident = sb("ident", [P, P])
        m.ones = sb("ones", [P, P])
        m.iota = sb("iota", [P, PAIR_PAD])
        m.iota_p = sb("iota_p", [P, 1])
        m.stats = sb("stats", [P, TILES, 6])
        m.mean = sb("mean", [P, TILES])
        m.rstd = sb("rstd", [P, TILES])
        m.tmp = sb("tmp", [P, TILES])
        with ExitStack() as edge:
            def esb(name, shape, dt=F32):
                return edge.enter_context(nc.sbuf_tensor(name, shape, dt))
            m.idx_t = esb("idx_t", [P, PAIR_PAD], I32)
            m.rel_t = esb("rel_t", [P, PAIR_PAD])
            m.node_t = esb("node_t", [1, PAIR_PAD], I32)
            m.score_t = esb("score_t", [P, TILES, 2 * HEADS])
            m.score_s = esb("score_s", [P, PARTS, TILES, 2 * HEADS], BF16)
            pair_tables(nc, m, src, dst)
            m.wide = esb("wide", [1, 1], I32)
            project(nc, m, x, W, a_src, a_dst)
            exact_bounds(nc, m)
            own_edges(nc, m)
            gather_edges(nc, m)
        finish_attention(nc, m, bias)
        m.w1 = sb("w1", [P, KF, HID])
        m.b1c = sb("b1c", [P, KH])
        m.prob = sb("prob", [P, TILES])
        m.pos = sb("pos", [P, TILES], I32)
        m.eid = sb("eid", [1, SORTED_TILES], I32)
        if DEBUG:
            dump(nc, m, out)
            return
        route(nc, m, W1, b1, Wg, bg)
        experts(nc, m, Wd, bd, out)


class Shared:
    pass


def scope(nc):
    ctx = ExitStack()
    sem = lambda name: ctx.enter_context(nc.semaphore(name))
    sb = lambda name, shape, dt=F32: ctx.enter_context(nc.sbuf_tensor(name, shape, dt))
    ps = lambda name, shape=(P, 512): ctx.enter_context(nc.psum_tensor(name, list(shape), F32))
    return ctx, sem, sb, ps


def layer_stats(v, m, chain):
    with v.Fori(0, GROUPS) as g:
        for k in range(GROUP):
            t = g * GROUP + k
            last = v.bn_stats(m.stats[:, bass.ds(t, 1), :].squeeze(1), m.xres[:, bass.ds(t, 1), :].squeeze(1))
        last.then_inc(chain.sem, 1)
    chain.n += GROUPS
    v.wait_ge(chain.sem, chain.n)
    st = m.stats
    chain.then(v.tensor_tensor(m.mean[:, :], st[:, :, 1], st[:, :, 4], ALU.add))
    chain.then(v.tensor_tensor(m.tmp[:, :], st[:, :, 1], st[:, :, 4], ALU.subtract))
    chain.then(v.tensor_tensor(m.tmp[:, :], m.tmp[:, :], m.tmp[:, :], ALU.mult))
    chain.then(v.tensor_tensor(m.rstd[:, :], st[:, :, 2], st[:, :, 5], ALU.add))
    chain.then(v.tensor_scalar(m.tmp[:, :], m.tmp[:, :], 0.25, EPS, ALU.mult, ALU.add))
    chain.then(v.tensor_scalar(m.mean[:, :], m.mean[:, :], 0.5, None, ALU.mult))
    chain.then(v.scalar_tensor_tensor(m.rstd[:, :], m.rstd[:, :], 1.0 / F, m.tmp[:, :], ALU.mult, ALU.add))


def pair_tables(nc, m, src, dst):
    ctx, sem, sb, ps = scope(nc)
    with ctx:
        PADN = PAIR_PAD * P - EDGES
        PADC = 153
        pad_src = sb("pad_src", [PADN // PADC, PADC], I32)
        pad_dst = sb("pad_dst", [PADN // PADC, PADC], I32)
        last_i = sb("last_i", [1, EDGE_TILES - 1], I32)
        last_f = sb("last_f", [1, EDGE_TILES - 1])
        iota_i = sb("iota_i", [P, PAIR_PAD], I32)
        iop_i = sb("iop_i", [P, 1], I32)
        bound = sb("bound", [P, 1])
        below = sb("below", [P, EDGE_TILES - 1])
        cnt = sb("cnt", [P, 1])
        turn = sb("turn", [P, 1])
        passed = sb("passed", [P, PAIR_PAD])
        inner = sb("inner", [P, 1])
        pair_i = sb("pair_i", [P, PAIR_COLS], I32)
        pair_f = sb("pair_f", [P, PAIR_COLS])
        tile_i = sb("tile_i", [P, PAIR_COLS], I32)
        first = sb("first", [P, PAIR_COLS])
        src_p = sb("src_p", [P, PAIR_COLS, P], I32)
        dst_p = sb("dst_p", [P, PAIR_COLS, P], I32)
        src_f = sb("src_f", [P, PAIR_COLS, P])
        rel_f = sb("rel_f", [P, PAIR_COLS, P])
        bank = [ps(f"tab{k}") for k in range(8)]
        s_fill, s_pad, s_edges, s_last = sem("fill"), sem("pads_stored"), sem("edges_stored"), sem("lasts_loaded")
        s_iota, s_ident, s_chain = sem("iota_made"), sem("ident_made"), sem("dve_step")
        s_lastf, s_bcast, s_passed, s_nodes = sem("lasts_ready"), sem("lasts_everywhere"), sem("passed_ready"), sem("nodes_ready")
        s_tile, s_rows, s_rel, s_tr = sem("tiles_ready"), sem("pair_rows_loaded"), sem("rel_ready"), sem("transposed")
        s_const = sem("constants_made")
        block = ctx.enter_context(nc.Block())

        @block.sync
        def _(sp):
            sp.dma_start(m.src_d[0:EDGES].rearrange("(a b) -> a b", a=16), src.rearrange("(a b) -> a b", a=16)).then_inc(s_edges, 16)
            sp.dma_start(m.dst_d[0:EDGES].rearrange("(a b) -> a b", a=16), dst.rearrange("(a b) -> a b", a=16)).then_inc(s_edges, 16)
            n = (EDGE_TILES - 1) * P
            with nc.allow_non_contiguous_dma(reason="the last destination of every full edge tile"):
                sp.dma_start(last_i[0:1, :], dst[0:n].rearrange("(t e) -> t e", e=P)[:, P - 1:P].rearrange("t a -> a t")).then_inc(s_last, 16)
            sp.wait_ge(s_fill, 2)
            sp.dma_start(m.src_d[EDGES:].rearrange("(a b) -> a b", b=PADC), pad_src[:, :]).then_inc(s_pad, 16)
            sp.dma_start(m.dst_d[EDGES:].rearrange("(a b) -> a b", b=PADC), pad_dst[:, :]).then_inc(s_pad, 16)

        @block.gpsimd
        def _(g):
            g.memset(pad_src[:, :], 0).then_inc(s_fill, 1)
            g.memset(pad_dst[:, :], PAD_DST).then_inc(s_fill, 1)
            g.iota(iota_i[:, :], [[1, PAIR_PAD]], base=0, channel_multiplier=0).then_inc(s_iota, 1)
            g.iota(iop_i[:, :], [[0, 1]], base=0, channel_multiplier=1).then_inc(s_iota, 1)
            g.iota(pair_i[:, :], [[P, PAIR_COLS]], base=0, channel_multiplier=1).then_inc(s_iota, 1)
            g.wait_ge(s_edges, 32)
            g.wait_ge(s_pad, 32)
            g.wait_ge(s_tile, 1)
            for j in range(PAIR_COLS):
                for table, rows in ((m.src_d, src_p), (m.dst_d, dst_p)):
                    g.indirect_dma_start(out=rows[:, j, :], out_offset=None, in_=table.rearrange("(t e) -> t e", e=P),
                                         in_offset=bass.IndirectOffsetOnAxis(ap=tile_i[:, j:j + 1], axis=0)).then_inc(s_rows, 16)

        @block.vector
        def _(v):
            chain = Steps(v, s_chain)
            v.memset(m.ones[:, :], 1.0).then_inc(s_const, 1)
            chain.then(v.memset(inner[:, :], 0.0))
            chain.then(v.memset(inner[0:NODE_TILES - 1, :], 1.0))
            v.wait_ge(s_last, 16)
            v.tensor_copy(last_f[:, :], last_i[:, :]).then_inc(s_lastf, 1)
            v.wait_ge(s_iota, 3)
            v.tensor_copy(m.iota[:, :], iota_i[:, :])
            v.tensor_copy(pair_f[:, :], pair_i[:, :])
            chain.then(v.tensor_copy(m.iota_p[:, :], iop_i[:, :]))
            v.tensor_scalar(m.ident[:, :], m.iota[:, 0:P], m.iota_p[:, 0:1], None, ALU.is_equal).then_inc(s_ident, 1)
            chain.then(v.tensor_scalar(bound[:, :], m.iota_p[:, :], float(P), float(P), ALU.mult, ALU.add))
            v.wait_ge(s_bcast, 1)
            v.tensor_scalar(below[:, 0:512], bank[0][:, :], bound[:, 0:1], None, ALU.is_lt)
            chain.then(v.tensor_scalar(below[:, 512:], bank[1][:, 0:EDGE_TILES - 1 - 512], bound[:, 0:1], None, ALU.is_lt))
            chain.then(v.tensor_reduce(cnt[:, :], below[:, :], axis=AX.X, op=ALU.add))
            chain.then(v.scalar_tensor_tensor(turn[:, :], cnt[:, :], 1.0, m.iota_p[:, :], ALU.add, ALU.add))
            v.tensor_scalar(passed[:, :], m.iota[:, :], turn[:, 0:1], None, ALU.is_ge).then_inc(s_passed, 1)
            v.wait_ge(s_nodes, 1)
            v.tensor_copy(m.node_t[:, 0:512], bank[2][0:1, :])
            v.tensor_copy(m.node_t[:, 512:], bank[3][0:1, 0:PAIR_PAD - 512])
            chain.then(v.tensor_copy(first[:, :], bank[4][:, 0:PAIR_COLS]))
            v.tensor_tensor(tile_i[:, :], pair_f[:, :], first[:, :], ALU.subtract).then_inc(s_tile, 1)
            chain.then(v.tensor_scalar(first[:, :], first[:, :], float(P), None, ALU.mult))
            v.wait_ge(s_rows, 32 * PAIR_COLS)
            v.tensor_copy(src_f[:, :, :], src_p[:, :, :])
            for j in range(PAIR_COLS):
                last = v.tensor_scalar(rel_f[:, j, :], dst_p[:, j, :], first[:, j:j + 1], None, ALU.subtract)
            last.then_inc(s_rel, 1)
            v.wait_ge(s_tr, 1)
            for table, b in ((m.idx_t, 4), (m.rel_t, 6)):
                v.tensor_copy(table[:, 0:512], bank[b][:, :])
                v.tensor_copy(table[:, 512:], bank[b + 1][:, 0:PAIR_PAD - 512])

        @block.tensor
        def _(pe):
            pe.wait_ge(s_const, 1)
            pe.wait_ge(s_lastf, 1)
            pe.matmul(bank[0][:, :], m.ones[0:1, :], last_f[0:1, 0:512], start=True, stop=True)
            pe.matmul(bank[1][:, 0:EDGE_TILES - 1 - 512], m.ones[0:1, :], last_f[0:1, 512:], start=True, stop=True).then_inc(s_bcast, 1)
            pe.wait_ge(s_passed, 1)
            pe.matmul(bank[2][0:1, :], inner[:, :], passed[:, 0:512], start=True, stop=True)
            pe.matmul(bank[3][0:1, 0:PAIR_PAD - 512], inner[:, :], passed[:, 512:], start=True, stop=True)
            for j in range(PAIR_COLS):
                last = pe.matmul(bank[4][:, j:j + 1], passed[:, j * P:(j + 1) * P], inner[:, :], start=True, stop=True)
            last.then_inc(s_nodes, 1)
            pe.wait_ge(s_ident, 1)
            pe.wait_ge(s_rel, 1)
            for rows, b in ((src_f, 4), (rel_f, 6)):
                for j in range(PAIR_COLS):
                    last = pe.transpose(bank[b + j // 4][:, (j % 4) * P:(j % 4 + 1) * P], rows[:, j, :], m.ident[:, :])
            last.then_inc(s_tr, 1)


def project(nc, m, x, W, a_src, a_dst):
    ctx, sem, sb, ps = scope(nc)
    with ctx:
        w = sb("w", [P, KF, F])
        a_col = sb("a_col", [P, KF, 2])
        a_blk = sb("a_blk", [P, KF, 2 * HEADS])
        head4 = sb("head4", [P, P // CH])
        wt = sb("wt", [P, KF, F + 2 * HEADS])
        xn = sb("xn", [P, GROUP, F])
        xt = sb("xt", [P, GROUP, F])
        ext = sb("ext", [P, 2 * HEADS])
        ext_c = sb("ext_c", [2 * HEADS, 1])
        ext_d = sb("ext_d", [2 * HEADS, 2 * HEADS])
        ext_b = sb("ext_b", [P, 2 * HEADS])
        width = sb("width", [1, HEADS])
        widest = sb("widest", [1, 1])
        low = [ps(f"pt{k}") for k in range(4)]
        high = [ps(f"pm{k}") for k in range(4)]
        s_xz, s_x, s_w, s_a = sem("x_zeroed"), sem("x_loaded"), sem("w_loaded"), sem("a_loaded")
        s_chain, s_blk, s_wt, s_wa, s_wtc = sem("dve_step"), sem("a_ready"), sem("w_transposed"), sem("wa_done"), sem("wt_ready")
        s_var, s_sd = sem("variance_ready"), sem("deviation_ready")
        s_xn, s_xfree, s_t, s_xt, s_mm, s_h = sem("xn_ready"), sem("xn_free"), sem("xn_transposed"), sem("xt_ready"), sem("h_done"), sem("h_kept")
        s_rows, s_ext, s_extT, s_extd, s_extb = (sem("rows_stored"), sem("extremes_ready"), sem("extremes_turned"),
            sem("extremes_diagonal"), sem("extremes_everywhere"))
        block = ctx.enter_context(nc.Block())

        @block.sync
        def _(sp):
            sp.wait_ge(s_xz, 1)
            full = (NODE_TILES - 1)
            for t0 in range(0, full, 12):
                sp.dma_start(m.xres[:, t0:t0 + 12, :], x[t0 * P:(t0 + 12) * P, :].rearrange("(t p) c -> p t c", p=P)).then_inc(s_x, 16)
            sp.dma_start(m.xres[0:LAST, full, :], x[full * P:, :]).then_inc(s_x, 16)
            with sp.Fori(0, GROUPS) as g:
                sp.wait_ge(s_h, (g + 1) * GROUP)
                sp.dma_start(m.rows_d[bass.ds(g * GROUP * P, GROUP * P), :].rearrange("(t p) c -> p t c", p=P),
                             m.acc[:, bass.ds(g * GROUP, GROUP), :]).then_inc(s_rows, 16)

        @block.gpsimd
        def _(g):
            g.memset(m.xres[:, NODE_TILES - 1:, :], 0.0).then_inc(s_xz, 1)

        @block.scalar
        def _(a):
            a.dma_start(w[:, :, :], W.rearrange("(k p) c -> p k c", p=P)).then_inc(s_w, 16)
            for n, vec in enumerate((a_src, a_dst)):
                with nc.allow_non_contiguous_dma(reason="a vector over the partitions"):
                    a.dma_start(a_col[:, :, n:n + 1], vec.rearrange("h c -> (h c)").rearrange("(k p a) -> p k a", p=P, a=1)).then_inc(s_a, 16)
            a.wait_ge(s_var, 1)
            a.activation(m.rstd[:, :], m.rstd[:, :], ACT.Sqrt).then_inc(s_sd, 1)
            with a.Fori(0, GROUPS) as g:
                for k in range(GROUP):
                    a.wait_ge(s_t, g * GROUP + k + 1)
                    a.activation(xt[:, k, :], low[k][:, 0:F], ACT.Copy).then_inc(s_xt, 1)

        @block.vector
        def _(v):
            chain = Steps(v, s_chain)
            for j in range(P // CH):
                chain.then(v.memset(head4[:, j:j + 1], 0.0))
                chain.then(v.memset(head4[j * CH:(j + 1) * CH, j:j + 1], 1.0))
            chain.then(v.memset(a_blk[:, :, :], 0.0))
            v.wait_ge(s_a, 32)
            for k in range(KF):
                for n in range(2):
                    h0 = n * HEADS + k * (P // CH)
                    last = v.tensor_scalar(a_blk[:, k, h0:h0 + P // CH], head4[:, :], a_col[:, k, n:n + 1], None, ALU.mult)
            last.then_inc(s_blk, 1)
            v.wait_ge(s_wa, 1)
            for k in range(KF):
                v.tensor_copy(wt[:, k, 0:F], low[k][:, 0:F])
                last = v.tensor_copy(wt[:, k, F:], low[2 + k][:, 0:2 * HEADS])
            last.then_inc(s_wtc, 1)
            v.wait_ge(s_x, 80)
            layer_stats(v, m, chain)
            v.sem_inc(s_var, 1)
            v.wait_ge(s_sd, 1)
            chain.then(v.reciprocal(m.rstd[:, :], m.rstd[:, :]))

            with v.Fori(0, GROUPS) as g:
                for k in range(GROUP):
                    t = g * GROUP + k
                    v.tensor_scalar(xn[:, k, :], m.xres[:, bass.ds(t, 1), :].squeeze(1), m.mean[:, bass.ds(t, 1)],
                                    m.rstd[:, bass.ds(t, 1)], ALU.subtract, ALU.mult).then_inc(s_xn, 1)
                for k in range(GROUP):
                    t = g * GROUP + k
                    v.wait_ge(s_mm, t + 1)
                    v.tensor_copy(m.acc[:, bass.ds(t, 1), :].squeeze(1), high[k][:, 0:ROW])
                    v.tensor_copy(m.score_t[:, bass.ds(t, 1), 0:HEADS].squeeze(1), high[k][:, ROW:ROW + HEADS]).then_inc(s_h, 1)
            v.wait_ge(s_h, TILES)
            as_h = m.acc[:, :, F:ROW].rearrange("p t h -> p h t")
            v.tensor_reduce(ext[:, 0:HEADS], as_h, axis=AX.X, op=ALU.max)
            chain.then(v.tensor_reduce(ext[:, HEADS:], as_h, axis=AX.X, op=ALU.min))
            v.tensor_scalar(ext[:, HEADS:], ext[:, HEADS:], -1.0, None, ALU.mult).then_inc(s_ext, 1)
            v.wait_ge(s_extT, 1)
            chain.then(v.tensor_reduce(ext_c[:, :], low[0][0:2 * HEADS, 0:P], axis=AX.X, op=ALU.max))
            v.tensor_scalar(ext_d[:, :], m.ident[0:2 * HEADS, 0:2 * HEADS], ext_c[:, 0:1], None, ALU.mult).then_inc(s_extd, 1)
            v.wait_ge(s_extb, 1)
            chain.then(v.tensor_copy(ext_b[:, :], low[1][:, 0:2 * HEADS]))
            dst_s, shift = m.score_t[:, :, 0:HEADS], m.score_t[:, :, HEADS:]
            chain.then(v.tensor_tensor(shift, dst_s, ext_b[:, 0:HEADS].unsqueeze(1).broadcast_to([P, TILES, HEADS]), ALU.add))
            chain.then(v.scalar_tensor_tensor(shift, shift, SLOPE, shift, ALU.mult, ALU.max))
            chain.then(v.tensor_tensor(width[:, :], ext_b[0:1, 0:HEADS], ext_b[0:1, HEADS:], ALU.add))
            chain.then(v.tensor_reduce(widest[:, :], width[:, :], axis=AX.X, op=ALU.max))
            chain.then(v.tensor_scalar(m.wide[:, :], widest[:, :], SPREAD, None, ALU.is_gt))
            v.wait_ge(s_rows, 16 * GROUPS)

        @block.tensor
        def _(pe):
            pe.wait_ge(s_w, 16)
            for ki in range(KF):
                for kc in range(KF):
                    pe.transpose(low[ki][:, kc * P:(kc + 1) * P], w[:, kc, ki * P:(ki + 1) * P], m.ident[:, :])
            pe.wait_ge(s_blk, 1)
            for ki in range(KF):
                for kc in range(KF):
                    last = pe.matmul(low[2 + ki][:, 0:2 * HEADS], w[:, kc, ki * P:(ki + 1) * P], a_blk[:, kc, :], start=(kc == 0), stop=(kc == KF - 1))
            last.then_inc(s_wa, 1)
            pe.wait_ge(s_wtc, 1)
            with pe.Fori(0, GROUPS) as g:
                for k in range(GROUP):
                    pe.wait_ge(s_xn, g * GROUP + k + 1)
                    for f in range(KF):
                        last = pe.transpose(low[k][:, f * P:(f + 1) * P], xn[:, k, f * P:(f + 1) * P], m.ident[:, :])
                    last.then_inc(s_t, 1)
                for k in range(GROUP):
                    pe.wait_ge(s_xt, g * GROUP + k + 1)
                    for f in range(KF):
                        last = pe.matmul(high[k][:, 0:F + 2 * HEADS], xt[:, k, f * P:(f + 1) * P], wt[:, f, :], start=(f == 0), stop=(f == KF - 1))
                    last.then_inc(s_mm, 1)
            pe.wait_ge(s_ext, 1)
            pe.transpose(low[0][0:2 * HEADS, 0:P], ext[:, :], m.ident[:, :]).then_inc(s_extT, 1)
            pe.wait_ge(s_extd, 1)
            pe.matmul(low[1][:, 0:2 * HEADS], m.ones[0:2 * HEADS, :], ext_d[:, :], start=True, stop=True).then_inc(s_extb, 1)


def exact_bounds(nc, m):
    ctx, sem, sb, ps = scope(nc)
    with ctx:
        best = sb("best", [P, TILES, HEADS])
        idx1 = sb("idx1", [P, 1], I32)
        row1 = sb("row1", [P, ROW])
        hot1 = sb("hot1", [P, P])
        off1 = sb("off1", [P, P])
        held = sb("held", [P, HEADS, P])
        top = sb("top", [P, HEADS])
        bank = [ps(f"held_t{k}") for k in range(2)]
        s_i, s_r, s_held, s_t, s_c, s_b = sem("pair_idx_ready"), sem("pair_rows"), sem("held_ready"), sem("held_turned"), sem("pair_step"), sem("dve_step")
        STEPS = 4
        block = ctx.enter_context(nc.Block())

        def when_wide(eng, engine):
            wide = nc.values_load_multi_w_load_instructions(m.wide[0:1, 0:1], engines=(engine,), min_val=0, max_val=1,
                                                            skip_runtime_bounds_check_because="the result of a comparison")[1][0]
            return eng.If(wide > 0)

        @block.gpsimd
        def _(g):
            with when_wide(g, mybir.EngineType.Pool):
                with g.Fori(0, PAIRS) as p:
                    g.wait_ge(s_i, p + 1)
                    g.nop(nofuse=True)
                    g.indirect_dma_start(out=row1[:, :], out_offset=None, in_=m.rows_d,
                                         in_offset=bass.IndirectOffsetOnAxis(ap=idx1[:, 0:1], axis=0)).then_inc(s_r, 16)
            g.nop(nofuse=True)

        @block.vector
        def _(v):
            with when_wide(v, mybir.EngineType.DVE):
                chain = Steps(v, s_b)
                chain.then(v.tensor_copy(best[:, :, :], m.acc[:, :, F:ROW]))
                with v.Fori(0, PAIRS) as p:
                    v.tensor_copy(idx1[:, :], m.idx_t[:, bass.ds(p, 1)]).then_inc(s_i, 1)
                    v.tensor_scalar(hot1[:, :], m.iota[:, 0:P], m.rel_t[:, bass.ds(p, 1)], None, ALU.is_equal).then_inc(s_c, 1)
                    v.wait_ge(s_c, p * STEPS + 1)
                    v.tensor_scalar(off1[:, :], hot1[:, :], HUGE, HUGE, ALU.mult, ALU.subtract).then_inc(s_c, 1)
                    v.wait_ge(s_c, p * STEPS + 2)
                    v.wait_ge(s_r, 16 * p + 16)
                    for h in range(HEADS):
                        last = v.scalar_tensor_tensor(held[:, h, :], hot1[:, :], row1[:, F + h:F + h + 1], off1[:, :], ALU.mult, ALU.add)
                    last.then_inc(s_held, 1)
                    node = nc.values_load_multi_w_load_instructions(
                        m.node_t[0:1, bass.ds(p, 1)], engines=(mybir.EngineType.DVE,), min_val=0, max_val=NODE_TILES - 1,
                        skip_runtime_bounds_check_because="counts at most 48 turns")[1][0]
                    v.wait_ge(s_t, p + 1)
                    for k in range(2):
                        last = v.tensor_reduce(top[:, 4 * k:4 * k + 4], bank[k][:, :].rearrange("p (h e) -> p h e", e=P), axis=AX.X, op=ALU.max)
                    last.then_inc(s_c, 1)
                    v.wait_ge(s_c, p * STEPS + 3)
                    b = best[:, bass.ds(node, 1), :].squeeze(1)
                    v.tensor_tensor(b, b, top[:, :], ALU.max).then_inc(s_c, 1)
                    v.wait_ge(s_c, p * STEPS + 4)
                shift = m.score_t[:, :, HEADS:]
                chain.then(v.tensor_tensor(shift, m.score_t[:, :, 0:HEADS], best[:, :, :], ALU.add))
                chain.then(v.scalar_tensor_tensor(shift, shift, SLOPE, shift, ALU.mult, ALU.max))
            v.nop(nofuse=True)

        @block.tensor
        def _(pe):
            with when_wide(pe, mybir.EngineType.PE):
                with pe.Fori(0, PAIRS) as p:
                    pe.wait_ge(s_held, p + 1)
                    for h in range(HEADS):
                        last = pe.transpose(bank[h // 4][:, (h % 4) * P:(h % 4 + 1) * P], held[:, h, :], m.ident[:, :])
                    last.then_inc(s_t, 1)
            pe.nop(nofuse=True)


def own_edges(nc, m):
    ctx, sem, sb, ps = scope(nc)
    with ctx:
        own = sb("own", [P, TILES, HEADS])
        rest_b = sb("rest_b", [P, TILES, 2 * HEADS])
        s_chain, s_own, s_ownx = sem("dve_step"), sem("own_ready"), sem("own_exp")
        block = ctx.enter_context(nc.Block())

        @block.scalar
        def _(a):
            a.wait_ge(s_own, 1)
            a.activation(m.acc[:, :, F:ROW], own[:, :, :], ACT.Exp).then_inc(s_ownx, 1)

        @block.vector
        def _(v):
            chain = Steps(v, s_chain)
            rest = rest_b[:, :, :]
            chain.then(v.tensor_copy(m.score_s[:, 0, :, :], m.score_t[:, :, :]))
            chain.then(v.tensor_tensor(rest, m.score_t[:, :, :], m.score_s[:, 0, :, :], ALU.subtract))
            chain.then(v.tensor_copy(m.score_s[:, 1, :, :], rest))
            chain.then(v.tensor_tensor(rest, rest, m.score_s[:, 1, :, :], ALU.subtract))
            chain.then(v.tensor_copy(m.score_s[:, 2, :, :], rest))
            dst_s, shift = m.score_t[:, :, 0:HEADS], m.score_t[:, :, HEADS:]
            chain.then(v.tensor_tensor(own[:, :, :], dst_s, m.acc[:, :, F:ROW], ALU.add))
            chain.then(v.scalar_tensor_tensor(own[:, :, :], own[:, :, :], SLOPE, own[:, :, :], ALU.mult, ALU.max))
            v.tensor_tensor(own[:, :, :], own[:, :, :], shift, ALU.subtract).then_inc(s_own, 1)
            v.wait_ge(s_ownx, 1)
            hh = m.acc[:, :, 0:F].rearrange("p t (h c) -> p t h c", h=HEADS)
            chain.then(v.tensor_tensor(hh, hh, m.acc[:, :, F:ROW].unsqueeze(3).broadcast_to([P, TILES, HEADS, CH]), ALU.mult))


def gather_edges(nc, m):
    ctx, sem, sb, ps = scope(nc)
    with ctx:
        idx = sb("idx", [P, RING, BATCH], I32)
        rows = sb("rows", [P, RING, BATCH, ROW])
        msg = sb("msg", [P, 2, BATCH, ROW])
        hot = sb("hot", [P, 4, BATCH, P])
        hot_t = sb("hot_t", [P, 2, BATCH, P], BF16)
        dst_z = sb("dst_z", [P, 4, BATCH, 2 * HEADS])
        z = sb("z", [P, 2, BATCH, HEADS])
        turn = [ps(f"turn{k}") for k in range(2)]
        dsts = ps("dsts")
        sums = [ps(f"sums{k}") for k in range(BANKS)]
        s_idx, s_rows = sem("idx_ready"), [sem(f"rows_gathered{k}") for k in range(RING)]
        s_free, s_hot, s_turn, s_hott = sem("rows_free"), sem("hot_ready"), sem("hot_turned"), sem("hot_t_ready")
        s_dst, s_dz, s_z, s_e, s_msg = sem("dst_scores_ready"), sem("dst_scores_kept"), sem("z_ready"), sem("exp_ready"), sem("msg_ready")
        s_sum, s_acc, s_step = sem("sums_ready"), sem("sums_added"), sem("dve_step")
        block = ctx.enter_context(nc.Block())

        def node_tiles(engine, first, n):
            return nc.values_load_multi_w_load_instructions(
                m.node_t[0:1, bass.ds(first, n)], engines=(engine,), min_val=0, max_val=NODE_TILES - 1,
                skip_runtime_bounds_check_because="counts at most 48 turns")[1]

        def all_batches(eng, body):
            body(0, 0, 0)
            with eng.Fori(0, ROUNDS) as i:
                for j in range(1, UNROLL + 1):
                    body(UNROLL * i + j, j % UNROLL, i + j // UNROLL)

        @block.sync
        def _(sp):
            pass

        @block.gpsimd
        def _(g):
            def gather(b, r, n):
                h = r % RING
                g.wait_ge(s_idx, b + 1)
                g.nop(nofuse=True)
                for k in range(BATCH):
                    g.indirect_dma_start(out=rows[:, h, k, :], out_offset=None, in_=m.rows_d,
                                         in_offset=bass.IndirectOffsetOnAxis(ap=idx[:, h, k:k + 1], axis=0)).then_inc(s_rows[h], 16)

            all_batches(g, gather)

        @block.scalar
        def _(a):
            def give_idx(b, r):
                a.wait_ge(s_free, b + 1)
                a.activation(idx[:, r % RING, :], m.idx_t[:, bass.ds(b * BATCH, BATCH)], ACT.Copy).then_inc(s_idx, 1)

            def turned(b, r):
                a.wait_ge(s_turn, b + 1)
                for k in range(2):
                    last = a.activation(hot_t[:, r % 2, 4 * k:4 * k + 4, :], turn[k][:, :].rearrange("p (k e) -> p k e", e=P), ACT.Copy)
                last.then_inc(s_hott, 1)

            def keep_scores(b, r):
                a.wait_ge(s_dst, b + 1)
                a.activation(dst_z[:, r % 4, :, :], dsts[:, 0:BATCH * 2 * HEADS].rearrange("p (k c) -> p k c", k=BATCH), ACT.Copy).then_inc(s_dz, 1)

            def batch(b, r, n):
                a.wait_ge(s_z, b + 1)
                a.activation(msg[:, r % 2, :, F:ROW], z[:, r % 2, :, :], ACT.Exp).then_inc(s_e, 1)
                give_idx(b + RING - 1, r + RING - 1)
                turned(b + 2, r + 2)
                keep_scores(b + 1, r + 1)

            a.sem_inc(s_free, RING)
            for b in range(RING - 1):
                give_idx(b, b)
            turned(0, 0)
            turned(1, 1)
            keep_scores(0, 0)
            all_batches(a, batch)

        @block.vector
        def _(v):
            def make_hot(b, r, ks=(0, BATCH)):
                n = ks[1] - ks[0]
                col = m.rel_t[:, bass.ds(b * BATCH + ks[0], n)]
                v.tensor_tensor(hot[:, r % 4, ks[0]:ks[1], :], m.iota[:, 0:P].unsqueeze(1).broadcast_to([P, n, P]),
                                col.unsqueeze(2).broadcast_to([P, n, P]), ALU.is_equal).then_inc(s_hot, 1)

            def add_sum(b, k, node):
                p = b * BATCH + k
                v.wait_ge(s_sum, p + 1)
                v.wait_ge(s_acc, p + BANKS)
                a = m.acc[:, bass.ds(node, 1), :].squeeze(1)
                v.tensor_tensor(a, a, sums[k % BANKS][:, 0:ROW], ALU.add).then_inc(s_acc, 1)

            def messages(b, r, q):
                h = r % 2
                v.tensor_tensor(msg[:, h, q:q + 2, 0:F].rearrange("p k (h c) -> p k h c", h=HEADS),
                                rows[:, r % RING, q:q + 2, 0:F].rearrange("p k (h c) -> p k h c", h=HEADS),
                                msg[:, h, q:q + 2, F:ROW].unsqueeze(3).broadcast_to([P, 2, HEADS, CH]), ALU.mult).then_inc(s_msg, 1)

            def batch(b, r, n, first=False):
                h = r % 2
                zz = z[:, h, :, :]
                last4 = None if first else node_tiles(mybir.EngineType.DVE, b * BATCH - 4, 4)
                v.wait_ge(s_rows[r % RING], 16 * BATCH * (n + 1))
                v.wait_ge(s_dz, b + 1)
                v.tensor_tensor(zz, rows[:, r % RING, :, F:ROW], dst_z[:, r % 4, :, 0:HEADS], ALU.add).then_inc(s_step, 1)
                if not first:
                    add_sum(b - 1, 4, last4[0])
                v.wait_ge(s_step, 2 * b + 1)
                v.scalar_tensor_tensor(zz, zz, SLOPE, zz, ALU.mult, ALU.max).then_inc(s_step, 1)
                if not first:
                    add_sum(b - 1, 5, last4[1])
                v.wait_ge(s_step, 2 * b + 2)
                v.tensor_tensor(zz, zz, dst_z[:, r % 4, :, HEADS:], ALU.subtract).then_inc(s_z, 1)
                if not first:
                    add_sum(b - 1, 6, last4[2])
                make_hot(b + 3, r + 3, (0, 2))
                if not first:
                    add_sum(b - 1, 7, last4[3])
                first4 = node_tiles(mybir.EngineType.DVE, b * BATCH, 4)
                v.wait_ge(s_e, b + 1)
                messages(b, r, 0)
                messages(b, r, 2)
                make_hot(b + 3, r + 3, (2, 4))
                add_sum(b, 0, first4[0])
                messages(b, r, 4)
                add_sum(b, 1, first4[1])
                messages(b, r, 6)
                add_sum(b, 2, first4[2])
                make_hot(b + 3, r + 3, (4, 8))
                v.wait_ge(s_msg, 4 * b + 4)
                v.sem_inc(s_free, 1)
                add_sum(b, 3, first4[3])

            v.sem_inc(s_acc, BANKS)
            for b in range(3):
                for ks in ((0, 2), (2, 4), (4, 8)):
                    make_hot(b, b, ks)
            batch(0, 0, 0, first=True)
            with v.Fori(0, ROUNDS) as i:
                for j in range(1, UNROLL + 1):
                    batch(UNROLL * i + j, j % UNROLL, i + j // UNROLL)
            node = node_tiles(mybir.EngineType.DVE, BATCHES * BATCH - 4, 4)
            for k in range(4):
                add_sum(BATCHES - 1, 4 + k, node[k])

        @block.tensor
        def _(pe):
            def turn_hot(b, r, first=False):
                pe.wait_ge(s_hot, 3 * b + 3)
                if not first:
                    pe.wait_ge(s_hott, b)
                for k in range(BATCH):
                    last = pe.transpose(turn[k // 4][:, (k % 4) * P:(k % 4 + 1) * P], hot[:, r % 4, k, :], m.ident[:, :])
                last.then_inc(s_turn, 1)

            def dst_scores(b, r, node, k):
                for part in range(PARTS):
                    last = pe.matmul(dsts[:, k * 2 * HEADS:(k + 1) * 2 * HEADS], hot_t[:, r % 2, k, :],
                                     m.score_s[:, part, bass.ds(node[k], 1), :].squeeze(1), start=(part == 0), stop=(part == PARTS - 1))
                if k == BATCH - 1:
                    last.then_inc(s_dst, 1)

            def batch(b, r, n):
                node = node_tiles(mybir.EngineType.PE, (b + 1) * BATCH, BATCH)
                turn_hot(b + 2, r + 2)
                for k in range(BATCH):
                    if k % 2 == 0:
                        pe.wait_ge(s_msg, 4 * b + k // 2 + 1)
                    pe.wait_ge(s_acc, b * BATCH + k + 1)
                    pe.matmul(sums[k % BANKS][:, 0:ROW], hot[:, r % 4, k, :], msg[:, r % 2, k, :], start=True, stop=True).then_inc(s_sum, 1)
                    if k == 0:
                        pe.wait_ge(s_hott, b + 2)
                        pe.wait_ge(s_dz, b + 1)
                    if k < BATCH // 2:
                        dst_scores(b + 1, r + 1, node, 2 * k)
                        dst_scores(b + 1, r + 1, node, 2 * k + 1)

            turn_hot(0, 0, first=True)
            turn_hot(1, 1)
            node = node_tiles(mybir.EngineType.PE, 0, BATCH)
            for k in range(BATCH):
                dst_scores(0, 0, node, k)
            all_batches(pe, batch)


def finish_attention(nc, m, bias):
    ctx, sem, sb, ps = scope(nc)
    with ctx:
        den = sb("den", [P, TILES, HEADS])
        bias_b = sb("bias_b", [P, F])
        s_bias, s_chain, s_var, s_sd = sem("bias_loaded"), sem("dve_step"), sem("variance_ready"), sem("deviation_ready")
        block = ctx.enter_context(nc.Block())

        @block.sync
        def _(sp):
            sp.dma_start(bias_b[:, :], bias.partition_broadcast(P)).then_inc(s_bias, 16)

        @block.scalar
        def _(a):
            a.wait_ge(s_var, 1)
            a.activation(m.rstd[:, :], m.rstd[:, :], ACT.Sqrt).then_inc(s_sd, 1)

        @block.vector
        def _(v):
            chain = Steps(v, s_chain)
            a = m.acc[:, :, 0:F]
            chain.then(v.tensor_scalar(den[:, :, :], m.acc[:, :, F:ROW], GUARD, None, ALU.add))
            chain.then(v.reciprocal(den[:, :, :], den[:, :, :]))
            ah = a.rearrange("p t (h c) -> p t h c", h=HEADS)
            chain.then(v.tensor_tensor(ah, ah, den[:, :, :].unsqueeze(3).broadcast_to([P, TILES, HEADS, CH]), ALU.mult))
            chain.then(v.tensor_tensor(m.xres[:, :, :], m.xres[:, :, :], a, ALU.add))
            v.wait_ge(s_bias, 16)
            chain.then(v.tensor_tensor(m.xres[:, :, :], m.xres[:, :, :], bias_b[:, :].unsqueeze(1).broadcast_to([P, TILES, F]), ALU.add))
            layer_stats(v, m, chain)
            v.sem_inc(s_var, 1)
            v.wait_ge(s_sd, 1)
            chain.then(v.reciprocal(m.rstd[:, :], m.rstd[:, :]))

        @block.gpsimd
        def _(g):
            pass

        @block.tensor
        def _(pe):
            pass



def route(nc, m, W1, b1, Wg, bg):
    ctx, sem, sb, ps = scope(nc)
    with ctx:
        wg = sb("wg", [P, KH, EXPERTS])
        bg_b = sb("bg_b", [P, EXPERTS])
        xn = sb("xn2", [P, GROUP, F])
        xt = sb("xt2", [P, KF, GROUP * P])
        ht = sb("ht", [P, KH, GROUP * P])
        logit = sb("logit", [P, TILES, EXPERTS])
        onehot = sb("onehot", [P, TILES, EXPERTS])
        before = sb("before", [P, TILES, EXPERTS])
        tot = sb("tot", [P, TILES, EXPERTS])
        run = [sb(f"run{k}", [P, TILES, EXPERTS]) for k in range(2)]
        seen = sb("seen", [P, TILES])
        valid = sb("valid", [P, TILES])
        tok_i = sb("tok_i", [P, TILES], I32)
        upper = sb("upper", [P, P])
        thr = sb("thr", [P, NODE_TILES])
        need = sb("need", [P, EXPERTS, NODE_TILES])
        ntile = sb("ntile", [P, EXPERTS])
        cum = [sb(f"cum{k}", [P, EXPERTS]) for k in range(2)]
        base = sb("base", [P, EXPERTS])
        ends = sb("ends", [1, SORTED_TILES, EXPERTS])
        eid_f = sb("eid_f", [1, SORTED_TILES])
        pos_f = sb("pos_f", [P, TILES])
        zeros = sb("zeros", [P, F])
        turned = [ps(f"turned{k}") for k in range(KF)]
        hid = [ps(f"hid{k}") for k in range(4)]
        gate = ps("gate")
        totals = ps("totals")
        s_w1, s_wg, s_zero, s_zeroed, s_tok = sem("w1_loaded"), sem("wg_loaded"), sem("zeros_made"), sem("sorted_zeroed"), sem("token_ids")
        s_xn, s_t, s_xt, s_hid, s_ht, s_gate, s_kept = (sem("xn_ready"), sem("xn_turned"), sem("xt_ready"), sem("hidden_done"),
            sem("gelu_done"), sem("gates_done"), sem("gates_kept"))
        s_chain, s_max, s_exp, s_oh, s_cnt, s_pos, s_scat = (sem("dve_step"), sem("max_taken"), sem("exp_done"), sem("onehot_ready"),
            sem("counted"), sem("places_ready"), sem("tokens_sorted"))
        block = ctx.enter_context(nc.Block())

        @block.sync
        def _(sp):
            sp.dma_start(m.w1[:, :, :], W1.rearrange("(k p) c -> p k c", p=P)).then_inc(s_w1, 16)
            with nc.allow_non_contiguous_dma(reason="a bias over the partitions"):
                sp.dma_start(m.b1c[:, :], b1.rearrange("(k p) -> p k", p=P)).then_inc(s_w1, 16)
            sp.dma_start(wg[:, :, :], Wg.rearrange("(k p) c -> p k c", p=P)).then_inc(s_wg, 16)
            sp.dma_start(bg_b[:, :], bg.partition_broadcast(P)).then_inc(s_wg, 16)
            sp.wait_ge(s_zero, 1)
            sp.dma_start(m.sorted_d.rearrange("(t p) c -> p t c", p=P),
                         zeros[:, :].unsqueeze(1).broadcast_to([P, SORTED_TILES, F])).then_inc(s_zeroed, 16)

        @block.gpsimd
        def _(g):
            g.memset(zeros[:, :], 0.0).then_inc(s_zero, 1)
            g.iota(tok_i[:, :], [[P, TILES]], base=0, channel_multiplier=1).then_inc(s_tok, 1)
            g.wait_ge(s_zeroed, 16)
            g.wait_ge(s_pos, 1)
            for t in range(NODE_TILES):
                n = P if t < NODE_TILES - 1 else LAST
                g.indirect_dma_start(out=m.sorted_d, out_offset=bass.IndirectOffsetOnAxis(ap=m.pos[0:n, t:t + 1], axis=0),
                                     in_=m.acc[0:n, t, 0:F], in_offset=None).then_inc(s_scat, 16)
            g.wait_ge(s_scat, 16 * NODE_TILES)
            g.nop(nofuse=True)

        @block.scalar
        def _(a):
            a.wait_ge(s_w1, 32)
            with a.Fori(0, GROUPS) as g:
                for k in range(KH):
                    a.wait_ge(s_hid, g * KH + k + 1)
                    a.activation(ht[:, k, :], hid[k % 4][:, :], ACT.Gelu, bias=m.b1c[:, k:k + 1]).then_inc(s_ht, 1)
            a.wait_ge(s_max, 1)
            a.activation(logit[:, :, :], logit[:, :, :], ACT.Exp).then_inc(s_exp, 1)

        @block.vector
        def _(v):
            chain = Steps(v, s_chain)

            def normal(to, t):
                return v.tensor_scalar(to, m.xres[:, bass.ds(t, 1), :].squeeze(1),
                                       m.mean[:, bass.ds(t, 1)], m.rstd[:, bass.ds(t, 1)], ALU.subtract, ALU.mult)

            with v.Fori(0, GROUPS) as g:
                for k in range(GROUP):
                    t = g * GROUP + k
                    last = normal(xn[:, k, :], t)
                last.then_inc(s_xn, 1)
                for k in range(GROUP):
                    normal(m.acc[:, bass.ds(g * GROUP + k, 1), 0:F].squeeze(1), g * GROUP + k)
                v.wait_ge(s_t, g + 1)
                for f in range(KF):
                    last = v.tensor_copy(xt[:, f, :], turned[f][:, :])
                last.then_inc(s_xt, 1)
                v.wait_ge(s_gate, g + 1)
                v.tensor_copy(logit[:, bass.ds(g * GROUP, GROUP), :], gate[:, 0:GROUP * EXPERTS].rearrange("p (t e) -> p t e", e=EXPERTS)).then_inc(s_kept, 1)
            v.wait_ge(s_kept, GROUPS)
            v.wait_ge(s_wg, 32)
            chain.then(v.tensor_tensor(logit[:, :, :], logit[:, :, :], bg_b[:, :].unsqueeze(1).broadcast_to([P, TILES, EXPERTS]), ALU.add))
            chain.then(v.tensor_reduce(seen[:, :], logit[:, :, :], axis=AX.X, op=ALU.max))
            wide = seen[:, :].unsqueeze(2).broadcast_to([P, TILES, EXPERTS])
            v.tensor_tensor(logit[:, :, :], logit[:, :, :], wide, ALU.subtract).then_inc(s_max, 1)
            v.wait_ge(s_exp, 1)
            chain.then(v.tensor_reduce(seen[:, :], logit[:, :, :], axis=AX.X, op=ALU.add))
            chain.then(v.reciprocal(seen[:, :], seen[:, :]))
            chain.then(v.tensor_tensor(logit[:, :, :], logit[:, :, :], wide, ALU.mult))
            chain.then(v.tensor_reduce(m.prob[:, :], logit[:, :, :], axis=AX.X, op=ALU.max))
            chain.then(v.tensor_tensor(logit[:, :, :], logit[:, :, :], m.prob[:, :].unsqueeze(2).broadcast_to([P, TILES, EXPERTS]), ALU.is_ge))
            v.wait_ge(s_tok, 1)
            chain.then(v.tensor_copy(valid[:, :], tok_i[:, :]))
            chain.then(v.tensor_scalar(valid[:, :], valid[:, :], float(NODES), None, ALU.is_lt))
            chain.then(v.memset(seen[:, :], 0.0))
            for e in range(EXPERTS):
                chain.then(v.tensor_tensor(onehot[:, :, e], logit[:, :, e], seen[:, :], ALU.is_gt))
                chain.then(v.tensor_tensor(seen[:, :], seen[:, :], logit[:, :, e], ALU.max))
            chain.then(v.tensor_scalar(upper[:, :], m.iota[:, 0:P], m.iota_p[:, 0:1], None, ALU.is_gt))
            v.tensor_tensor(onehot[:, :, :], onehot[:, :, :], valid[:, :].unsqueeze(2).broadcast_to([P, TILES, EXPERTS]), ALU.mult).then_inc(s_oh, 1)
            v.wait_ge(s_cnt, 1)
            flat = lambda b: b[:, :, :].rearrange("p t e -> p (t e)")
            v.tensor_copy(flat(before), turned[0][:, 0:TILES * EXPERTS])
            chain.then(v.tensor_copy(flat(tot), totals[:, 0:TILES * EXPERTS]))
            chain.then(v.tensor_copy(flat(run[0]), flat(tot)))
            n, s = 0, 1
            while s < TILES:
                v.tensor_copy(run[1 - n][:, 0:s, :], run[n][:, 0:s, :])
                chain.then(v.tensor_tensor(run[1 - n][:, s:, :], run[n][:, s:, :], run[n][:, 0:TILES - s, :], ALU.add))
                n, s = 1 - n, 2 * s
            count = run[n][:, TILES - 1, :]
            chain.then(v.tensor_scalar(thr[:, :], m.iota[:, 0:NODE_TILES], float(P), None, ALU.mult))
            chain.then(v.tensor_tensor(need[:, :, :], count.unsqueeze(2).broadcast_to([P, EXPERTS, NODE_TILES]),
                                       thr[:, :].unsqueeze(1).broadcast_to([P, EXPERTS, NODE_TILES]), ALU.is_gt))
            chain.then(v.tensor_reduce(ntile[:, :], need[:, :, :], axis=AX.X, op=ALU.add))
            chain.then(v.tensor_copy(cum[0][:, :], ntile[:, :]))
            c, s = 0, 1
            while s < EXPERTS:
                v.tensor_copy(cum[1 - c][:, 0:s], cum[c][:, 0:s])
                chain.then(v.tensor_tensor(cum[1 - c][:, s:], cum[c][:, s:], cum[c][:, 0:EXPERTS - s], ALU.add))
                c, s = 1 - c, 2 * s
            chain.then(v.tensor_tensor(base[:, :], cum[c][:, :], ntile[:, :], ALU.subtract))
            chain.then(v.tensor_scalar(base[:, :], base[:, :], float(P), None, ALU.mult))
            chain.then(v.tensor_tensor(before[:, :, :], before[:, :, :], run[n][:, :, :], ALU.add))
            chain.then(v.tensor_tensor(before[:, :, :], before[:, :, :], tot[:, :, :], ALU.subtract))
            chain.then(v.tensor_tensor(before[:, :, :], before[:, :, :], base[:, :].unsqueeze(1).broadcast_to([P, TILES, EXPERTS]), ALU.add))
            chain.then(v.tensor_tensor(before[:, :, :], before[:, :, :], onehot[:, :, :], ALU.mult))
            chain.then(v.tensor_reduce(pos_f[:, :], before[:, :, :], axis=AX.X, op=ALU.add))
            v.tensor_copy(m.pos[:, :], pos_f[:, :]).then_inc(s_pos, 1)
            chain.then(v.tensor_tensor(ends[:, :, :], m.iota[0:1, 0:SORTED_TILES].unsqueeze(2).broadcast_to([1, SORTED_TILES, EXPERTS]),
                                       cum[c][0:1, :].unsqueeze(1).broadcast_to([1, SORTED_TILES, EXPERTS]), ALU.is_ge))
            chain.then(v.tensor_reduce(eid_f[:, :], ends[:, :, :], axis=AX.X, op=ALU.add))
            chain.then(v.tensor_scalar(m.eid[:, :], eid_f[:, :], float(EXPERTS - 1), None, ALU.min))

        @block.tensor
        def _(pe):
            pe.wait_ge(s_w1, 32)
            pe.wait_ge(s_wg, 32)
            pe.sem_inc(s_ht, 4)
            with pe.Fori(0, GROUPS) as g:
                pe.wait_ge(s_xn, g + 1)
                for k in range(GROUP):
                    for f in range(KF):
                        last = pe.transpose(turned[f][:, k * P:(k + 1) * P], xn[:, k, f * P:(f + 1) * P], m.ident[:, :])
                last.then_inc(s_t, 1)
                pe.wait_ge(s_xt, g + 1)
                for k in range(KH):
                    pe.wait_ge(s_ht, g * KH + k + 1)
                    for f in range(KF):
                        last = pe.matmul(hid[k % 4][:, :], m.w1[:, f, k * P:(k + 1) * P], xt[:, f, :], start=(f == 0), stop=(f == KF - 1))
                    last.then_inc(s_hid, 1)
                pe.wait_ge(s_ht, (g + 1) * KH + 4)
                for k in range(GROUP):
                    for f in range(KH):
                        last = pe.matmul(gate[:, k * EXPERTS:(k + 1) * EXPERTS], ht[:, f, k * P:(k + 1) * P], wg[:, f, :], start=(f == 0), stop=(f == KH - 1))
                last.then_inc(s_gate, 1)
            pe.wait_ge(s_oh, 1)
            oh = onehot[:, :, :].rearrange("p t e -> p (t e)")
            pe.matmul(turned[0][:, 0:TILES * EXPERTS], upper[:, :], oh, start=True, stop=True)
            pe.matmul(totals[:, 0:TILES * EXPERTS], m.ones[:, :], oh, start=True, stop=True).then_inc(s_cnt, 1)


def experts(nc, m, Wd, bd, out):
    ctx, sem, sb, ps = scope(nc)
    with ctx:
        wd = sb("wd", [P, EXPERTS, KH, F])
        bd_r = sb("bd_r", [1, EXPERTS, F])
        flat, at = m.acc[:, :, :].rearrange("p t c -> p (t c)"), 0
        views = []
        for a, b, c in ((2, GROUP, F), (2, GROUP, F), (1, KF, GROUP * P), (1, KH, GROUP * P)):
            views.append(flat[:, at:at + a * b * c].rearrange("p (a b c) -> p a b c", a=a, b=b))
            at += a * b * c
        xs, yb, xt, ht = views[0], views[1], views[2].squeeze(1), views[3].squeeze(1)
        turned = [ps(f"xturned{k}") for k in range(KF)]
        hid = [ps(f"xhid{k}") for k in range(4)]
        ybank = [ps(f"ybank{k}") for k in range(2)]
        s_wd, s_bd, s_xs, s_t, s_xt = sem("wd_loaded"), sem("bd_loaded"), [sem(f"tokens_loaded{k}") for k in range(2)], sem("tokens_turned"), sem("xt_ready")
        s_hid, s_ht, s_y, s_yk, s_ys = sem("hidden_done"), sem("gelu_done"), sem("y_done"), sem("y_kept"), [sem(f"y_stored{k}") for k in range(2)]
        s_back, s_out, s_fin = sem("y_back"), sem("out_ready"), sem("out_stored")
        block = ctx.enter_context(nc.Block())
        SG = SORTED_TILES // GROUP // 2

        def rows(table, g):
            return table[bass.ds(g * GROUP * P, GROUP * P), :].rearrange("(t p) c -> p t c", p=P)

        @block.sync
        def _(sp):
            sp.dma_start(bd_r[:, :, :], bd.unsqueeze(0)).then_inc(s_bd, 16)
            sp.sem_inc(s_t, 2)
            for h in range(2):
                sp.dma_start(xs[:, h, :, :], m.sorted_d[h * GROUP * P:(h + 1) * GROUP * P, :].rearrange("(t p) c -> p t c", p=P)).then_inc(s_xs[h], 16)
            for e in range(EXPERTS):
                sp.dma_start(wd[:, e, :, :], Wd[e].rearrange("(k p) c -> p k c", p=P)).then_inc(s_wd, 16)
            with sp.Fori(1, SG) as i:
                for h in range(2):
                    sp.wait_ge(s_t, 2 * i + h + 1)
                    sp.dma_start(xs[:, h, :, :], rows(m.sorted_d, 2 * i + h)).then_inc(s_xs[h], 16)
            for g in range(GROUPS - 1):
                sp.wait_ge(s_out, (g + 1) * GROUP)
                sp.dma_start(out[g * GROUP * P:(g + 1) * GROUP * P, :].rearrange("(t p) c -> p t c", p=P),
                             m.xres[:, g * GROUP:(g + 1) * GROUP, :]).then_inc(s_fin, 16)
            sp.wait_ge(s_out, NODE_TILES)
            sp.dma_start(out[(NODE_TILES - 1) * P:, :], m.xres[0:LAST, NODE_TILES - 1, :]).then_inc(s_fin, 16)
            sp.wait_ge(s_fin, 16 * GROUPS)

        @block.gpsimd
        def _(g):
            for h in range(2):
                g.wait_ge(s_ys[h], 16 * (SG + 1))
            for t in range(NODE_TILES):
                n = P if t < NODE_TILES - 1 else LAST
                g.indirect_dma_start(out=m.acc[0:n, t, 0:F], out_offset=None, in_=m.y_d,
                                     in_offset=bass.IndirectOffsetOnAxis(ap=m.pos[0:n, t:t + 1], axis=0)).then_inc(s_back, 16)

        @block.scalar
        def _(a):
            with a.Fori(0, SG) as i:
                for h in range(2):
                    g = 2 * i + h
                    for k in range(KH):
                        a.wait_ge(s_hid, g * KH + k + 1)
                        a.activation(ht[:, k, :], hid[k % 4][:, :], ACT.Gelu, bias=m.b1c[:, k:k + 1]).then_inc(s_ht, 1)
                    a.wait_ge(s_yk, (g + 1) * GROUP + 2)
                    a.dma_start(rows(m.y_d, g), yb[:, h, :, :]).then_inc(s_ys[h], 16)

        @block.vector
        def _(v):
            for h in range(2):
                v.sem_inc(s_ys[h], 16)
            with v.Fori(0, SG) as i:
                for h in range(2):
                    g = 2 * i + h
                    v.wait_ge(s_t, g + 3)
                    for f in range(KF):
                        last = v.tensor_copy(xt[:, f, :], turned[f][:, :])
                    last.then_inc(s_xt, 1)
                    v.wait_ge(s_ys[h], 16 * (i + 1))
                    for k in range(GROUP):
                        v.wait_ge(s_y, g * GROUP + k + 1)
                        v.tensor_copy(yb[:, h, k, :], ybank[k % 2][:, 0:F]).then_inc(s_yk, 1)
            v.wait_ge(s_back, 16 * NODE_TILES)
            for t in range(NODE_TILES):
                n = P if t < NODE_TILES - 1 else LAST
                v.scalar_tensor_tensor(m.xres[0:n, t, :], m.acc[0:n, t, 0:F], m.prob[0:n, t:t + 1], m.xres[0:n, t, :], ALU.mult, ALU.add).then_inc(s_out, 1)

        @block.tensor
        def _(pe):
            pe.sem_inc(s_ht, 4)
            pe.sem_inc(s_yk, 2)
            pe.wait_ge(s_bd, 16)
            pe.wait_ge(s_wd, 16 * EXPERTS)
            with pe.Fori(0, SG) as i:
                for h in range(2):
                    g = 2 * i + h
                    pe.wait_ge(s_xs[h], 16 * (i + 1))
                    for k in range(GROUP):
                        for f in range(KF):
                            last = pe.transpose(turned[f][:, k * P:(k + 1) * P], xs[:, h, k, f * P:(f + 1) * P], m.ident[:, :])
                    last.then_inc(s_t, 1)
                    pe.wait_ge(s_xt, g + 1)
                    for k in range(KH):
                        pe.wait_ge(s_ht, g * KH + k + 1)
                        for f in range(KF):
                            last = pe.matmul(hid[k % 4][:, :], m.w1[:, f, k * P:(k + 1) * P], xt[:, f, :], start=(f == 0), stop=(f == KF - 1))
                        last.then_inc(s_hid, 1)
                    _, expert = nc.values_load_multi_w_load_instructions(
                        m.eid[0:1, bass.ds(g * GROUP, GROUP)], engines=(mybir.EngineType.PE,), min_val=0, max_val=EXPERTS - 1,
                        skip_runtime_bounds_check_because="the smaller of a count and 7")
                    pe.wait_ge(s_ht, (g + 1) * KH + 4)
                    for k in range(GROUP):
                        pe.wait_ge(s_yk, g * GROUP + k + 1)
                        for f in range(KH):
                            pe.matmul(ybank[k % 2][:, 0:F], ht[:, f, k * P:(k + 1) * P], wd[:, bass.ds(expert[k], 1), f, :].squeeze(1), start=(f == 0), stop=False)
                        pe.matmul(ybank[k % 2][:, 0:F], m.ones[0:1, :], bd_r[0:1, bass.ds(expert[k], 1), :].squeeze(1), start=False, stop=True).then_inc(s_y, 1)


DEBUG = False


def dump(nc, m, out):
    ctx, sem, sb, ps = scope(nc)
    with ctx:
        s = sem("out_stored")
        block = ctx.enter_context(nc.Block())

        @block.sync
        def _(sp):
            full = NODE_TILES - 1
            sp.dma_start(out[0:full * P, :].rearrange("(t p) c -> p t c", p=P), m.xres[:, 0:full, :]).then_inc(s, 16)
            sp.dma_start(out[full * P:, :], m.xres[0:LAST, full, :]).then_inc(s, 16)
            sp.wait_ge(s, 32)


_INS = ['x', 'src', 'dst', 'L0_gnn_W', 'L0_gnn_a_src', 'L0_gnn_a_dst', 'L0_gnn_bias', 'L0_ffn_W1', 'L0_ffn_b1', 'L0_ffn_Wg',
        'L0_ffn_bg', 'L0_ffn_Wd', 'L0_ffn_bd']


def kernel(**inputs):
    import numpy as _np
    import concourse.bacc as _bacc
    from concourse import mybir as _mybir
    from concourse.bass_utils import run_bass_kernel_spmd as _run

    nc = _bacc.Bacc("TRN2", target_bir_lowering=False, num_devices=1)
    arrays, args = {}, []
    for name in _INS:
        a = _np.ascontiguousarray(inputs[name])
        arrays[f"in_{name}_dram"] = a
        args.append(nc.dram_tensor(f"in_{name}_dram", a.shape, _mybir.dt.from_np(a.dtype), kind="ExternalInput").ap())
    args.append(nc.dram_tensor("out_dram", (NODES, F), F32, kind="ExternalOutput").ap())
    build(nc, *args)
    r = _run(nc, [arrays], core_ids=[0])
    return r.results[0]["out_dram"]
```

```python
from contextlib import ExitStack

import numpy as np

import concourse.bass as bass
from concourse import mybir

F32 = mybir.dt.float32
BF16 = mybir.dt.bfloat16
F32R = mybir.dt.float32r
I32 = mybir.dt.int32
ALU = mybir.AluOpType
ACT = mybir.ActivationFunctionType
AX = mybir.AxisListType

P = 128
NODES, EDGES, F = 6250, 100000, 256
HEADS, CH = 8, 32
HID, EXPERTS = 1024, 8
SLOPE, EPS = 0.2, 1e-5
NODE_TILES = -(-NODES // P)
GROUP = 4
GROUPS = -(-NODE_TILES // GROUP)
TILES = GROUPS * GROUP
LAST = NODES - (NODE_TILES - 1) * P
EDGE_TILES = -(-EDGES // P)
PAIRS = EDGE_TILES + NODE_TILES - 1
BATCH = 8
BATCHES = -(-PAIRS // BATCH)
UNROLL = 4
ROUNDS = (BATCHES - 1) // UNROLL
RING = 4
BANKS = 4
PARTS = 3
PAIR_COLS = -(-(BATCHES + 3) * BATCH // P)
PAIR_PAD = PAIR_COLS * P
ROW = HEADS + F
PROB, TOKEN = ROW + F, ROW + F + 1
REC = ROW + F + 2
SREC = REC - HEADS
PAD_TOKEN = 1 << 14
PAD_DST = 16384
KF, KH = F // P, HID // P
SORTED_TILES = (NODES + EXPERTS * (P - 1)) // P
SORTED = SORTED_TILES * P
SPREAD = 40.0
HUGE = 3e38
GUARD = 1e-16 * float(np.exp(-SPREAD))


class Steps:

    def __init__(self, eng, sem):
        self.eng, self.sem, self.n = eng, sem, 0

    def then(self, ins):
        self.n += 1
        ins.then_inc(self.sem, 1)
        self.eng.wait_ge(self.sem, self.n)


def build(nc, x, src, dst, W, a_src, a_dst, bias, W1, b1, Wg, bg, Wd, bd, out):
    ctx = ExitStack()
    with ctx:
        def dram(name, shape, dt=F32):
            return nc.dram_tensor(name, shape, dt, kind="Internal").ap()

        def sb(name, shape, dt=F32):
            return ctx.enter_context(nc.sbuf_tensor(name, shape, dt))

        m = Shared()
        m.rows_d = dram("rows_d", (TILES * P, ROW))
        m.src_d = dram("src_d", (PAIR_PAD * P,), I32)
        m.dst_d = dram("dst_d", (PAIR_PAD * P,), I32)
        m.sorted_d = dram("sorted_d", (SORTED, SREC))
        m.ident = sb("ident", [P, P])
        m.ones = sb("ones", [P, P])
        m.iota = sb("iota", [P, PAIR_PAD])
        m.iota_p = sb("iota_p", [P, 1])
        m.b1c = sb("b1c", [P, KH])
        m.eid = sb("eid", [1, SORTED_TILES], I32)
        with ExitStack() as records:
            m.big = records.enter_context(nc.sbuf_tensor("big", [P, TILES, REC], F32, side="right"))
            m.stats = records.enter_context(nc.sbuf_tensor("stats", [P, TILES, 6], F32, side="right"))
            m.mean = records.enter_context(nc.sbuf_tensor("mean", [P, TILES], F32, side="right"))
            m.rstd = records.enter_context(nc.sbuf_tensor("rstd", [P, TILES], F32, side="right"))
            m.tmp = records.enter_context(nc.sbuf_tensor("tmp", [P, TILES], F32, side="right"))
            m.acc = m.big[:, :, 0:ROW]
            m.xres = m.big[:, :, ROW:ROW + F]
            with ExitStack() as edge:
                def esb(name, shape, dt=F32):
                    return edge.enter_context(nc.sbuf_tensor(name, shape, dt))
                m.idx_t = esb("idx_t", [P, PAIR_PAD], I32)
                m.rel_t = esb("rel_t", [P, PAIR_PAD])
                m.node_t = esb("node_t", [1, PAIR_PAD], I32)
                m.score_t = esb("score_t", [P, TILES, 2 * HEADS])
                m.score_s = esb("score_s", [P, PARTS, TILES, 2 * HEADS], BF16)
                m.wide = esb("wide", [1, 1], I32)
                m.wt = esb("wt", [P, KF, F + 2 * HEADS])
                pair_tables(nc, m, x, src, dst, W, a_src, a_dst)
                project(nc, m)
                exact_bounds(nc, m)
                gather_edges(nc, m)
            m.pos = sb("pos", [P, TILES], I32)
            m.w1h = sb("w1h", [P, KF, HID], F32R)
            m.w1l = sb("w1l", [P, KF, HID], F32R)
            route(nc, m, bias, W1, b1, Wg, bg)
        experts(nc, m, Wd, bd, out)


class Shared:
    pass


def scope(nc):
    ctx = ExitStack()
    sem = lambda name: ctx.enter_context(nc.semaphore(name))
    sb = lambda name, shape, dt=F32: ctx.enter_context(nc.sbuf_tensor(name, shape, dt))
    ps = lambda name, shape=(P, 512): ctx.enter_context(nc.psum_tensor(name, list(shape), F32))
    return ctx, sem, sb, ps


def row_moments(v, m, done):
    with v.Fori(0, GROUPS) as g:
        for k in range(GROUP):
            t = g * GROUP + k
            last = v.bn_stats(m.stats[:, bass.ds(t, 1), :].squeeze(1), m.xres[:, bass.ds(t, 1), :].squeeze(1))
        last.then_inc(done, 1)
    v.wait_ge(done, GROUPS)


def layer_stats(v, m, chain):
    st = m.stats
    chain.then(v.tensor_tensor(m.mean[:, :], st[:, :, 1], st[:, :, 4], ALU.add))
    chain.then(v.tensor_tensor(m.tmp[:, :], st[:, :, 1], st[:, :, 4], ALU.subtract))
    chain.then(v.tensor_tensor(m.tmp[:, :], m.tmp[:, :], m.tmp[:, :], ALU.mult))
    chain.then(v.tensor_tensor(m.rstd[:, :], st[:, :, 2], st[:, :, 5], ALU.add))
    chain.then(v.tensor_scalar(m.tmp[:, :], m.tmp[:, :], 0.25, EPS, ALU.mult, ALU.add))
    chain.then(v.tensor_scalar(m.mean[:, :], m.mean[:, :], 0.5, None, ALU.mult))
    chain.then(v.scalar_tensor_tensor(m.rstd[:, :], m.rstd[:, :], 1.0 / F, m.tmp[:, :], ALU.mult, ALU.add))


def pair_tables(nc, m, x, src, dst, W, a_src, a_dst):
    ctx, sem, sb, ps = scope(nc)
    with ctx:
        PADN = PAIR_PAD * P - EDGES
        PADC = 153
        pad_src = sb("pad_src", [PADN // PADC, PADC], I32)
        pad_dst = sb("pad_dst", [PADN // PADC, PADC], I32)
        last_i = sb("last_i", [1, EDGE_TILES - 1], I32)
        last_f = sb("last_f", [1, EDGE_TILES - 1])
        iota_i = sb("iota_i", [P, PAIR_PAD], I32)
        iop_i = sb("iop_i", [P, 1], I32)
        bound = sb("bound", [P, 1])
        below = sb("below", [P, EDGE_TILES - 1])
        cnt = sb("cnt", [P, 1])
        turn = sb("turn", [P, 1])
        passed = sb("passed", [P, PAIR_PAD])
        inner = sb("inner", [P, 1])
        pair_i = sb("pair_i", [P, PAIR_COLS], I32)
        pair_f = sb("pair_f", [P, PAIR_COLS])
        tile_i = sb("tile_i", [P, PAIR_COLS], I32)
        first = sb("first", [P, PAIR_COLS])
        src_p = sb("src_p", [P, PAIR_COLS, P], I32)
        dst_p = sb("dst_p", [P, PAIR_COLS, P], I32)
        src_f = sb("src_f", [P, PAIR_COLS, P])
        rel_f = sb("rel_f", [P, PAIR_COLS, P])
        w = sb("w", [P, KF, F])
        a_col = sb("a_col", [P, KF, 2])
        a_blk = sb("a_blk", [P, KF, 2 * HEADS])
        head4 = sb("head4", [P, P // CH])
        bank = [ps(f"tab{k}") for k in range(8)]
        s_fill, s_pad, s_edges, s_last = sem("fill"), sem("pads_stored"), sem("edges_stored"), sem("lasts_loaded")
        s_iota, s_ident, s_chain = sem("iota_made"), sem("ident_made"), sem("dve_step")
        s_lastf, s_bcast, s_passed, s_nodes = sem("lasts_ready"), sem("lasts_everywhere"), sem("passed_ready"), sem("nodes_ready")
        s_tile, s_rows, s_rel, s_tr = sem("tiles_ready"), sem("pair_rows_loaded"), sem("rel_ready"), sem("transposed")
        s_w, s_a, s_blk, s_wa = sem("w_loaded"), sem("a_loaded"), sem("a_ready"), sem("wa_done")
        s_const, s_xz, s_x, s_moment = sem("constants_made"), sem("x_zeroed"), sem("x_loaded"), sem("moments_taken")
        block = ctx.enter_context(nc.Block())

        @block.sync
        def _(sp):
            sp.dma_start(m.src_d[0:EDGES].rearrange("(a b) -> a b", a=16), src.rearrange("(a b) -> a b", a=16)).then_inc(s_edges, 16)
            sp.dma_start(m.dst_d[0:EDGES].rearrange("(a b) -> a b", a=16), dst.rearrange("(a b) -> a b", a=16)).then_inc(s_edges, 16)
            n = (EDGE_TILES - 1) * P
            with nc.allow_non_contiguous_dma(reason="the last destination of every full edge tile"):
                sp.dma_start(last_i[0:1, :], dst[0:n].rearrange("(t e) -> t e", e=P)[:, P - 1:P].rearrange("t a -> a t")).then_inc(s_last, 16)
            sp.wait_ge(s_fill, 2)
            sp.dma_start(m.src_d[EDGES:].rearrange("(a b) -> a b", b=PADC), pad_src[:, :]).then_inc(s_pad, 16)
            sp.dma_start(m.dst_d[EDGES:].rearrange("(a b) -> a b", b=PADC), pad_dst[:, :]).then_inc(s_pad, 16)
            sp.wait_ge(s_xz, 1)
            full = NODE_TILES - 1
            for t0 in range(0, full, 12):
                sp.dma_start(m.xres[:, t0:t0 + 12, :], x[t0 * P:(t0 + 12) * P, :].rearrange("(t p) c -> p t c", p=P)).then_inc(s_x, 16)
            sp.dma_start(m.xres[0:LAST, full, :], x[full * P:, :]).then_inc(s_x, 16)

        @block.scalar
        def _(a):
            a.dma_start(w[:, :, :], W.rearrange("(k p) c -> p k c", p=P)).then_inc(s_w, 16)
            for n, vec in enumerate((a_src, a_dst)):
                with nc.allow_non_contiguous_dma(reason="a vector over the partitions"):
                    a.dma_start(a_col[:, :, n:n + 1], vec.rearrange("h c -> (h c)").rearrange("(k p a) -> p k a", p=P, a=1)).then_inc(s_a, 16)

        @block.gpsimd
        def _(g):
            g.memset(pad_src[:, :], 0).then_inc(s_fill, 1)
            g.memset(pad_dst[:, :], PAD_DST).then_inc(s_fill, 1)
            g.iota(iota_i[:, :], [[1, PAIR_PAD]], base=0, channel_multiplier=0).then_inc(s_iota, 1)
            g.iota(iop_i[:, :], [[0, 1]], base=0, channel_multiplier=1).then_inc(s_iota, 1)
            g.iota(pair_i[:, :], [[P, PAIR_COLS]], base=0, channel_multiplier=1).then_inc(s_iota, 1)
            g.memset(m.xres[:, NODE_TILES - 1:, :], 0.0).then_inc(s_xz, 1)
            g.wait_ge(s_edges, 32)
            g.wait_ge(s_pad, 32)
            g.wait_ge(s_tile, 1)
            for j in range(PAIR_COLS):
                for table, rows in ((m.src_d, src_p), (m.dst_d, dst_p)):
                    g.indirect_dma_start(out=rows[:, j, :], out_offset=None, in_=table.rearrange("(t e) -> t e", e=P),
                                         in_offset=bass.IndirectOffsetOnAxis(ap=tile_i[:, j:j + 1], axis=0)).then_inc(s_rows, 16)

        @block.vector
        def _(v):
            chain = Steps(v, s_chain)
            v.memset(m.ones[:, :], 1.0).then_inc(s_const, 1)
            chain.then(v.memset(inner[:, :], 0.0))
            chain.then(v.memset(inner[0:NODE_TILES - 1, :], 1.0))
            v.wait_ge(s_last, 16)
            v.tensor_copy(last_f[:, :], last_i[:, :]).then_inc(s_lastf, 1)
            v.wait_ge(s_iota, 3)
            v.tensor_copy(m.iota[:, :], iota_i[:, :])
            v.tensor_copy(pair_f[:, :], pair_i[:, :])
            chain.then(v.tensor_copy(m.iota_p[:, :], iop_i[:, :]))
            v.tensor_scalar(m.ident[:, :], m.iota[:, 0:P], m.iota_p[:, 0:1], None, ALU.is_equal).then_inc(s_ident, 1)
            chain.then(v.tensor_scalar(bound[:, :], m.iota_p[:, :], float(P), float(P), ALU.mult, ALU.add))
            v.wait_ge(s_bcast, 1)
            v.tensor_scalar(below[:, 0:512], bank[0][:, :], bound[:, 0:1], None, ALU.is_lt)
            chain.then(v.tensor_scalar(below[:, 512:], bank[1][:, 0:EDGE_TILES - 1 - 512], bound[:, 0:1], None, ALU.is_lt))
            chain.then(v.tensor_reduce(cnt[:, :], below[:, :], axis=AX.X, op=ALU.add))
            chain.then(v.scalar_tensor_tensor(turn[:, :], cnt[:, :], 1.0, m.iota_p[:, :], ALU.add, ALU.add))
            v.tensor_scalar(passed[:, :], m.iota[:, :], turn[:, 0:1], None, ALU.is_ge).then_inc(s_passed, 1)
            v.wait_ge(s_nodes, 1)
            v.tensor_copy(m.node_t[:, 0:512], bank[2][0:1, :])
            v.tensor_copy(m.node_t[:, 512:], bank[3][0:1, 0:PAIR_PAD - 512])
            chain.then(v.tensor_copy(first[:, :], bank[4][:, 0:PAIR_COLS]))
            v.tensor_tensor(tile_i[:, :], pair_f[:, :], first[:, :], ALU.subtract).then_inc(s_tile, 1)
            chain.then(v.tensor_scalar(first[:, :], first[:, :], float(P), None, ALU.mult))
            for j in range(P // CH):
                chain.then(v.memset(head4[:, j:j + 1], 0.0))
                chain.then(v.memset(head4[j * CH:(j + 1) * CH, j:j + 1], 1.0))
            chain.then(v.memset(a_blk[:, :, :], 0.0))
            v.wait_ge(s_a, 32)
            for k in range(KF):
                for n in range(2):
                    h0 = n * HEADS + k * (P // CH)
                    last = v.tensor_scalar(a_blk[:, k, h0:h0 + P // CH], head4[:, :], a_col[:, k, n:n + 1], None, ALU.mult)
            last.then_inc(s_blk, 1)
            v.wait_ge(s_wa, 1)
            for k in range(KF):
                v.tensor_copy(m.wt[:, k, HEADS:ROW], bank[k][:, 0:F])
                v.tensor_copy(m.wt[:, k, 0:HEADS], bank[5 + k][:, 0:HEADS])
                v.tensor_copy(m.wt[:, k, ROW:], bank[5 + k][:, HEADS:2 * HEADS])
            v.wait_ge(s_x, 80)
            row_moments(v, m, s_moment)
            v.wait_ge(s_rows, 32 * PAIR_COLS)
            v.tensor_copy(src_f[:, :, :], src_p[:, :, :])
            for j in range(PAIR_COLS):
                last = v.tensor_scalar(rel_f[:, j, :], dst_p[:, j, :], first[:, j:j + 1], None, ALU.subtract)
            last.then_inc(s_rel, 1)
            v.wait_ge(s_tr, 1)
            for table, b in ((m.idx_t, 4), (m.rel_t, 6)):
                v.tensor_copy(table[:, 0:512], bank[b][:, :])
                v.tensor_copy(table[:, 512:], bank[b + 1][:, 0:PAIR_PAD - 512])

        @block.tensor
        def _(pe):
            pe.wait_ge(s_const, 1)
            pe.wait_ge(s_lastf, 1)
            pe.matmul(bank[0][:, :], m.ones[0:1, :], last_f[0:1, 0:512], start=True, stop=True)
            pe.matmul(bank[1][:, 0:EDGE_TILES - 1 - 512], m.ones[0:1, :], last_f[0:1, 512:], start=True, stop=True).then_inc(s_bcast, 1)
            pe.wait_ge(s_passed, 1)
            pe.matmul(bank[2][0:1, :], inner[:, :], passed[:, 0:512], start=True, stop=True)
            pe.matmul(bank[3][0:1, 0:PAIR_PAD - 512], inner[:, :], passed[:, 512:], start=True, stop=True)
            for j in range(PAIR_COLS):
                last = pe.matmul(bank[4][:, j:j + 1], passed[:, j * P:(j + 1) * P], inner[:, :], start=True, stop=True)
            last.then_inc(s_nodes, 1)
            pe.wait_ge(s_ident, 1)
            pe.wait_ge(s_w, 16)
            for ki in range(KF):
                for kc in range(KF):
                    pe.transpose(bank[ki][:, kc * P:(kc + 1) * P], w[:, kc, ki * P:(ki + 1) * P], m.ident[:, :])
            pe.wait_ge(s_blk, 1)
            for ki in range(KF):
                for kc in range(KF):
                    last = pe.matmul(bank[5 + ki][:, 0:2 * HEADS], w[:, kc, ki * P:(ki + 1) * P], a_blk[:, kc, :], start=(kc == 0), stop=(kc == KF - 1))
            last.then_inc(s_wa, 1)
            pe.wait_ge(s_rel, 1)
            for rows, b in ((src_f, 4), (rel_f, 6)):
                for j in range(PAIR_COLS):
                    last = pe.transpose(bank[b + j // 4][:, (j % 4) * P:(j % 4 + 1) * P], rows[:, j, :], m.ident[:, :])
            last.then_inc(s_tr, 1)


def project(nc, m):
    ctx, sem, sb, ps = scope(nc)
    with ctx:
        xn = sb("xn", [P, GROUP, F])
        xt = sb("xt", [P, GROUP, F])
        ext = sb("ext", [P, 2 * HEADS])
        ext_c = sb("ext_c", [2 * HEADS, 1])
        ext_d = sb("ext_d", [2 * HEADS, 2 * HEADS])
        ext_b = sb("ext_b", [P, 2 * HEADS])
        width = sb("width", [1, HEADS])
        widest = sb("widest", [1, 1])
        low = [ps(f"pt{k}") for k in range(4)]
        high = [ps(f"pm{k}") for k in range(4)]
        s_chain = sem("dve_step")
        s_var, s_sd = sem("variance_ready"), sem("deviation_ready")
        s_xn, s_t, s_xt, s_mm, s_h = sem("xn_ready"), sem("xn_transposed"), sem("xt_ready"), sem("h_done"), sem("h_kept")
        s_rows, s_ext, s_extT, s_extd, s_extb = (sem("rows_stored"), sem("extremes_ready"), sem("extremes_turned"),
            sem("extremes_diagonal"), sem("extremes_everywhere"))
        block = ctx.enter_context(nc.Block())

        @block.sync
        def _(sp):
            with sp.Fori(0, GROUPS) as g:
                sp.wait_ge(s_h, (g + 1) * GROUP)
                sp.dma_start(m.rows_d[bass.ds(g * GROUP * P, GROUP * P), :].rearrange("(t p) c -> p t c", p=P),
                             m.acc[:, bass.ds(g * GROUP, GROUP), :]).then_inc(s_rows, 16)

        @block.scalar
        def _(a):
            a.wait_ge(s_var, 1)
            a.activation(m.rstd[:, :], m.rstd[:, :], ACT.Sqrt).then_inc(s_sd, 1)
            with a.Fori(0, GROUPS) as g:
                for k in range(GROUP):
                    a.wait_ge(s_t, g * GROUP + k + 1)
                    a.activation(xt[:, k, :], low[k][:, 0:F], ACT.Copy).then_inc(s_xt, 1)

        @block.vector
        def _(v):
            chain = Steps(v, s_chain)
            layer_stats(v, m, chain)
            v.sem_inc(s_var, 1)
            v.wait_ge(s_sd, 1)
            chain.then(v.reciprocal(m.rstd[:, :], m.rstd[:, :]))

            def normal(t, k):
                v.tensor_scalar(xn[:, k, :], m.xres[:, bass.ds(t, 1), :].squeeze(1), m.mean[:, bass.ds(t, 1)],
                                m.rstd[:, bass.ds(t, 1)], ALU.subtract, ALU.mult).then_inc(s_xn, 1)

            def keep_h(t, k):
                v.wait_ge(s_mm, t + 1)
                v.tensor_copy(m.acc[:, bass.ds(t, 1), :].squeeze(1), high[k][:, 0:ROW])
                v.tensor_copy(m.score_t[:, bass.ds(t, 1), 0:HEADS].squeeze(1), high[k][:, ROW:ROW + HEADS]).then_inc(s_h, 1)

            for k in range(GROUP):
                normal(k, k)
            with v.Fori(0, GROUPS - 1) as g:
                for k in range(GROUP):
                    v.wait_ge(s_t, g * GROUP + k + 1)
                    normal((g + 1) * GROUP + k, k)
                    keep_h(g * GROUP + k, k)
            for k in range(GROUP):
                keep_h(TILES - GROUP + k, k)
            v.wait_ge(s_h, TILES)
            as_h = m.acc[:, :, 0:HEADS].rearrange("p t h -> p h t")
            v.tensor_reduce(ext[:, 0:HEADS], as_h, axis=AX.X, op=ALU.max)
            chain.then(v.tensor_reduce(ext[:, HEADS:], as_h, axis=AX.X, op=ALU.min))
            v.tensor_scalar(ext[:, HEADS:], ext[:, HEADS:], -1.0, None, ALU.mult).then_inc(s_ext, 1)
            v.wait_ge(s_extT, 1)
            chain.then(v.tensor_reduce(ext_c[:, :], low[0][0:2 * HEADS, 0:P], axis=AX.X, op=ALU.max))
            v.tensor_scalar(ext_d[:, :], m.ident[0:2 * HEADS, 0:2 * HEADS], ext_c[:, 0:1], None, ALU.mult).then_inc(s_extd, 1)
            v.wait_ge(s_extb, 1)
            chain.then(v.tensor_copy(ext_b[:, :], low[1][:, 0:2 * HEADS]))
            dst_s, shift = m.score_t[:, :, 0:HEADS], m.score_t[:, :, HEADS:]
            chain.then(v.tensor_tensor(shift, dst_s, ext_b[:, 0:HEADS].unsqueeze(1).broadcast_to([P, TILES, HEADS]), ALU.add))
            chain.then(v.scalar_tensor_tensor(shift, shift, SLOPE, shift, ALU.mult, ALU.max))
            chain.then(v.tensor_tensor(width[:, :], ext_b[0:1, 0:HEADS], ext_b[0:1, HEADS:], ALU.add))
            chain.then(v.tensor_reduce(widest[:, :], width[:, :], axis=AX.X, op=ALU.max))
            chain.then(v.tensor_scalar(m.wide[:, :], widest[:, :], SPREAD, None, ALU.is_gt))
            v.wait_ge(s_rows, 16 * GROUPS)

        @block.tensor
        def _(pe):
            def turn_xn(t, k):
                pe.wait_ge(s_xn, t + 1)
                for f in range(KF):
                    last = pe.transpose(low[k][:, f * P:(f + 1) * P], xn[:, k, f * P:(f + 1) * P], m.ident[:, :])
                last.then_inc(s_t, 1)

            def make_h(t, k, first=False):
                pe.wait_ge(s_xt, t + 1)
                if not first:
                    pe.wait_ge(s_h, t + 1 - GROUP)
                for f in range(KF):
                    last = pe.matmul(high[k][:, 0:F + 2 * HEADS], xt[:, k, f * P:(f + 1) * P], m.wt[:, f, :], start=(f == 0), stop=(f == KF - 1))
                last.then_inc(s_mm, 1)

            for k in range(GROUP):
                turn_xn(k, k)
            for k in range(GROUP):
                make_h(k, k, first=True)
                turn_xn(GROUP + k, k)
            with pe.Fori(1, GROUPS - 1) as g:
                for k in range(GROUP):
                    make_h(g * GROUP + k, k)
                    turn_xn((g + 1) * GROUP + k, k)
            for k in range(GROUP):
                make_h(TILES - GROUP + k, k)
            pe.wait_ge(s_ext, 1)
            pe.transpose(low[0][0:2 * HEADS, 0:P], ext[:, :], m.ident[:, :]).then_inc(s_extT, 1)
            pe.wait_ge(s_extd, 1)
            pe.matmul(low[1][:, 0:2 * HEADS], m.ones[0:2 * HEADS, :], ext_d[:, :], start=True, stop=True).then_inc(s_extb, 1)


def exact_bounds(nc, m):
    ctx, sem, sb, ps = scope(nc)
    with ctx:
        best = sb("best", [P, TILES, HEADS])
        idx1 = sb("idx1", [P, 1], I32)
        row1 = sb("row1", [P, ROW])
        hot1 = sb("hot1", [P, P])
        off1 = sb("off1", [P, P])
        held = sb("held", [P, HEADS, P])
        top = sb("top", [P, HEADS])
        bank = [ps(f"held_t{k}") for k in range(2)]
        s_i, s_r, s_held, s_t, s_c, s_b = sem("pair_idx_ready"), sem("pair_rows"), sem("held_ready"), sem("held_turned"), sem("pair_step"), sem("dve_step")
        STEPS = 4
        block = ctx.enter_context(nc.Block())

        def when_wide(eng, engine):
            wide = nc.values_load_multi_w_load_instructions(m.wide[0:1, 0:1], engines=(engine,), min_val=0, max_val=1,
                                                            skip_runtime_bounds_check_because="the result of a comparison")[1][0]
            return eng.If(wide > 0)

        @block.gpsimd
        def _(g):
            with when_wide(g, mybir.EngineType.Pool):
                with g.Fori(0, PAIRS) as p:
                    g.wait_ge(s_i, p + 1)
                    g.nop(nofuse=True)
                    g.indirect_dma_start(out=row1[:, :], out_offset=None, in_=m.rows_d,
                                         in_offset=bass.IndirectOffsetOnAxis(ap=idx1[:, 0:1], axis=0)).then_inc(s_r, 16)
            g.nop(nofuse=True)

        @block.vector
        def _(v):
            with when_wide(v, mybir.EngineType.DVE):
                chain = Steps(v, s_b)
                chain.then(v.tensor_copy(best[:, :, :], m.acc[:, :, 0:HEADS]))
                with v.Fori(0, PAIRS) as p:
                    v.tensor_copy(idx1[:, :], m.idx_t[:, bass.ds(p, 1)]).then_inc(s_i, 1)
                    v.tensor_scalar(hot1[:, :], m.iota[:, 0:P], m.rel_t[:, bass.ds(p, 1)], None, ALU.is_equal).then_inc(s_c, 1)
                    v.wait_ge(s_c, p * STEPS + 1)
                    v.tensor_scalar(off1[:, :], hot1[:, :], HUGE, HUGE, ALU.mult, ALU.subtract).then_inc(s_c, 1)
                    v.wait_ge(s_c, p * STEPS + 2)
                    v.wait_ge(s_r, 16 * p + 16)
                    for h in range(HEADS):
                        last = v.scalar_tensor_tensor(held[:, h, :], hot1[:, :], row1[:, h:h + 1], off1[:, :], ALU.mult, ALU.add)
                    last.then_inc(s_held, 1)
                    node = nc.values_load_multi_w_load_instructions(
                        m.node_t[0:1, bass.ds(p, 1)], engines=(mybir.EngineType.DVE,), min_val=0, max_val=NODE_TILES - 1,
                        skip_runtime_bounds_check_because="counts at most 48 turns")[1][0]
                    v.wait_ge(s_t, p + 1)
                    for k in range(2):
                        last = v.tensor_reduce(top[:, 4 * k:4 * k + 4], bank[k][:, :].rearrange("p (h e) -> p h e", e=P), axis=AX.X, op=ALU.max)
                    last.then_inc(s_c, 1)
                    v.wait_ge(s_c, p * STEPS + 3)
                    b = best[:, bass.ds(node, 1), :].squeeze(1)
                    v.tensor_tensor(b, b, top[:, :], ALU.max).then_inc(s_c, 1)
                    v.wait_ge(s_c, p * STEPS + 4)
                shift = m.score_t[:, :, HEADS:]
                chain.then(v.tensor_tensor(shift, m.score_t[:, :, 0:HEADS], best[:, :, :], ALU.add))
                chain.then(v.scalar_tensor_tensor(shift, shift, SLOPE, shift, ALU.mult, ALU.max))
            v.nop(nofuse=True)

        @block.tensor
        def _(pe):
            with when_wide(pe, mybir.EngineType.PE):
                with pe.Fori(0, PAIRS) as p:
                    pe.wait_ge(s_held, p + 1)
                    for h in range(HEADS):
                        last = pe.transpose(bank[h // 4][:, (h % 4) * P:(h % 4 + 1) * P], held[:, h, :], m.ident[:, :])
                    last.then_inc(s_t, 1)
            pe.nop(nofuse=True)


def gather_edges(nc, m):
    ctx, sem, sb, ps = scope(nc)
    with ctx:
        idx = sb("idx", [P, RING, BATCH], I32)
        rows = sb("rows", [P, RING, BATCH, ROW])
        msg = sb("msg", [P, 2, BATCH, ROW])
        hot = sb("hot", [P, 4, BATCH, P])
        hot_t = sb("hot_t", [P, 2, BATCH, P], BF16)
        dst_z = sb("dst_z", [P, 4, BATCH, 2 * HEADS])
        z = sb("z", [P, 2, BATCH, HEADS])
        turn = [ps(f"turn{k}") for k in range(2)]
        dsts = ps("dsts")
        sums = [ps(f"sums{k}") for k in range(BANKS)]
        s_idx, s_rows = sem("idx_ready"), [sem(f"rows_gathered{k}") for k in range(RING)]
        s_free, s_hot, s_turn, s_hott = sem("rows_free"), sem("hot_ready"), sem("hot_turned"), sem("hot_t_ready")
        s_dst, s_dz, s_z, s_e, s_msg = sem("dst_scores_ready"), sem("dst_scores_kept"), sem("z_ready"), sem("exp_ready"), sem("msg_ready")
        s_sum, s_acc, s_step = sem("sums_ready"), sem("sums_added"), sem("dve_step")
        s_chain, s_parts, s_own, s_ownx = sem("own_step"), sem("score_parts"), sem("own_ready"), sem("own_exp")
        spare = msg[:, 0, :, :].rearrange("p k c -> p (k c)")
        own = spare[:, 0:TILES * HEADS].rearrange("p (t h) -> p t h", h=HEADS)
        rest = spare[:, TILES * HEADS:3 * TILES * HEADS].rearrange("p (t h) -> p t h", h=2 * HEADS)
        block = ctx.enter_context(nc.Block())

        def node_tiles(engine, first, n):
            return nc.values_load_multi_w_load_instructions(
                m.node_t[0:1, bass.ds(first, n)], engines=(engine,), min_val=0, max_val=NODE_TILES - 1,
                skip_runtime_bounds_check_because="counts at most 48 turns")[1]

        def all_batches(eng, body):
            body(0, 0, 0)
            with eng.Fori(0, ROUNDS) as i:
                for j in range(1, UNROLL + 1):
                    body(UNROLL * i + j, j % UNROLL, i + j // UNROLL)
            for b in range(ROUNDS * UNROLL + 1, BATCHES):
                body(b, b % UNROLL, b // UNROLL)

        @block.gpsimd
        def _(g):
            def gather(b, r, n):
                h = r % RING
                g.wait_ge(s_idx, b + 1)
                g.nop(nofuse=True)
                for k in range(BATCH):
                    g.indirect_dma_start(out=rows[:, h, k, :], out_offset=None, in_=m.rows_d,
                                         in_offset=bass.IndirectOffsetOnAxis(ap=idx[:, h, k:k + 1], axis=0)).then_inc(s_rows[h], 16)

            all_batches(g, gather)

        @block.scalar
        def _(a):
            def give_idx(b, r):
                a.wait_ge(s_free, b + 1)
                a.activation(idx[:, r % RING, :], m.idx_t[:, bass.ds(b * BATCH, BATCH)], ACT.Copy).then_inc(s_idx, 1)

            def turned(b, r):
                a.wait_ge(s_turn, b + 1)
                for k in range(2):
                    last = a.activation(hot_t[:, r % 2, 4 * k:4 * k + 4, :], turn[k][:, :].rearrange("p (k e) -> p k e", e=P), ACT.Copy)
                last.then_inc(s_hott, 1)

            def keep_scores(b, r):
                a.wait_ge(s_dst, b + 1)
                a.activation(dst_z[:, r % 4, :, :], dsts[:, 0:BATCH * 2 * HEADS].rearrange("p (k c) -> p k c", k=BATCH), ACT.Copy).then_inc(s_dz, 1)

            def batch(b, r, n):
                a.wait_ge(s_z, b + 1)
                a.activation(msg[:, r % 2, :, 0:HEADS], z[:, r % 2, :, :], ACT.Exp).then_inc(s_e, 1)
                give_idx(b + RING - 1, r + RING - 1)
                turned(b + 2, r + 2)
                keep_scores(b + 1, r + 1)

            a.sem_inc(s_free, RING)
            for b in range(RING - 1):
                give_idx(b, b)
            turned(0, 0)
            turned(1, 1)
            a.wait_ge(s_own, 1)
            a.activation(m.acc[:, :, 0:HEADS], own, ACT.Exp).then_inc(s_ownx, 1)
            keep_scores(0, 0)
            all_batches(a, batch)

        @block.vector
        def _(v):
            def make_hot(b, r, ks=(0, BATCH)):
                n = ks[1] - ks[0]
                col = m.rel_t[:, bass.ds(b * BATCH + ks[0], n)]
                v.tensor_tensor(hot[:, r % 4, ks[0]:ks[1], :], m.iota[:, 0:P].unsqueeze(1).broadcast_to([P, n, P]),
                                col.unsqueeze(2).broadcast_to([P, n, P]), ALU.is_equal).then_inc(s_hot, 1)

            def add_sum(b, k, node):
                p = b * BATCH + k
                v.wait_ge(s_sum, p + 1)
                v.wait_ge(s_acc, p + BANKS)
                a = m.acc[:, bass.ds(node, 1), :].squeeze(1)
                v.tensor_tensor(a, a, sums[k % BANKS][:, 0:ROW], ALU.add).then_inc(s_acc, 1)

            def messages(b, r, q):
                h = r % 2
                v.tensor_tensor(msg[:, h, q:q + 2, HEADS:ROW].rearrange("p k (h c) -> p k h c", h=HEADS),
                                rows[:, r % RING, q:q + 2, HEADS:ROW].rearrange("p k (h c) -> p k h c", h=HEADS),
                                msg[:, h, q:q + 2, 0:HEADS].unsqueeze(3).broadcast_to([P, 2, HEADS, CH]), ALU.mult).then_inc(s_msg, 1)

            def batch(b, r, n):
                h = r % 2
                first = isinstance(b, int) and b == 0
                zz = z[:, h, :, :]
                last4 = None if first else node_tiles(mybir.EngineType.DVE, b * BATCH - 4, 4)
                v.wait_ge(s_rows[r % RING], 16 * BATCH * (n + 1))
                v.wait_ge(s_dz, b + 1)
                v.tensor_tensor(zz, rows[:, r % RING, :, 0:HEADS], dst_z[:, r % 4, :, 0:HEADS], ALU.add).then_inc(s_step, 1)
                if not first:
                    add_sum(b - 1, 4, last4[0])
                v.wait_ge(s_step, 2 * b + 1)
                v.scalar_tensor_tensor(zz, zz, SLOPE, zz, ALU.mult, ALU.max).then_inc(s_step, 1)
                if not first:
                    add_sum(b - 1, 5, last4[1])
                v.wait_ge(s_step, 2 * b + 2)
                v.tensor_tensor(zz, zz, dst_z[:, r % 4, :, HEADS:], ALU.subtract).then_inc(s_z, 1)
                if not first:
                    add_sum(b - 1, 6, last4[2])
                make_hot(b + 3, r + 3, (0, 2))
                if not first:
                    add_sum(b - 1, 7, last4[3])
                first4 = node_tiles(mybir.EngineType.DVE, b * BATCH, 4)
                v.wait_ge(s_e, b + 1)
                messages(b, r, 0)
                messages(b, r, 2)
                make_hot(b + 3, r + 3, (2, 4))
                add_sum(b, 0, first4[0])
                messages(b, r, 4)
                add_sum(b, 1, first4[1])
                messages(b, r, 6)
                add_sum(b, 2, first4[2])
                make_hot(b + 3, r + 3, (4, 8))
                v.wait_ge(s_msg, 4 * b + 4)
                v.sem_inc(s_free, 1)
                add_sum(b, 3, first4[3])

            def own_edges():
                chain = Steps(v, s_chain)
                chain.then(v.tensor_copy(m.score_s[:, 0, :, :], m.score_t[:, :, :]))
                chain.then(v.tensor_tensor(rest, m.score_t[:, :, :], m.score_s[:, 0, :, :], ALU.subtract))
                chain.then(v.tensor_copy(m.score_s[:, 1, :, :], rest))
                chain.then(v.tensor_tensor(rest, rest, m.score_s[:, 1, :, :], ALU.subtract))
                v.tensor_copy(m.score_s[:, 2, :, :], rest).then_inc(s_parts, 1)
                dst_s, shift = m.score_t[:, :, 0:HEADS], m.score_t[:, :, HEADS:]
                chain.then(v.tensor_tensor(own, dst_s, m.acc[:, :, 0:HEADS], ALU.add))
                chain.then(v.scalar_tensor_tensor(own, own, SLOPE, own, ALU.mult, ALU.max))
                v.tensor_tensor(own, own, shift, ALU.subtract).then_inc(s_own, 1)
                v.wait_ge(s_ownx, 1)
                by_head = m.acc[:, :, HEADS:ROW].rearrange("p t (h c) -> p t h c", h=HEADS)
                chain.then(v.tensor_tensor(by_head, by_head, m.acc[:, :, 0:HEADS].unsqueeze(3).broadcast_to([P, TILES, HEADS, CH]), ALU.mult))

            v.sem_inc(s_acc, BANKS)
            for b in range(3):
                for ks in ((0, 2), (2, 4), (4, 8)):
                    make_hot(b, b, ks)
            own_edges()
            all_batches(v, batch)
            node = node_tiles(mybir.EngineType.DVE, BATCHES * BATCH - 4, 4)
            for k in range(4):
                add_sum(BATCHES - 1, 4 + k, node[k])

        @block.tensor
        def _(pe):
            def turn_hot(b, r, first=False):
                pe.wait_ge(s_hot, 3 * b + 3)
                if not first:
                    pe.wait_ge(s_hott, b)
                for k in range(BATCH):
                    last = pe.transpose(turn[k // 4][:, (k % 4) * P:(k % 4 + 1) * P], hot[:, r % 4, k, :], m.ident[:, :])
                last.then_inc(s_turn, 1)

            def dst_scores(b, r, node, k):
                for part in range(PARTS):
                    last = pe.matmul(dsts[:, k * 2 * HEADS:(k + 1) * 2 * HEADS], hot_t[:, r % 2, k, :],
                                     m.score_s[:, part, bass.ds(node[k], 1), :].squeeze(1), start=(part == 0), stop=(part == PARTS - 1))
                if k == BATCH - 1:
                    last.then_inc(s_dst, 1)

            def batch(b, r, n):
                node = node_tiles(mybir.EngineType.PE, (b + 1) * BATCH, BATCH)
                turn_hot(b + 2, r + 2)
                for k in range(BATCH):
                    if k % 2 == 0:
                        pe.wait_ge(s_msg, 4 * b + k // 2 + 1)
                    pe.wait_ge(s_acc, b * BATCH + k + 1)
                    pe.matmul(sums[k % BANKS][:, 0:ROW], hot[:, r % 4, k, :], msg[:, r % 2, k, :], start=True, stop=True).then_inc(s_sum, 1)
                    if k == 0:
                        pe.wait_ge(s_hott, b + 2)
                        pe.wait_ge(s_dz, b + 1)
                    if k < BATCH // 2:
                        dst_scores(b + 1, r + 1, node, 2 * k)
                        dst_scores(b + 1, r + 1, node, 2 * k + 1)

            turn_hot(0, 0, first=True)
            turn_hot(1, 1)
            pe.wait_ge(s_parts, 1)
            node = node_tiles(mybir.EngineType.PE, 0, BATCH)
            for k in range(BATCH):
                dst_scores(0, 0, node, k)
            all_batches(pe, batch)


def route(nc, m, bias, W1, b1, Wg, bg):
    ctx, sem, sb, ps = scope(nc)
    with ctx:
        den = sb("den", [P, TILES, HEADS])
        bias_b = sb("bias_b", [P, F])
        wg = sb("wg", [P, KH, EXPERTS])
        wg_hl = sb("wg_hl", [P, KH, 2 * EXPERTS], F32R)
        wg_h0 = sb("wg_h0", [P, KH, 2 * EXPERTS], F32R)
        bg_b = sb("bg_b", [P, EXPERTS])
        xn = sb("xn2", [P, GROUP, F])
        w1 = sb("w1", [P, KF, HID])
        xh = sb("xh2", [P, 2, KF, GROUP * P], F32R)
        xl = sb("xl2", [P, 2, KF, GROUP * P], F32R)
        gate_s = sb("gate_s", [2 * EXPERTS, GROUP * P])
        prob = sb("prob", [P, TILES])
        hh = sb("hh2", [P, 4, GROUP * P], F32R)
        hl = sb("hl2", [P, 4, GROUP * P], F32R)
        hf = sb("hf2", [P, 2, GROUP * P])
        logit = sb("logit", [P, TILES, EXPERTS])
        onehot = sb("onehot", [P, TILES, EXPERTS])
        before = sb("before", [P, TILES, EXPERTS])
        tot = sb("tot", [P, TILES, EXPERTS])
        run = [sb(f"run{k}", [P, TILES, EXPERTS]) for k in range(2)]
        seen = sb("seen", [P, TILES])
        valid = sb("valid", [P, TILES])
        tok_i = sb("tok_i", [P, TILES], I32)
        upper = sb("upper", [P, P])
        thr = sb("thr", [P, NODE_TILES])
        need = sb("need", [P, EXPERTS, NODE_TILES])
        ntile = sb("ntile", [P, EXPERTS])
        cum = [sb(f"cum{k}", [P, EXPERTS]) for k in range(2)]
        base = sb("base", [P, EXPERTS])
        ends = sb("ends", [1, SORTED_TILES, EXPERTS])
        eid_f = sb("eid_f", [1, SORTED_TILES])
        pos_f = sb("pos_f", [P, TILES])
        zeros = sb("zeros", [P, SREC])
        turned = [ps(f"turned{k}") for k in range(KF)]
        hid = [ps(f"hid{k}") for k in range(4)]
        gate = ps("gate")
        gate_t = ps("gate_t")
        s_w1, s_wg, s_zero, s_zeroed, s_tok = sem("w1_loaded"), sem("wg_loaded"), sem("zeros_made"), sem("sorted_zeroed"), sem("token_ids")
        s_xn, s_t, s_xt, s_hid, s_ht, s_gate, s_kept, s_gt, s_gback = (sem("xn_ready"), sem("xn_turned"), sem("xt_ready"), sem("hidden_done"),
            sem("gelu_done"), sem("gates_done"), sem("gates_kept"), sem("gates_out"), sem("gates_turned"))
        s_bias, s_biased, s_lift, s_sd, s_hl = (sem("bias_loaded"), sem("bias_added"), sem("lift_step"),
            sem("deviation_ready"), sem("gelu_low"))
        s_wsplit, s_split, s_fill = sem("w1_split"), sem("high_parts"), sem("fill_number")
        s_w1h = sem("w1_high")
        s_recs, s_rstd, s_wg2 = sem("records_ready"), sem("statistics_ready"), sem("wg_split")
        LIFT = 7
        s_chain, s_max, s_exp, s_oh, s_cnt = (sem("dve_step"), sem("max_taken"), sem("exp_done"), sem("onehot_ready"),
            sem("counted"))
        block = ctx.enter_context(nc.Block())

        @block.sync
        def _(sp):
            sp.dma_start(bias_b[:, :], bias.partition_broadcast(P)).then_inc(s_bias, 16)
            sp.dma_start(w1[:, :, :], W1.rearrange("(k p) c -> p k c", p=P)).then_inc(s_w1, 16)
            with nc.allow_non_contiguous_dma(reason="a bias over the partitions"):
                sp.dma_start(m.b1c[:, :], b1.rearrange("(k p) -> p k", p=P)).then_inc(s_w1, 16)
            sp.dma_start(wg[:, :, :], Wg.rearrange("(k p) c -> p k c", p=P)).then_inc(s_wg, 16)
            sp.dma_start(bg_b[:, :], bg.partition_broadcast(P)).then_inc(s_wg, 16)
            sp.wait_ge(s_fill, 1)
            sp.dma_start(m.sorted_d.rearrange("(t p) c -> p t c", p=P),
                         zeros[:, :].unsqueeze(1).broadcast_to([P, SORTED_TILES, SREC])).then_inc(s_zeroed, 16)

        @block.gpsimd
        def _(g):
            g.wait_ge(s_bias, 16)
            with g.Fori(0, GROUPS) as i:
                xs = m.xres[:, bass.ds(i * GROUP, GROUP), :]
                g.tensor_tensor(xs, xs, bias_b[:, :].unsqueeze(1).broadcast_to([P, GROUP, F]), ALU.add).then_inc(s_biased, 1)
            g.memset(zeros[:, :], 0.0).then_inc(s_zero, 1)
            g.wait_ge(s_zero, 1)
            g.memset(zeros[:, SREC - 1:].bitcast(I32), PAD_TOKEN).then_inc(s_fill, 1)
            g.iota(tok_i[:, :], [[P, TILES]], base=0, channel_multiplier=1).then_inc(s_tok, 1)
            with g.Fori(0, GROUPS) as i:
                g.wait_ge(s_rstd, i + 1)
                ts = bass.ds(i * GROUP, GROUP)
                to = m.acc[:, ts, HEADS:ROW]
                wide = lambda c: c.unsqueeze(2).broadcast_to([P, GROUP, F])
                g.tensor_tensor(to, m.xres[:, ts, :], wide(m.mean[:, ts]), ALU.subtract).then_inc(s_recs, 1)
                g.wait_ge(s_recs, 2 * i + 1)
                g.tensor_tensor(to, to, wide(m.rstd[:, ts]), ALU.mult).then_inc(s_recs, 1)
            g.wait_ge(s_recs, 2 * GROUPS)
            g.wait_ge(s_zeroed, 16)

        @block.scalar
        def _(a):
            def deviation(g):
                a.wait_ge(s_lift, LIFT * g + LIFT)
                c = m.rstd[:, bass.ds(g * GROUP, GROUP)]
                a.activation(c, c, ACT.Sqrt).then_inc(s_sd, 1)

            def group(g, first=False, deviates=True):
                for k in range(KH):
                    a.wait_ge(s_hid, g * KH + k + 1)
                    a.wait_ge(s_hl, g * KH + k + 1)
                    a.activation(hh[:, k % 4, :], hid[k % 4][:, :], ACT.Gelu, bias=m.b1c[:, k:k + 1])
                    a.activation(hf[:, k % 2, :], hid[k % 4][:, :], ACT.Gelu, bias=m.b1c[:, k:k + 1]).then_inc(s_ht, 1)
                    if k == 0 and first:
                        deviation(1)
                    if k == 0 and deviates:
                        deviation(g + 2)

            a.wait_ge(s_w1, 32)
            a.activation(m.w1h[:, :, :], w1[:, :, :], ACT.Copy).then_inc(s_w1h, 1)
            deviation(0)
            group(0, first=True)
            with a.Fori(1, GROUPS - 2) as g:
                group(g)
            group(GROUPS - 2, deviates=False)
            group(GROUPS - 1, deviates=False)
            a.wait_ge(s_max, 1)
            a.activation(logit[:, :, :], logit[:, :, :], ACT.Exp).then_inc(s_exp, 1)

        @block.vector
        def _(v):
            chain = Steps(v, s_chain)

            def normal(to, t):
                return v.tensor_scalar(to, m.xres[:, bass.ds(t, 1), :].squeeze(1),
                                       m.mean[:, bass.ds(t, 1)], m.rstd[:, bass.ds(t, 1)], ALU.subtract, ALU.mult)

            def normals(g):
                v.wait_ge(s_sd, g + 1)
                v.nop(nofuse=True)
                c = m.rstd[:, bass.ds(g * GROUP, GROUP)]
                v.reciprocal(c, c).then_inc(s_rstd, 1)
                v.wait_ge(s_rstd, g + 1)
                for k in range(GROUP):
                    last = normal(xn[:, k, :], g * GROUP + k)
                last.then_inc(s_xn, 1)

            def lift(g, step):
                ts = bass.ds(g * GROUP, GROUP)
                sums = m.acc[:, ts, HEADS:ROW]
                mean, tmp, rstd, st = m.mean[:, ts], m.tmp[:, ts], m.rstd[:, ts], m.stats
                if step > 0:
                    v.wait_ge(s_lift, LIFT * g + step)
                if step == 0:
                    by_head = sums.rearrange("p t (h c) -> p t h c", h=HEADS)
                    last = v.tensor_tensor(by_head, by_head, den[:, ts, :].unsqueeze(3).broadcast_to([P, GROUP, HEADS, CH]), ALU.mult)
                elif step == 1:
                    v.wait_ge(s_biased, g + 1)
                    last = v.tensor_tensor(m.xres[:, ts, :], m.xres[:, ts, :], sums, ALU.add)
                elif step == 2:
                    for k in range(GROUP):
                        t = bass.ds(g * GROUP + k, 1)
                        last = v.bn_stats(m.stats[:, t, :].squeeze(1), m.xres[:, t, :].squeeze(1))
                elif step == 3:
                    v.tensor_tensor(mean, st[:, ts, 1], st[:, ts, 4], ALU.add)
                    v.tensor_tensor(tmp, st[:, ts, 1], st[:, ts, 4], ALU.subtract)
                    last = v.tensor_tensor(rstd, st[:, ts, 2], st[:, ts, 5], ALU.add)
                elif step == 4:
                    v.tensor_tensor(tmp, tmp, tmp, ALU.mult)
                    last = v.tensor_scalar(mean, mean, 0.5, None, ALU.mult)
                elif step == 5:
                    last = v.tensor_scalar(tmp, tmp, 0.25, EPS, ALU.mult, ALU.add)
                else:
                    last = v.scalar_tensor_tensor(rstd, rstd, 1.0 / F, tmp, ALU.mult, ALU.add)
                last.then_inc(s_lift, 1)

            def split_high(g, h):
                v.wait_ge(s_t, g + 1)
                for f in range(KF):
                    v.tensor_copy(xh[:, h, f, :], turned[f][:, :]).then_inc(s_split, 1)

            def split_low(g, h):
                v.wait_ge(s_split, 2 * g + 2)
                for f in range(KF):
                    last = v.tensor_tensor(xl[:, h, f, :], turned[f][:, :], xh[:, h, f, :].bitcast(F32), ALU.subtract)
                last.then_inc(s_xt, 1)

            def take_gates(g):
                v.wait_ge(s_gate, g + 1)
                v.tensor_copy(gate_s[:, :], gate[0:2 * EXPERTS, :]).then_inc(s_gt, 1)

            def keep_gates(g):
                v.wait_ge(s_gback, g + 1)
                two = gate_t[:, 0:GROUP * 2 * EXPERTS].rearrange("p (t n e) -> p t n e", t=GROUP, n=2)
                v.tensor_copy(logit[:, bass.ds(g * GROUP, GROUP), :], two[:, :, 0, :]).then_inc(s_kept, 1)
                v.wait_ge(s_kept, 2 * g + 1)
                lg = logit[:, bass.ds(g * GROUP, GROUP), :]
                v.tensor_tensor(lg, lg, two[:, :, 1, :], ALU.add).then_inc(s_kept, 1)

            def group(g, h, first=False, last=False, lifts=True):
                lift_steps = ((), (0,), (1,), (), (), (2,), (3, 4), (5, 6))
                for k in range(KH):
                    if k == 1 and not first:
                        take_gates(g - 1)
                    v.wait_ge(s_ht, g * KH + k + 5)
                    v.tensor_tensor(hl[:, k % 4, :], hf[:, k % 2, :], hh[:, k % 4, :].bitcast(F32), ALU.subtract).then_inc(s_hl, 1)
                    if not last:
                        if k == 0:
                            normals(g + 1)
                        if k == 3:
                            split_high(g + 1, 1 - h)
                        if k == 4:
                            split_low(g + 1, 1 - h)
                    if k == 5 and not first:
                        keep_gates(g - 1)
                    if lifts:
                        for step in lift_steps[k]:
                            lift(g + 3, step)

            chain.then(v.tensor_scalar(den[:, :, :], m.acc[:, :, 0:HEADS], GUARD, None, ALU.add))
            chain.then(v.reciprocal(den[:, :, :], den[:, :, :]))
            for step in range(LIFT):
                lift(0, step)
            normals(0)
            v.wait_ge(s_w1, 32)
            v.wait_ge(s_w1h, 1)
            for f in range(KF):
                last = v.tensor_tensor(m.w1l[:, f, :], w1[:, f, :], m.w1h[:, f, :].bitcast(F32), ALU.subtract)
            last.then_inc(s_wsplit, 1)
            split_high(0, 0)
            split_low(0, 0)
            v.wait_ge(s_wg, 32)
            chain.then(v.tensor_copy(wg_hl[:, :, 0:EXPERTS], wg[:, :, :]))
            v.tensor_tensor(wg_hl[:, :, EXPERTS:], wg[:, :, :], wg_hl[:, :, 0:EXPERTS].bitcast(F32), ALU.subtract)
            v.tensor_copy(wg_h0[:, :, 0:EXPERTS], wg_hl[:, :, 0:EXPERTS].bitcast(F32))
            v.tensor_scalar(wg_h0[:, :, EXPERTS:], wg[:, :, :], 0.0, None, ALU.mult).then_inc(s_wg2, 1)
            for g in (1, 2):
                for step in range(LIFT):
                    lift(g, step)
            v.sem_inc(s_hl, 2)
            group(0, 0, first=True)
            with v.Fori(0, (GROUPS - 5) // 2) as i:
                for h in (1, 0):
                    group(2 * i + 2 - h, h)
            group(GROUPS - 4, 1)
            group(GROUPS - 3, 0, lifts=False)
            group(GROUPS - 2, 1, lifts=False)
            group(GROUPS - 1, 0, last=True, lifts=False)
            take_gates(GROUPS - 1)
            keep_gates(GROUPS - 1)
            v.wait_ge(s_kept, 2 * GROUPS)
            chain.then(v.tensor_tensor(logit[:, :, :], logit[:, :, :], bg_b[:, :].unsqueeze(1).broadcast_to([P, TILES, EXPERTS]), ALU.add))
            chain.then(v.tensor_reduce(seen[:, :], logit[:, :, :], axis=AX.X, op=ALU.max))
            wide = seen[:, :].unsqueeze(2).broadcast_to([P, TILES, EXPERTS])
            v.tensor_tensor(logit[:, :, :], logit[:, :, :], wide, ALU.subtract).then_inc(s_max, 1)
            v.wait_ge(s_exp, 1)
            chain.then(v.tensor_reduce(seen[:, :], logit[:, :, :], axis=AX.X, op=ALU.add))
            chain.then(v.reciprocal(seen[:, :], seen[:, :]))
            chain.then(v.tensor_tensor(logit[:, :, :], logit[:, :, :], wide, ALU.mult))
            chain.then(v.tensor_reduce(prob[:, :], logit[:, :, :], axis=AX.X, op=ALU.max))
            chain.then(v.tensor_tensor(logit[:, :, :], logit[:, :, :], prob[:, :].unsqueeze(2).broadcast_to([P, TILES, EXPERTS]), ALU.is_ge))
            v.wait_ge(s_tok, 1)
            v.tensor_copy(m.big[:, :, PROB:PROB + 1], prob[:, :].unsqueeze(2))
            chain.then(v.tensor_copy(m.big[:, :, TOKEN:TOKEN + 1].bitcast(I32), tok_i[:, :].unsqueeze(2)))
            chain.then(v.tensor_copy(valid[:, :], tok_i[:, :]))
            chain.then(v.tensor_scalar(valid[:, :], valid[:, :], float(NODES), None, ALU.is_lt))
            chain.then(v.memset(seen[:, :], 0.0))
            for e in range(EXPERTS):
                chain.then(v.tensor_tensor(onehot[:, :, e], logit[:, :, e], seen[:, :], ALU.is_gt))
                chain.then(v.tensor_tensor(seen[:, :], seen[:, :], logit[:, :, e], ALU.max))
            chain.then(v.tensor_scalar(upper[:, :], m.iota[:, 0:P], m.iota_p[:, 0:1], None, ALU.is_gt))
            v.tensor_tensor(onehot[:, :, :], onehot[:, :, :], valid[:, :].unsqueeze(2).broadcast_to([P, TILES, EXPERTS]), ALU.mult).then_inc(s_oh, 1)
            v.wait_ge(s_cnt, 1)
            flat = lambda b: b[:, :, :].rearrange("p t e -> p (t e)")
            v.tensor_copy(flat(before), turned[0][:, 0:TILES * EXPERTS])
            chain.then(v.tensor_copy(flat(tot), turned[1][:, 0:TILES * EXPERTS]))
            chain.then(v.tensor_copy(flat(run[0]), flat(tot)))
            n, s = 0, 1
            while s < TILES:
                v.tensor_copy(run[1 - n][:, 0:s, :], run[n][:, 0:s, :])
                chain.then(v.tensor_tensor(run[1 - n][:, s:, :], run[n][:, s:, :], run[n][:, 0:TILES - s, :], ALU.add))
                n, s = 1 - n, 2 * s
            count = run[n][:, TILES - 1, :]
            chain.then(v.tensor_scalar(thr[:, :], m.iota[:, 0:NODE_TILES], float(P), None, ALU.mult))
            chain.then(v.tensor_tensor(need[:, :, :], count.unsqueeze(2).broadcast_to([P, EXPERTS, NODE_TILES]),
                                       thr[:, :].unsqueeze(1).broadcast_to([P, EXPERTS, NODE_TILES]), ALU.is_gt))
            chain.then(v.tensor_reduce(ntile[:, :], need[:, :, :], axis=AX.X, op=ALU.add))
            chain.then(v.tensor_copy(cum[0][:, :], ntile[:, :]))
            c, s = 0, 1
            while s < EXPERTS:
                v.tensor_copy(cum[1 - c][:, 0:s], cum[c][:, 0:s])
                chain.then(v.tensor_tensor(cum[1 - c][:, s:], cum[c][:, s:], cum[c][:, 0:EXPERTS - s], ALU.add))
                c, s = 1 - c, 2 * s
            chain.then(v.tensor_tensor(base[:, :], cum[c][:, :], ntile[:, :], ALU.subtract))
            chain.then(v.tensor_scalar(base[:, :], base[:, :], float(P), None, ALU.mult))
            chain.then(v.tensor_tensor(before[:, :, :], before[:, :, :], run[n][:, :, :], ALU.add))
            chain.then(v.tensor_tensor(before[:, :, :], before[:, :, :], tot[:, :, :], ALU.subtract))
            chain.then(v.tensor_tensor(before[:, :, :], before[:, :, :], base[:, :].unsqueeze(1).broadcast_to([P, TILES, EXPERTS]), ALU.add))
            chain.then(v.tensor_tensor(before[:, :, :], before[:, :, :], onehot[:, :, :], ALU.mult))
            chain.then(v.tensor_reduce(pos_f[:, :], before[:, :, :], axis=AX.X, op=ALU.add))
            v.tensor_copy(m.pos[:, :], pos_f[:, :])
            chain.then(v.tensor_tensor(ends[:, :, :], m.iota[0:1, 0:SORTED_TILES].unsqueeze(2).broadcast_to([1, SORTED_TILES, EXPERTS]),
                                       cum[c][0:1, :].unsqueeze(1).broadcast_to([1, SORTED_TILES, EXPERTS]), ALU.is_ge))
            chain.then(v.tensor_reduce(eid_f[:, :], ends[:, :, :], axis=AX.X, op=ALU.add))
            chain.then(v.tensor_scalar(m.eid[:, :], eid_f[:, :], float(EXPERTS - 1), None, ALU.min))

        @block.tensor
        def _(pe):
            def turn_x(g):
                pe.wait_ge(s_xn, g + 1)
                for k in range(GROUP):
                    for f in range(KF):
                        last = pe.transpose(turned[f][:, k * P:(k + 1) * P], xn[:, k, f * P:(f + 1) * P], m.ident[:, :])
                last.then_inc(s_t, 1)

            def turn_gates(g):
                pe.wait_ge(s_gt, g + 1)
                pe.nop(nofuse=True)
                n = 2 * EXPERTS
                for k in range(GROUP):
                    last = pe.transpose(gate_t[:, k * n:(k + 1) * n], gate_s[:, k * P:(k + 1) * P], m.ident[0:n, 0:n])
                last.then_inc(s_gback, 1)

            def add_gates(g, k, first=False):
                pe.wait_ge(s_hl, g * KH + k + 3)
                if k == 0 and not first:
                    pe.wait_ge(s_gt, g)
                rows = gate[0:2 * EXPERTS, :]
                pe.matmul(rows, wg_hl[:, k, :], hh[:, k % 4, :], start=(k == 0), stop=False)
                done = pe.matmul(rows, wg_h0[:, k, :], hl[:, k % 4, :], start=False, stop=(k == KH - 1))
                if k == KH - 1:
                    done.then_inc(s_gate, 1)

            def group(g, h, first=False, last=False):
                pe.wait_ge(s_xt, g + 1)
                for k in range(KH):
                    pe.wait_ge(s_ht, g * KH + k + 1)
                    hidden_chunk(pe, m, hid[k % 4], xh[:, h], xl[:, h], k).then_inc(s_hid, 1)
                    if k >= 3:
                        add_gates(g, k - 3, first)
                    elif not first:
                        add_gates(g - 1, KH - 3 + k)
                    if k == 2 and not last:
                        turn_x(g + 1)
                    if k == 4 and not first:
                        turn_gates(g - 1)
                if last:
                    for k in range(KH - 3, KH):
                        add_gates(g, k)

            pe.sem_inc(s_ht, 4)
            turn_x(0)
            pe.wait_ge(s_wsplit, 1)
            pe.wait_ge(s_wg2, 1)
            group(0, 0, first=True)
            with pe.Fori(0, (GROUPS - 3) // 2) as i:
                for h in (1, 0):
                    group(2 * i + 2 - h, h)
            group(GROUPS - 2, 1)
            group(GROUPS - 1, 0, last=True)
            turn_gates(GROUPS - 1)
            pe.wait_ge(s_oh, 1)
            oh = onehot[:, :, :].rearrange("p t e -> p (t e)")
            pe.matmul(turned[0][:, 0:TILES * EXPERTS], upper[:, :], oh, start=True, stop=True)
            pe.matmul(turned[1][:, 0:TILES * EXPERTS], m.ones[:, :], oh, start=True, stop=True).then_inc(s_cnt, 1)


def hidden_chunk(pe, m, bank, xh, xl, k):
    passes = [(w, x, f) for f in range(KF) for w, x in ((m.w1h, xh), (m.w1h, xl), (m.w1l, xh))]
    for n, (w, x, f) in enumerate(passes):
        done = pe.matmul(bank[:, :], w[:, f, k * P:(k + 1) * P], x[:, f, :], start=(n == 0), stop=(n == len(passes) - 1))
    return done


def experts(nc, m, Wd, bd, out):
    ctx, sem, sb, ps = scope(nc)
    with ctx:
        wd = sb("wd", [P, EXPERTS, 2, KH, F], F32R)
        bd_b = sb("bd_b", [P, EXPERTS, F])
        rec = sb("rec", [P, 2, GROUP, SREC])
        xh = sb("xh3", [P, 2, KF, GROUP * P], F32R)
        xl = sb("xl3", [P, 2, KF, GROUP * P], F32R)
        hh = sb("hh", [P, 2, GROUP * P], F32R)
        hl = sb("hl", [P, 2, GROUP * P], F32R)
        hf = sb("hf", [P, 2, GROUP * P])
        normal_x, result = rec[:, :, :, 0:F], rec[:, :, :, F:2 * F]
        turned = [ps(f"xturned{k}") for k in range(KF)]
        hid = [ps(f"xhid{k}") for k in range(2)]
        ybank = [ps(f"ybank{k}") for k in range(GROUP)]
        s_raw, s_wh, s_wl, s_bd = [sem(f"wd_loaded{k}") for k in range(EXPERTS)], sem("wd_high"), sem("wd_low"), sem("bd_loaded")
        s_rec, s_t, s_xh, s_xt = [sem(f"tokens_loaded{k}") for k in range(2)], sem("tokens_turned"), sem("x_high"), sem("x_split")
        s_hid, s_ht, s_hl = sem("hidden_done"), sem("gelu_done"), sem("gelu_low")
        s_y, s_biased, s_res, s_out = sem("y_done"), sem("y_biased"), sem("result_ready"), [sem(f"results_stored{k}") for k in range(2)]
        block = ctx.enter_context(nc.Block())
        s_scat = sem("records_sorted")
        SG = SORTED_TILES // GROUP // 2
        EARLY = 5

        def tile_experts(engine, first, n):
            return nc.values_load_multi_w_load_instructions(
                m.eid[0:1, bass.ds(first, n)], engines=(engine,), min_val=0, max_val=EXPERTS - 1,
                skip_runtime_bounds_check_because="the smaller of a count and 7")[1]

        @block.sync
        def _(sp):
            def load_wd(e):
                sp.dma_start(wd[:, e, 1, :, :].bitcast(F32), Wd[e].rearrange("(k p) c -> p k c", p=P)).then_inc(s_raw[e], 16)

            for e in range(EARLY):
                load_wd(e)
            sp.wait_ge(s_scat, 16 * NODE_TILES)
            for h in range(2):
                sp.dma_start(rec[:, h, :, :], m.sorted_d[h * GROUP * P:(h + 1) * GROUP * P, :].rearrange("(t p) c -> p t c", p=P)).then_inc(s_rec[h], 16)
            for e in range(EARLY, EXPERTS):
                load_wd(e)
            sp.dma_start(bd_b[:, :, :], bd.partition_broadcast(P)).then_inc(s_bd, 16)
            with sp.Fori(1, SG) as i:
                for h in range(2):
                    sp.wait_ge(s_out[h], 16 * GROUP * i)
                    sp.dma_start(rec[:, h, :, :], m.sorted_d[bass.ds((2 * i + h) * GROUP * P, GROUP * P), :].rearrange("(t p) c -> p t c", p=P)).then_inc(s_rec[h], 16)
            for h in range(2):
                sp.wait_ge(s_out[h], 16 * GROUP * SG)

        @block.gpsimd
        def _(g):
            for t in range(NODE_TILES):
                n = P if t < NODE_TILES - 1 else LAST
                g.indirect_dma_start(out=m.sorted_d, out_offset=bass.IndirectOffsetOnAxis(ap=m.pos[0:n, t:t + 1], axis=0),
                                     in_=m.big[0:n, t, HEADS:REC], in_offset=None).then_inc(s_scat, 16)
            with g.Fori(0, SG) as i:
                for h in range(2):
                    for k in range(GROUP):
                        g.wait_ge(s_res, (2 * i + h) * GROUP + k + 1)
                        g.nop(nofuse=True)
                        g.indirect_dma_start(out=out, out_offset=bass.IndirectOffsetOnAxis(ap=rec[:, h, k, SREC - 1:].bitcast(I32), axis=0),
                                             in_=result[:, h, k, :], in_offset=None, bounds_check=NODES - 1, oob_is_err=False).then_inc(s_out[h], 16)

        @block.scalar
        def _(a):
            for e in range(EXPERTS):
                a.wait_ge(s_raw[e], 16)
                a.activation(wd[:, e, 0, :, :], wd[:, e, 1, :, :].bitcast(F32), ACT.Copy).then_inc(s_wh, 1)
            with a.Fori(0, SG) as i:
                for h in range(2):
                    g = 2 * i + h
                    for k in range(KH):
                        a.wait_ge(s_hid, g * KH + k + 1)
                        a.wait_ge(s_hl, g * KH + k + 1)
                        a.activation(hh[:, k % 2, :], hid[k % 2][:, :], ACT.Gelu, bias=m.b1c[:, k:k + 1])
                        a.activation(hf[:, k % 2, :], hid[k % 2][:, :], ACT.Gelu, bias=m.b1c[:, k:k + 1]).then_inc(s_ht, 1)

        @block.vector
        def _(v):
            def split_high(g, h):
                v.wait_ge(s_t, g + 1)
                for f in range(KF):
                    last = v.tensor_copy(xh[:, h, f, :], turned[f][:, :])
                last.then_inc(s_xh, 1)

            def split_low(g, h):
                v.wait_ge(s_xh, g + 1)
                for f in range(KF):
                    last = v.tensor_tensor(xl[:, h, f, :], turned[f][:, :], xh[:, h, f, :].bitcast(F32), ALU.subtract)
                last.then_inc(s_xt, 1)

            def take_y(g, h, expert):
                for k in range(GROUP):
                    v.wait_ge(s_y, g * GROUP + k + 1)
                    v.tensor_tensor(normal_x[:, h, k, :], ybank[k][:, 0:F], bd_b[:, bass.ds(expert[k], 1), :].squeeze(1), ALU.add).then_inc(s_biased, 1)

            def results(g, h):
                for k in range(GROUP):
                    v.wait_ge(s_biased, g * GROUP + k + 1 + GROUP)
                    v.scalar_tensor_tensor(result[:, h, k, :], normal_x[:, h, k, :], rec[:, h, k, 2 * F:2 * F + 1],
                                           result[:, h, k, :], ALU.mult, ALU.add).then_inc(s_res, 1)

            def group(g, h, first=False, last=False):
                expert = None if first else tile_experts(mybir.EngineType.DVE, (g - 1) * GROUP, GROUP)
                for k in range(KH):
                    if k == 0 and not first:
                        take_y(g - 1, 1 - h, expert)
                    v.wait_ge(s_ht, g * KH + k + 3)
                    v.tensor_tensor(hl[:, k % 2, :], hf[:, k % 2, :], hh[:, k % 2, :].bitcast(F32), ALU.subtract).then_inc(s_hl, 1)
                    if k == 0 and not first:
                        results(g - 1, 1 - h)
                    if k == 5 and not last:
                        split_high(g + 1, 1 - h)
                    if k == 6 and not last:
                        split_low(g + 1, 1 - h)

            for e in range(EXPERTS):
                if e == EARLY:
                    split_high(0, 0)
                    split_low(0, 0)
                v.wait_ge(s_wh, e + 1)
                v.tensor_tensor(wd[:, e, 1, :, :], wd[:, e, 1, :, :].bitcast(F32), wd[:, e, 0, :, :].bitcast(F32), ALU.subtract).then_inc(s_wl, 1)
            v.sem_inc(s_hl, 2)
            v.wait_ge(s_bd, 16)
            for h in range(2):
                group(h, h, first=(h == 0))
            with v.Fori(1, SG - 1) as i:
                for h in range(2):
                    group(2 * i + h, h)
            for h in range(2):
                group(2 * SG - 2 + h, h, last=(h == 1))
            take_y(2 * SG - 1, 1, tile_experts(mybir.EngineType.DVE, (2 * SG - 1) * GROUP, GROUP))
            results(2 * SG - 1, 1)

        @block.tensor
        def _(pe):
            def turn_x(g, h, i):
                pe.wait_ge(s_rec[h], 16 * (i + 1))
                for k in range(GROUP):
                    for f in range(KF):
                        last = pe.transpose(turned[f][:, k * P:(k + 1) * P], rec[:, h, k, f * P:(f + 1) * P], m.ident[:, :])
                last.then_inc(s_t, 1)

            def down(g, k, expert, first=False):
                pe.wait_ge(s_hl, g * KH + k + 3)
                if k == 0 and first:
                    pe.wait_ge(s_wl, EXPERTS)
                for t in range(GROUP):
                    if k == 0:
                        pe.wait_ge(s_biased, g * GROUP + t + 1)
                    y, cols = ybank[t][:, 0:F], slice(t * P, (t + 1) * P)
                    high, low = (wd[:, bass.ds(expert[t], 1), part, k, :].squeeze(1) for part in range(2))
                    pe.matmul(y, hh[:, k % 2, cols], high, start=(k == 0), stop=False)
                    pe.matmul(y, hh[:, k % 2, cols], low, start=False, stop=False)
                    done = pe.matmul(y, hl[:, k % 2, cols], high, start=False, stop=(k == KH - 1))
                    if k == KH - 1:
                        done.then_inc(s_y, 1)

            def group(g, h, i, first=False, last=False):
                if first:
                    expert = tile_experts(mybir.EngineType.PE, g * GROUP, GROUP)
                else:
                    both = tile_experts(mybir.EngineType.PE, (g - 1) * GROUP, 2 * GROUP)
                    before, expert = both[:GROUP], both[GROUP:]
                pe.wait_ge(s_xt, g + 1)
                for k in range(KH):
                    pe.wait_ge(s_ht, g * KH + k + 1)
                    hidden_chunk(pe, m, hid[k % 2], xh[:, h], xl[:, h], k).then_inc(s_hid, 1)
                    if k > 0:
                        down(g, k - 1, expert, first)
                    elif not first:
                        down(g - 1, KH - 1, before)
                    if k == 5 and not last:
                        turn_x(g + 1, 1 - h, i + h)
                if last:
                    down(g, KH - 1, expert)

            pe.sem_inc(s_ht, 2)
            pe.sem_inc(s_biased, GROUP)
            turn_x(0, 0, 0)
            for h in range(2):
                group(h, h, 0, first=(h == 0))
            with pe.Fori(1, SG - 1) as i:
                for h in range(2):
                    group(2 * i + h, h, i)
            for h in range(2):
                group(2 * SG - 2 + h, h, SG - 1, last=(h == 1))


_INS = ['x', 'src', 'dst', 'L0_gnn_W', 'L0_gnn_a_src', 'L0_gnn_a_dst', 'L0_gnn_bias', 'L0_ffn_W1', 'L0_ffn_b1', 'L0_ffn_Wg',
        'L0_ffn_bg', 'L0_ffn_Wd', 'L0_ffn_bd']


def kernel(**inputs):
    import numpy as _np
    import concourse.bacc as _bacc
    from concourse import mybir as _mybir
    from concourse.bass_utils import run_bass_kernel_spmd as _run

    nc = _bacc.Bacc("TRN2", target_bir_lowering=False, num_devices=1)
    arrays, args = {}, []
    for name in _INS:
        a = _np.ascontiguousarray(inputs[name])
        arrays[f"in_{name}_dram"] = a
        args.append(nc.dram_tensor(f"in_{name}_dram", a.shape, _mybir.dt.from_np(a.dtype), kind="ExternalInput").ap())
    args.append(nc.dram_tensor("out_dram", (NODES, F), F32, kind="ExternalOutput").ap())
    build(nc, *args)
    r = _run(nc, [arrays], core_ids=[0])
    return r.results[0]["out_dram"]
```
